# Optimizing a Trainium2 kernel written in Bass

```python
import numpy as np
import jax
import jax.numpy as jnp

def _softmax(x, axis=-1):
    return jax.nn.softmax(x, axis=axis)
def _gelu(x):
    return jax.nn.gelu(x, approximate=True)
def _silu(x):
    return jax.nn.silu(x)
def _sigmoid(x):
    return jax.nn.sigmoid(x)
def _layernorm(x, axis=-1, eps=1e-5):
    m = jnp.mean(x, axis=axis, keepdims=True)
    v = jnp.var(x, axis=axis, keepdims=True)
    return (x - m) / jnp.sqrt(v + eps)
def _scatter_add(tgt, idx, src, axis=0):
    return tgt.at[idx].add(src)
def _segment_sum(src, seg, n):
    return jax.ops.segment_sum(src, seg, n)

kernel_name = 'mk_adj_ffn_d2_adj_256_6cd0a5'

def setup_inputs(seed: int = 0):
    np.random.seed(seed)
    _w = jnp.asarray
    def _rec_inputs():
        import jax
        import jax.numpy as jnp
        _gk = jax.random.key(seed)
        x = -0.0005207 + 1.001 * jax.random.normal(jax.random.fold_in(_gk, 1), (4096, 256), jnp.float32)
        _a = jax.random.bernoulli(jax.random.fold_in(_gk, 2), 0.0078125, (4096, 4096))
        _a = jnp.logical_or(_a, jnp.swapaxes(_a, -1, -2))
        _a = jnp.logical_or(_a, jnp.eye(4096, dtype=bool))
        _af = _a.astype(jnp.float32)
        _af = _af * jax.random.uniform(jax.random.fold_in(_gk, 3), (4096, 4096), jnp.float32, 0.05, 2.05)
        adj = _af
        return x, adj
    x, adj = _rec_inputs()
    def _L0_gnn_setup():
        import jax, jax.numpy as jnp
        import numpy as np
        N = 8192
        D = 256
        CUTOFF = 1.0
        MU = 1.0
        SIGMA = 0.5

        def sensitivity(r, mu, sigma):
            return jnp.exp(-(1.0 / r - 1.0 / mu) ** 2 / (2.0 * sigma * sigma))
        key = jax.random.key(seed)
        k_z, k_d, k_w = jax.random.split(key, 3)
        z = jax.random.normal(k_z, (N, D), dtype=jnp.float32)
        dist_matrix = jax.random.uniform(k_d, (N, N), dtype=jnp.float32) * 2.0 + 0.05
        W = jax.random.normal(k_w, (D, D), dtype=jnp.float32)
        B = jnp.zeros((D,), dtype=jnp.float32)
        return {'z': z, 'dist_matrix': dist_matrix, 'W': W, 'B': B}
    _L0_gnn_all = _L0_gnn_setup()
    _L0_gnn_in = {k: v for k, v in _L0_gnn_all.items() if k in ('W', 'B', )}
    del _L0_gnn_all

    def _L0_ffn_setup():
        import jax, jax.numpy as jnp
        import numpy as np
        D_MODEL = 256
        D_STATE = 64
        D_CONV = 4
        EXPAND = 2
        HEADDIM = 64
        D_INNER = EXPAND * D_MODEL
        NHEADS = D_INNER // HEADDIM
        CONV_DIM = D_INNER + 2 * D_STATE
        D_IN_PROJ = 2 * D_INNER + 2 * D_STATE + NHEADS
        CHUNK = 256
        EPS = 1e-05

        def segsum(a):
            T = a.shape[-1]
            cs = jnp.cumsum(a, axis=-1)
            ss = cs[..., :, None] - cs[..., None, :]
            mask = jnp.tril(jnp.ones((T, T), dtype=bool))
            return jnp.where(mask, ss, -jnp.inf)

        def mamba2_block(x, W_in, conv_w, conv_b, dt_bias, A_log, D, norm_w, W_out, W_lin, b_lin):
            Bsz, L, _ = x.shape
            zxbcdt = x @ W_in
            z, xBC, dt = jnp.split(zxbcdt, [D_INNER, D_INNER + CONV_DIM], axis=-1)
            xp = jnp.pad(xBC, ((0, 0), (D_CONV - 1, 0), (0, 0)))
            conv = conv_b + sum((xp[:, k:k + L, :] * conv_w[:, k] for k in range(D_CONV)))
            xBC = jax.nn.silu(conv)
            xh, Bmat, Cmat = jnp.split(xBC, [D_INNER, D_INNER + D_STATE], axis=-1)
            dt = jax.nn.softplus(dt + dt_bias)
            A = -jnp.exp(A_log)
            nc = L // CHUNK
            xh = xh.reshape(Bsz, nc, CHUNK, NHEADS, HEADDIM)
            Bc = Bmat.reshape(Bsz, nc, CHUNK, D_STATE)
            Cc = Cmat.reshape(Bsz, nc, CHUNK, D_STATE)
            dtc = dt.reshape(Bsz, nc, CHUNK, NHEADS)
            dA = jnp.einsum('bclh,h->bhcl', dtc, A)
            A_cum = jnp.cumsum(dA, axis=-1)
            Lmat = jnp.exp(segsum(dA))
            xdt = xh * dtc[..., None]
            Y_diag = jnp.einsum('bcln,bcsn,bhcls,bcshp->bclhp', Cc, Bc, Lmat, xdt)
            decay_states = jnp.exp(A_cum[..., -1:] - A_cum)
            states = jnp.einsum('bcln,bhcl,bclhp->bchpn', Bc, decay_states, xdt)
            chunk_decay = jnp.exp(A_cum[..., -1])

            def step(h, inp):
                s, d = inp
                return (h * d[..., None, None] + s, h)
            _, prevs = jax.lax.scan(step, jnp.zeros_like(states[:, 0]), (jnp.moveaxis(states, 1, 0), jnp.moveaxis(chunk_decay, 2, 0)))
            prevs = jnp.moveaxis(prevs, 0, 1)
            Y_off = jnp.einsum('bcln,bchpn,bhcl->bclhp', Cc, prevs, jnp.exp(A_cum))
            Y = (Y_diag + Y_off + xh * D[:, None]).reshape(Bsz, L, D_INNER)
            Y = Y * jax.nn.silu(z)
            Y = Y * jax.lax.rsqrt(jnp.mean(Y * Y, axis=-1, keepdims=True) + EPS) * norm_w
            out = Y @ W_out
            return out @ W_lin + b_lin
        key = jax.random.key(seed)
        ks = jax.random.split(key, 12)
        B, L = (8, 4096)

        def gauss(k, shape, scale):
            return jax.random.normal(k, shape, dtype=jnp.float32) * scale
        return {'x': gauss(ks[0], (B, L, D_MODEL), 1.0), 'W_in': gauss(ks[1], (D_MODEL, D_IN_PROJ), D_MODEL ** (-0.5)), 'conv_w': gauss(ks[2], (CONV_DIM, D_CONV), 0.3), 'conv_b': gauss(ks[3], (CONV_DIM,), 0.1), 'dt_bias': jax.random.uniform(ks[4], (NHEADS,), minval=-4.0, maxval=-1.0), 'A_log': jnp.log(jax.random.uniform(ks[5], (NHEADS,), minval=1.0, maxval=16.0)), 'D': jnp.ones((NHEADS,), jnp.float32), 'norm_w': jnp.ones((D_INNER,), jnp.float32), 'W_out': gauss(ks[6], (D_INNER, D_MODEL), D_INNER ** (-0.5)), 'W_lin': gauss(ks[7], (D_MODEL, D_MODEL), D_MODEL ** (-0.5)), 'b_lin': jnp.zeros((D_MODEL,), jnp.float32)}
    _L0_ffn_all = _L0_ffn_setup()
    _L0_ffn_in = {k: v for k, v in _L0_ffn_all.items() if k in ('W_in', 'conv_w', 'conv_b', 'dt_bias', 'A_log', 'D', 'norm_w', 'W_out', 'W_lin', 'b_lin', )}
    del _L0_ffn_all

    def _L1_gnn_setup():
        import jax, jax.numpy as jnp
        import numpy as np
        from jax import lax
        D_MODEL = 256
        D_STATE = 16
        D_CONV = 4
        EXPAND = 2
        D_INNER = EXPAND * D_MODEL
        DT_RANK = (D_MODEL + 15) // 16
        N = 4096
        EPS = 1e-05

        def _mamba(h, w_in, conv_w, conv_b, w_xp, w_dt, b_dt, A_log, D_skip, w_out):
            L = h.shape[0]
            xz = h @ w_in
            xc, z = (xz[:, :D_INNER], xz[:, D_INNER:])
            xpad = jnp.pad(xc, ((D_CONV - 1, 0), (0, 0)))
            xconv = sum((xpad[k:k + L] * conv_w[:, k] for k in range(D_CONV))) + conv_b
            u = jax.nn.silu(xconv)
            dbc = u @ w_xp
            dt = jax.nn.softplus(dbc[:, :DT_RANK] @ w_dt + b_dt)
            B = dbc[:, DT_RANK:DT_RANK + D_STATE]
            C = dbc[:, DT_RANK + D_STATE:]
            A = -jnp.exp(A_log)
            dA = jnp.exp(dt[:, :, None] * A[None])
            dBu = dt[:, :, None] * B[:, None, :] * u[:, :, None]

            def step(hst, inp):
                dAt, dBut, Ct = inp
                hst = dAt * hst + dBut
                return (hst, hst @ Ct)
            _, ys = lax.scan(step, jnp.zeros((D_INNER, D_STATE), h.dtype), (dA, dBu, C))
            y = ys + u * D_skip
            y = y * jax.nn.silu(z)
            return y @ w_out
        key = jax.random.key(seed)
        ks = jax.random.split(key, 16)
        x = jax.random.normal(ks[0], (N, D_MODEL), dtype=jnp.float32)
        a = jax.random.uniform(ks[1], (N, N), dtype=jnp.float32)
        adj = a / a.sum(axis=1, keepdims=True)
        s = lambda fi, fo: 1.0 / np.sqrt(fi)
        gcn_w = jax.random.uniform(ks[2], (D_MODEL, D_MODEL), jnp.float32, -s(D_MODEL, 0), s(D_MODEL, 0))
        gcn_b = jnp.zeros((D_MODEL,), jnp.float32)
        ln_g = jnp.ones((D_MODEL,), jnp.float32)
        ln_b = jnp.zeros((D_MODEL,), jnp.float32)
        w_in = jax.random.normal(ks[3], (D_MODEL, 2 * D_INNER), jnp.float32) * s(D_MODEL, 0)
        conv_w = jax.random.normal(ks[4], (D_INNER, D_CONV), jnp.float32) * s(D_CONV, 0)
        conv_b = jnp.zeros((D_INNER,), jnp.float32)
        w_xp = jax.random.normal(ks[5], (D_INNER, DT_RANK + 2 * D_STATE), jnp.float32) * s(D_INNER, 0)
        w_dt = jax.random.normal(ks[6], (DT_RANK, D_INNER), jnp.float32) * s(DT_RANK, 0)
        b_dt = jnp.log(jnp.expm1(jnp.exp(jax.random.uniform(ks[7], (D_INNER,), jnp.float32, np.log(0.001), np.log(0.1)))))
        A_log = jnp.log(jnp.broadcast_to(jnp.arange(1, D_STATE + 1, dtype=jnp.float32), (D_INNER, D_STATE)))
        D_skip = jnp.ones((D_INNER,), jnp.float32)
        w_out = jax.random.normal(ks[8], (D_INNER, D_MODEL), jnp.float32) * s(D_INNER, 0)
        return dict(x=x, adj=adj, gcn_w=gcn_w, gcn_b=gcn_b, ln_g=ln_g, ln_b=ln_b, w_in=w_in, conv_w=conv_w, conv_b=conv_b, w_xp=w_xp, w_dt=w_dt, b_dt=b_dt, A_log=A_log, D_skip=D_skip, w_out=w_out)
    _L1_gnn_all = _L1_gnn_setup()
    _L1_gnn_in = {k: v for k, v in _L1_gnn_all.items() if k in ('gcn_w', 'gcn_b', 'ln_g', 'ln_b', 'w_in', 'conv_w', 'conv_b', 'w_xp', 'w_dt', 'b_dt', 'A_log', 'D_skip', 'w_out', )}
    del _L1_gnn_all

    def _L1_ffn_setup():
        import math
        import jax, jax.numpy as jnp
        import numpy as np
        CAPACITY_FACTOR = 1.25
        TOP_K = 2
        LN_EPS = 1e-05

        def _layer_norm(x, gamma, beta):
            mu = jnp.mean(x, axis=-1, keepdims=True)
            var = jnp.var(x, axis=-1, keepdims=True)
            return (x - mu) * jax.lax.rsqrt(var + LN_EPS) * gamma + beta
        key = jax.random.key(seed)
        ks = jax.random.split(key, 4)
        B, S, D, F, E = (8, 4096, 256, 512, 8)
        x = jax.random.normal(ks[0], (B, S, D), dtype=jnp.float32)
        Wr = jax.random.normal(ks[1], (D, E), dtype=jnp.float32) / np.sqrt(D)
        br = jnp.zeros((E,), jnp.float32)
        W1 = jax.random.normal(ks[2], (E, D, F), dtype=jnp.float32) / np.sqrt(D)
        b1 = jnp.zeros((E, F), jnp.float32)
        W2 = jax.random.normal(ks[3], (E, F, D), dtype=jnp.float32) / np.sqrt(F)
        b2 = jnp.zeros((E, D), jnp.float32)
        gamma = jnp.ones((D,), jnp.float32)
        beta = jnp.zeros((D,), jnp.float32)
        return {'x': x, 'Wr': Wr, 'br': br, 'W1': W1, 'b1': b1, 'W2': W2, 'b2': b2, 'gamma': gamma, 'beta': beta}
    _L1_ffn_all = _L1_ffn_setup()
    _L1_ffn_in = {k: v for k, v in _L1_ffn_all.items() if k in ('Wr', 'br', 'W1', 'b1', 'W2', 'b2', 'gamma', 'beta', )}
    del _L1_ffn_all

    return {
        "x": x,
        "adj": adj,
        "L0_gnn_W": _L0_gnn_in["W"],
        "L0_gnn_B": _L0_gnn_in["B"],
        "L0_ffn_W_in": _L0_ffn_in["W_in"],
        "L0_ffn_conv_w": _L0_ffn_in["conv_w"],
        "L0_ffn_conv_b": _L0_ffn_in["conv_b"],
        "L0_ffn_dt_bias": _L0_ffn_in["dt_bias"],
        "L0_ffn_A_log": _L0_ffn_in["A_log"],
        "L0_ffn_D": _L0_ffn_in["D"],
        "L0_ffn_norm_w": _L0_ffn_in["norm_w"],
        "L0_ffn_W_out": _L0_ffn_in["W_out"],
        "L0_ffn_W_lin": _L0_ffn_in["W_lin"],
        "L0_ffn_b_lin": _L0_ffn_in["b_lin"],
        "L1_gnn_gcn_w": _L1_gnn_in["gcn_w"],
        "L1_gnn_gcn_b": _L1_gnn_in["gcn_b"],
        "L1_gnn_ln_g": _L1_gnn_in["ln_g"],
        "L1_gnn_ln_b": _L1_gnn_in["ln_b"],
        "L1_gnn_w_in": _L1_gnn_in["w_in"],
        "L1_gnn_conv_w": _L1_gnn_in["conv_w"],
        "L1_gnn_conv_b": _L1_gnn_in["conv_b"],
        "L1_gnn_w_xp": _L1_gnn_in["w_xp"],
        "L1_gnn_w_dt": _L1_gnn_in["w_dt"],
        "L1_gnn_b_dt": _L1_gnn_in["b_dt"],
        "L1_gnn_A_log": _L1_gnn_in["A_log"],
        "L1_gnn_D_skip": _L1_gnn_in["D_skip"],
        "L1_gnn_w_out": _L1_gnn_in["w_out"],
        "L1_ffn_Wr": _L1_ffn_in["Wr"],
        "L1_ffn_br": _L1_ffn_in["br"],
        "L1_ffn_W1": _L1_ffn_in["W1"],
        "L1_ffn_b1": _L1_ffn_in["b1"],
        "L1_ffn_W2": _L1_ffn_in["W2"],
        "L1_ffn_b2": _L1_ffn_in["b2"],
        "L1_ffn_gamma": _L1_ffn_in["gamma"],
        "L1_ffn_beta": _L1_ffn_in["beta"],
    }

def reference(x, adj, L0_gnn_W, L0_gnn_B, L0_ffn_W_in, L0_ffn_conv_w, L0_ffn_conv_b, L0_ffn_dt_bias, L0_ffn_A_log, L0_ffn_D, L0_ffn_norm_w, L0_ffn_W_out, L0_ffn_W_lin, L0_ffn_b_lin, L1_gnn_gcn_w, L1_gnn_gcn_b, L1_gnn_ln_g, L1_gnn_ln_b, L1_gnn_w_in, L1_gnn_conv_w, L1_gnn_conv_b, L1_gnn_w_xp, L1_gnn_w_dt, L1_gnn_b_dt, L1_gnn_A_log, L1_gnn_D_skip, L1_gnn_w_out, L1_ffn_Wr, L1_ffn_br, L1_ffn_W1, L1_ffn_b1, L1_ffn_W2, L1_ffn_b2, L1_ffn_gamma, L1_ffn_beta):
    import jax
    import jax.numpy as jnp
    def _L0_gnn_ref(z, dist_matrix, W, B):
        import jax, jax.numpy as jnp
        import numpy as np
        N = 8192
        D = 256
        CUTOFF = 1.0
        MU = 1.0
        SIGMA = 0.5

        def sensitivity(r, mu, sigma):
            return jnp.exp(-(1.0 / r - 1.0 / mu) ** 2 / (2.0 * sigma * sigma))
        msg = z @ W + B
        sens = sensitivity(dist_matrix, MU, SIGMA)
        weights = jnp.where(dist_matrix < CUTOFF, sens, 0.0)
        return weights @ msg

    def _L0_ffn_ref(x, W_in, conv_w, conv_b, dt_bias, A_log, D, norm_w, W_out, W_lin, b_lin):
        import jax, jax.numpy as jnp
        import numpy as np
        D_MODEL = 256
        D_STATE = 64
        D_CONV = 4
        EXPAND = 2
        HEADDIM = 64
        D_INNER = EXPAND * D_MODEL
        NHEADS = D_INNER // HEADDIM
        CONV_DIM = D_INNER + 2 * D_STATE
        D_IN_PROJ = 2 * D_INNER + 2 * D_STATE + NHEADS
        CHUNK = 256
        EPS = 1e-05

        def segsum(a):
            T = a.shape[-1]
            cs = jnp.cumsum(a, axis=-1)
            ss = cs[..., :, None] - cs[..., None, :]
            mask = jnp.tril(jnp.ones((T, T), dtype=bool))
            return jnp.where(mask, ss, -jnp.inf)

        def mamba2_block(x, W_in, conv_w, conv_b, dt_bias, A_log, D, norm_w, W_out, W_lin, b_lin):
            Bsz, L, _ = x.shape
            zxbcdt = x @ W_in
            z, xBC, dt = jnp.split(zxbcdt, [D_INNER, D_INNER + CONV_DIM], axis=-1)
            xp = jnp.pad(xBC, ((0, 0), (D_CONV - 1, 0), (0, 0)))
            conv = conv_b + sum((xp[:, k:k + L, :] * conv_w[:, k] for k in range(D_CONV)))
            xBC = jax.nn.silu(conv)
            xh, Bmat, Cmat = jnp.split(xBC, [D_INNER, D_INNER + D_STATE], axis=-1)
            dt = jax.nn.softplus(dt + dt_bias)
            A = -jnp.exp(A_log)
            nc = L // CHUNK
            xh = xh.reshape(Bsz, nc, CHUNK, NHEADS, HEADDIM)
            Bc = Bmat.reshape(Bsz, nc, CHUNK, D_STATE)
            Cc = Cmat.reshape(Bsz, nc, CHUNK, D_STATE)
            dtc = dt.reshape(Bsz, nc, CHUNK, NHEADS)
            dA = jnp.einsum('bclh,h->bhcl', dtc, A)
            A_cum = jnp.cumsum(dA, axis=-1)
            Lmat = jnp.exp(segsum(dA))
            xdt = xh * dtc[..., None]
            Y_diag = jnp.einsum('bcln,bcsn,bhcls,bcshp->bclhp', Cc, Bc, Lmat, xdt)
            decay_states = jnp.exp(A_cum[..., -1:] - A_cum)
            states = jnp.einsum('bcln,bhcl,bclhp->bchpn', Bc, decay_states, xdt)
            chunk_decay = jnp.exp(A_cum[..., -1])

            def step(h, inp):
                s, d = inp
                return (h * d[..., None, None] + s, h)
            _, prevs = jax.lax.scan(step, jnp.zeros_like(states[:, 0]), (jnp.moveaxis(states, 1, 0), jnp.moveaxis(chunk_decay, 2, 0)))
            prevs = jnp.moveaxis(prevs, 0, 1)
            Y_off = jnp.einsum('bcln,bchpn,bhcl->bclhp', Cc, prevs, jnp.exp(A_cum))
            Y = (Y_diag + Y_off + xh * D[:, None]).reshape(Bsz, L, D_INNER)
            Y = Y * jax.nn.silu(z)
            Y = Y * jax.lax.rsqrt(jnp.mean(Y * Y, axis=-1, keepdims=True) + EPS) * norm_w
            out = Y @ W_out
            return out @ W_lin + b_lin
        return mamba2_block(x, W_in, conv_w, conv_b, dt_bias, A_log, D, norm_w, W_out, W_lin, b_lin)

    def _L1_gnn_ref(x, adj, gcn_w, gcn_b, ln_g, ln_b, w_in, conv_w, conv_b, w_xp, w_dt, b_dt, A_log, D_skip, w_out):
        import jax, jax.numpy as jnp
        import numpy as np
        from jax import lax
        D_MODEL = 256
        D_STATE = 16
        D_CONV = 4
        EXPAND = 2
        D_INNER = EXPAND * D_MODEL
        DT_RANK = (D_MODEL + 15) // 16
        N = 4096
        EPS = 1e-05

        def _mamba(h, w_in, conv_w, conv_b, w_xp, w_dt, b_dt, A_log, D_skip, w_out):
            L = h.shape[0]
            xz = h @ w_in
            xc, z = (xz[:, :D_INNER], xz[:, D_INNER:])
            xpad = jnp.pad(xc, ((D_CONV - 1, 0), (0, 0)))
            xconv = sum((xpad[k:k + L] * conv_w[:, k] for k in range(D_CONV))) + conv_b
            u = jax.nn.silu(xconv)
            dbc = u @ w_xp
            dt = jax.nn.softplus(dbc[:, :DT_RANK] @ w_dt + b_dt)
            B = dbc[:, DT_RANK:DT_RANK + D_STATE]
            C = dbc[:, DT_RANK + D_STATE:]
            A = -jnp.exp(A_log)
            dA = jnp.exp(dt[:, :, None] * A[None])
            dBu = dt[:, :, None] * B[:, None, :] * u[:, :, None]

            def step(hst, inp):
                dAt, dBut, Ct = inp
                hst = dAt * hst + dBut
                return (hst, hst @ Ct)
            _, ys = lax.scan(step, jnp.zeros((D_INNER, D_STATE), h.dtype), (dA, dBu, C))
            y = ys + u * D_skip
            y = y * jax.nn.silu(z)
            return y @ w_out
        h = jax.nn.relu(adj @ x @ gcn_w + gcn_b)
        mu = h.mean(-1, keepdims=True)
        var = h.var(-1, keepdims=True)
        h = (h - mu) * lax.rsqrt(var + EPS) * ln_g + ln_b
        return _mamba(h, w_in, conv_w, conv_b, w_xp, w_dt, b_dt, A_log, D_skip, w_out)

    def _L1_ffn_ref(x, Wr, br, W1, b1, W2, b2, gamma, beta):
        import math
        import jax, jax.numpy as jnp
        import numpy as np
        CAPACITY_FACTOR = 1.25
        TOP_K = 2
        LN_EPS = 1e-05

        def _layer_norm(x, gamma, beta):
            mu = jnp.mean(x, axis=-1, keepdims=True)
            var = jnp.var(x, axis=-1, keepdims=True)
            return (x - mu) * jax.lax.rsqrt(var + LN_EPS) * gamma + beta
        B, S, D = x.shape
        E = Wr.shape[1]
        N = B * S
        K = TOP_K
        logits = jnp.mean(x, axis=1) @ Wr + br
        routing_weights = jax.nn.softmax(logits, axis=-1)
        capacity = float(math.ceil(N * CAPACITY_FACTOR / E))
        expected_loads = routing_weights.sum(axis=0) * (N / B)
        scale = jnp.where(expected_loads > capacity, capacity / expected_loads, 1.0)
        routing_weights = jax.nn.softmax(routing_weights * scale, axis=-1)
        rw_tok = jnp.broadcast_to(routing_weights[:, None, :], (B, S, E)).reshape(N, E)
        top_w, top_i = jax.lax.top_k(rw_tok, K)
        top_w = jax.nn.softmax(top_w, axis=-1)
        xf = x.reshape(N, D)
        h = jax.nn.gelu(jnp.einsum('nd,edf->enf', xf, W1) + b1[:, None, :], approximate=False)
        y = jnp.einsum('enf,efd->end', h, W2) + b2[:, None, :]
        w_dense = jnp.zeros((N, E), x.dtype).at[jnp.arange(N)[:, None], top_i].add(top_w)
        out = jnp.einsum('ne,end->nd', w_dense, y).reshape(B, S, D)
        out = _layer_norm(out + x, gamma, beta)
        return out

    x = x + _L0_gnn_ref(_layernorm(x, axis=-1), adj, L0_gnn_W, L0_gnn_B)
    x = x + _L0_ffn_ref((_layernorm(x, axis=-1))[None], L0_ffn_W_in, L0_ffn_conv_w, L0_ffn_conv_b, L0_ffn_dt_bias, L0_ffn_A_log, L0_ffn_D, L0_ffn_norm_w, L0_ffn_W_out, L0_ffn_W_lin, L0_ffn_b_lin)[0]
    x = x + _L1_gnn_ref(_layernorm(x, axis=-1), adj, L1_gnn_gcn_w, L1_gnn_gcn_b, L1_gnn_ln_g, L1_gnn_ln_b, L1_gnn_w_in, L1_gnn_conv_w, L1_gnn_conv_b, L1_gnn_w_xp, L1_gnn_w_dt, L1_gnn_b_dt, L1_gnn_A_log, L1_gnn_D_skip, L1_gnn_w_out)
    x = x + _L1_ffn_ref((_layernorm(x, axis=-1))[None], L1_ffn_Wr, L1_ffn_br, L1_ffn_W1, L1_ffn_b1, L1_ffn_W2, L1_ffn_b2, L1_ffn_gamma, L1_ffn_beta)[0]
    return x


_drawn_inputs = setup_inputs


def setup_inputs(seed=0):
    import zlib

    import numpy as np

    out = dict(_drawn_inputs(seed))
    spreads = {'L0_gnn_B': (0.0, 0.1),
     'L0_ffn_D': (1.0, 0.2),
     'L0_ffn_norm_w': (1.0, 0.2),
     'L0_ffn_b_lin': (0.0, 0.1),
     'L1_gnn_gcn_b': (0.0, 0.1),
     'L1_gnn_ln_g': (1.0, 0.2),
     'L1_gnn_ln_b': (0.0, 0.1),
     'L1_gnn_conv_b': (0.0, 0.1),
     'L1_gnn_D_skip': (1.0, 0.2),
     'L1_ffn_br': (0.0, 0.1),
     'L1_ffn_b1': (0.0, 0.1),
     'L1_ffn_b2': (0.0, 0.1),
     'L1_ffn_gamma': (1.0, 0.2),
     'L1_ffn_beta': (0.0, 0.1)}
    factors = {}
    for name, (base, spread) in spreads.items():
        noise = np.random.default_rng([zlib.crc32(name.encode()), seed]).standard_normal(out[name].shape)
        drawn = base * np.exp(spread * noise) if base else spread * noise
        out[name] = jnp.asarray(drawn.astype(out[name].dtype))
    for name, factor in factors.items():
        out[name] = (out[name] * factor).astype(out[name].dtype)
    return out
```

```python
import numpy as np
import concourse.bass as bass
from concourse import mybir
from contextlib import ExitStack

F32 = mybir.dt.float32
U32 = mybir.dt.uint32
ALU = mybir.AluOpType
ACT = mybir.ActivationFunctionType
AX = mybir.AxisListType

N, D, TB = 4096, 256, 512
NB = N // TB
NJ = N // 128
EPS = 1e-5
TINY = 1e-18
LNEXP = "natural_log_exp_and_others"
TANH = "exp_and_others"
GELU = "gelu_and_others"

COLS = {}
_at = 0
for _name, _n in (("cw0", 24), ("cb0", 6), ("cw1", 16), ("cb1", 4), ("D0", 4), ("nw", 4), ("blin", 2), ("gcnb", 2),
                  ("lng", 2), ("lnb", 2), ("bdt", 4), ("A1", 64), ("D1", 4), ("gamma", 2), ("beta", 2)):
    COLS[_name] = (_at, _n)
    _at += _n
NCOL = _at
HALVED = COLS["D0"][0]
NROW = 256 + 32 + 8


class Line:

    def __init__(self, sem):
        self.sem, self.count, self.ops = sem, 0, []

    def __call__(self, fn, *after, signal=True):
        self.ops.append((list(after), fn, self.sem if signal else None, 1))
        self.count += signal
        return (self.sem, self.count) if signal else None

    def dma(self, lane, out, in_, *after, **kw):
        lane.count += 16
        self.ops.append((list(after), lambda e: e.dma_start(out, in_, **kw), lane.sem, 16))
        return (lane.sem, lane.count)

    def play(self, engine):
        seen = {}
        for after, fn, sem, step in self.ops:
            for s, value in flat(after):
                if seen.get(id(s), 0) < value:
                    seen[id(s)] = value
                    engine.wait_ge(s, value)
            ins = fn(engine)
            if sem is not None:
                ins.then_inc(sem, step)


class Lane:

    def __init__(self, sem):
        self.sem, self.count = sem, 0


def flat(after):
    for a in after:
        if a is None:
            continue
        if isinstance(a, list):
            yield from flat(a)
        else:
            yield a


class Slot:

    def __init__(self, buf):
        self.buf, self.free = buf, []


class Ring:
    def __init__(self, bufs):
        self.slots, self.at = [Slot(b) for b in bufs], 0

    def take(self):
        s = self.slots[self.at % len(self.slots)]
        self.at += 1
        assert s.free is not None, "the slot has no reader yet"
        over, s.free = s.free, None
        return s, over


def build(nc, t):
    with ExitStack() as ctx:
        def sem(name):
            return ctx.enter_context(nc.semaphore(name))

        def sb(c, name, shape, dt=F32):
            return c.enter_context(nc.sbuf_tensor(name, shape, dt))

        PE, DVE, SCA, POOL, SP = (Line(sem(n)) for n in ("s_pe", "s_dve", "s_act", "s_pool", "s_sp"))
        lanes = {}

        def lane(name):
            if name not in lanes:
                lanes[name] = Lane(sem("d_" + name))
            return lanes[name]

        def mm(out, lhsT, rhs, start, stop, *after, signal=False, skip=False):
            return PE(lambda e: e.matmul(out, lhsT, rhs, start=start, stop=stop, skip_group_check=skip),
                      *after, signal=signal)

        def tr(out, in_, ident, *after, signal=False):
            return PE(lambda e: e.transpose(out, in_, ident), *after, signal=signal)

        table = [None]

        def act(out, in_, func, *after, scale=1.0, bias=0.0, accum=None):
            need = {ACT.Ln: LNEXP, ACT.Exp: LNEXP, ACT.Tanh: TANH, ACT.Gelu: GELU}.get(func)
            if need is not None and table[0] != need:
                table[0] = need
                SCA(lambda e: e.preload_act_table_set(need), signal=False)
            if accum is None:
                return SCA(lambda e: e.activation(out, in_, func, bias=bias, scale=scale), *after)
            return SCA(lambda e: e.activation(out, in_, func, bias=bias, scale=scale, accum_out=accum), *after)

        def tt(line, out, a, b, op, *after):
            return line(lambda e: e.tensor_tensor(out, a, b, op), *after)

        def ts(line, out, a, s1, s2, op0, op1, *after):
            if op1 is None:
                return line(lambda e: e.tensor_scalar(out, a, s1, None, op0), *after)
            return line(lambda e: e.tensor_scalar(out, a, s1, s2, op0, op1), *after)

        def stt(out, a, s, b, op0, op1, *after):
            return DVE(lambda e: e.scalar_tensor_tensor(out, a, s, b, op0, op1), *after)

        def barrier():
            now = [(l.sem, l.count) for l in (PE, DVE, SCA, POOL) if l.count]
            now += [(l.sem, l.count) for l in lanes.values() if not l.sem in raw_sems]
            return now

        P = [ctx.enter_context(nc.psum_tensor(f"ps{i}", [128, 512], F32)) for i in range(8)]
        consts = sb(ctx, "consts", [128, 5, 128])
        ident, tri, trig, avg, one = (consts[:, i, :] for i in range(5))
        cols = sb(ctx, "cols", [128, NCOL])
        raw = [sb(ctx, f"raw{i}", [128, 2, TB]) for i in range(4)]
        msg2 = sb(ctx, "msg2", [128, NJ, D])

        def col(name, i=0, n=1):
            a = COLS[name][0] + i
            return cols[:, a:a + n]

        c_tok = SP.dma(lane("consts"), consts[:, :, :], t["consts"])
        k_tok = SP.dma(lane("cols"), cols[:, :], t["cols"])
        k_tok = ts(DVE, cols[:, 0:HALVED], cols[:, 0:HALVED], 0.5, None, ALU.mult, None, k_tok)

        NCH = NB * NJ // 2
        raw_tok = {}
        raw_lanes = [lane(f"raw{i}") for i in range(4)]
        raw_sems = [l.sem for l in raw_lanes]

        def load_raw(g, *after):
            if g >= 2 * NCH:
                return
            ib, q = divmod(g % NCH, NJ // 2)
            raw_tok[g] = SP.dma(raw_lanes[g % 4], raw[g % 4][:, :, :], t["adjT"][ib, :, 2 * q:2 * q + 2, :], *after)

        for g in range(4):
            load_raw(g)

        def layer_norm(take, x, xc, sq, r, x_tok, free):
            m, over = take()
            for k in range(2):
                tok = mm(m.buf[:, :], avg, x[:, k, :], k == 0, k == 1, over, x_tok, c_tok, signal=k == 1)
            sub = tt(DVE, xc[:, :, :], x[:, :, :], m.buf[:, None, :].broadcast_to([128, 2, TB]), ALU.subtract, tok, free)
            m.free = [sub]
            yield
            s = act(sq[:, :, :], xc[:, :, :], ACT.Square, sub, free)
            v, over = take()
            for k in range(2):
                tok = mm(v.buf[:, :], avg, sq[:, k, :], k == 0, k == 1, over, s, signal=k == 1)
            yield
            l = act(r[:, :], v.buf[:, :], ACT.Ln, tok, free, bias=EPS)
            v.free = [l]
            l = act(r[:, :], r[:, :], ACT.Exp, l, scale=-0.5)
            yield
            done[0] = tt(DVE, xc[:, :, :], xc[:, :, :], r[:, None, :].broadcast_to([128, 2, TB]), ALU.mult, l)

        done = [None]

        def run(gen):
            for _ in gen:
                pass

        cA = ExitStack()
        msg1 = sb(cA, "msg1", [128, NJ, D])
        wgt = [sb(cA, f"wgt{i}", [128, 2, TB]) for i in range(3)]
        W0 = sb(cA, "W0", [128, 2, D])
        Win = sb(cA, "Win", [128, 2, 1160])
        Wc = sb(cA, "Wc", [128, 4, D])
        rows = sb(cA, "rows", [128, NROW])
        Bbc, dtb, Abc = rows[:, 0:256], rows[:, 256:288], rows[:, 288:296]
        diagD = sb(cA, "diagD", [128, 4, 128])
        xb = sb(cA, "xb", [128, 2, TB])
        xc = sb(cA, "xc", [128, 2, TB])
        sq = sb(cA, "sq", [128, 2, TB])
        rr = sb(cA, "rr", [128, TB])
        xbc = sb(cA, "xbc", [128, 6, TB + 3])
        cc = sb(cA, "cc", [128, 6, TB])
        th = sb(cA, "th", [128, 2, TB])
        z = sb(cA, "z", [128, 4, TB])
        sm = sb(cA, "sm", [128, 8, 32])
        ecd = sb(cA, "ecd", [128, 3, 4, 8])
        ms = sb(cA, "ms", [128, 4])
        rms = sb(cA, "rms", [128, 4])
        rdA = sb(cA, "rdA", [128, 8, 128])
        E = [sb(cA, f"E{i}", [128, 8, 128]) for i in range(2)]
        xdt = [sb(cA, f"xdt{i}", [128, 512]) for i in range(2)]
        xdec = sb(cA, "xdec", [128, 512])
        bn = sb(cA, "bn", [128, 64])
        cbm = sb(cA, "cbm", [128, 128])
        tmp = sb(cA, "tmp", [128, 512])
        Y2 = sb(cA, "Y2", [128, 4, 512])
        YT = sb(cA, "YT", [128, 4, TB])
        h0 = sb(cA, "hs0", [64, 512])
        hd = sb(cA, "hd", [64, 512])

        w0_tok = SP.dma(lane("W0"), W0[:, :, :], t["W0"])
        rows_tok = SP.dma(lane("rows"), rows[:, :], t["rows"].broadcast_to([128, NROW]))
        win_tok = SP.dma(lane("Win"), Win[:, :, :], t["Win"])
        wout_tok = SP.dma(lane("Wout"), Y2[:, :, :], t["WoutT"])
        wlin_tok = SP.dma(lane("Wlin"), YT[:, 0:2, 0:256], t["Wlin"])

        ring = Ring(P[2:8])
        take = ring.take

        a_tok = act(Abc, Abc, ACT.Exp, rows_tok)
        a_tok = ts(DVE, Abc, Abc, -1.0, None, ALU.mult, None, a_tok)
        win_tok = ts(DVE, Win[:, :, 0:512], Win[:, :, 0:512], 0.5, None, ALU.mult, None, win_tok)
        for m in range(4):
            dd_tok = ts(DVE, diagD[:, m, :], ident, col("D0", m), None, ALU.mult, None, c_tok, k_tok)
        woutT = Y2[:, 0:2, :]
        for m in range(4):
            b, over = take()
            for k in range(2):
                tok = mm(b.buf[:, 0:256], woutT[:, k, m * 128:(m + 1) * 128], YT[:, k, 0:256], k == 0, k == 1,
                         over, wout_tok, wlin_tok, signal=k == 1)
            wc_tok = ts(DVE, Wc[:, m, :], b.buf[:, 0:256], col("nw", m), None, ALU.mult, None, tok, k_tok)
            b.free = [wc_tok]
        zero_tok = [POOL(lambda e: e.memset(xbc[:, :, 0:3], 0.0)), POOL(lambda e: e.memset(h0[:, :], 0.0))]

        raw_read = {}
        w_tok = {}
        w_free = {}

        def prep_a(g):
            if g >= NCH:
                return
            w, r = wgt[g % 3], raw[g % 4]
            a = act(w[:, :, :], r[:, :, :], ACT.Ln, raw_tok[g], w_free.get(g - 3), bias=TINY)
            a = act(w[:, :, :], w[:, :, :], ACT.Exp, a, scale=-1.0)
            a = act(w[:, :, :], w[:, :, :], ACT.Square, a, bias=-1.0)
            a = act(w[:, :, :], w[:, :, :], ACT.Exp, a, scale=-2.0)
            w_tok[g] = stt(w[:, :, :], r[:, :, :], 1.0, w[:, :, :], ALU.is_lt, ALU.mult, a)
            load_raw(g + 4, w_tok[g])

        P_free = [[], []]
        P_tok = [None, None]
        msg1_tok = {}

        def product_a(ib):
            if ib == 0:
                prep_a(0)
                prep_a(1)
            for q in range(NJ // 2):
                g = ib * (NJ // 2) + q
                prep_a(g + 2)
                for l in range(2):
                    j = 2 * q + l
                    for d in range(2):
                        tok = mm(P[d][:, :], msg1[:, j, d * 128:(d + 1) * 128], wgt[g % 3][:, l, :], j == 0, j == NJ - 1,
                                 w_tok[g], msg1_tok[j], P_free[d] if j == 0 else None,
                                 signal=(l == 1 and d == 1) or j == NJ - 1)
                        if j == NJ - 1:
                            P_tok[d] = tok
                    if l == 0:
                        yield
                w_free[g] = tok
                yield

        x_free = []

        def messages_0(ib, xb, xc, sq, rr, ln):
            x_tok = SP.dma(lane("x" + ln), xb[:, :, :], t["xT"][:, :, ib * TB:(ib + 1) * TB], bufs.get(ln))
            yield from layer_norm(take, xb, xc, sq, rr, x_tok, bufs.get(ln))
            xn = done[0]
            yield
            last = []
            for s in range(4):
                b, over = take()
                for k in range(2):
                    tok = mm(b.buf[:, 0:256], xc[:, k, s * 128:(s + 1) * 128], W0[:, k, :], k == 0, k == 1,
                             over, xn, w0_tok, signal=k == 1)
                msg1_tok[4 * ib + s] = tt(DVE, msg1[:, 4 * ib + s, :], b.buf[:, 0:256], Bbc, ALU.add, tok, rows_tok)
                b.free = [msg1_tok[4 * ib + s]]
                last = [tok]
                yield
            bufs[ln] = last

        bufs = {}
        p = product_a(0)
        second = (cc[:, 0:2, :], cc[:, 2:4, :], cc[:, 4:6, :], th[:, 0, :])
        for pair in range(NB // 2):
            one_, two = messages_0(2 * pair, xb, xc, sq, rr, "a"), messages_0(2 * pair + 1, *second, "b")
            next(one_)
            live = [one_, two]
            while live:
                for gen in list(live):
                    if next(gen, "end") == "end":
                        live.remove(gen)
            for _ in range(8):
                next(p, None)
        run(p)

        h_tok, h_read = zero_tok, []
        x2_tok, msg2_tok = {}, {}
        halo_tok = zero_tok
        free = {"xb": bufs["a"], "xc": bufs["a"], "cc": bufs["b"], "th": bufs["b"]}

        def mamba_a(ib):
            nonlocal h_tok, h_read, halo_tok
            x_tok = SP.dma(lane("xa"), xb[:, :, :], t["xT"][:, :, ib * TB:(ib + 1) * TB], free["xb"])
            for k in range(2):
                x_tok = tt(DVE, xb[:, k, :], xb[:, k, :], P[k][:, :], ALU.add, x_tok, P_tok[k])
                P_free[k] = [x_tok]
            yield
            yield from layer_norm(take, xb, xc, sq, rr, x_tok, free["xc"])
            xn = done[0]
            yield
            b, over = take()
            for s in range(4):
                for k in range(2):
                    tok = mm(b.buf[:, 8 * s:8 * s + 8], xc[:, k, s * 128:(s + 1) * 128], Win[:, k, 1152:1160],
                             k == 0, k == 1, over, xn, win_tok, signal=k == 1)
            v, av, dt, dA = sm[:, 0, :], sm[:, 1, :], sm[:, 2, :], sm[:, 3, :]
            a = tt(DVE, v, b.buf[:, 0:32], dtb, ALU.add, tok, rows_tok, free.get("sm"))
            b.free = [a]
            a = act(av, v, ACT.Abs, a)
            a = act(av, av, ACT.Exp, a, scale=-1.0)
            a = act(av, av, ACT.Ln, a, bias=1.0)
            dt_tok = stt(dt, v, 0.0, av, ALU.max, ALU.add, a)
            dA_tok = tt(DVE, dA.rearrange("p (c h) -> p c h", c=4), dt.rearrange("p (c h) -> p c h", c=4),
                        Abc[:, None, :].broadcast_to([128, 4, 8]), ALU.mult, dt_tok, a_tok)
            yield
            cv = []
            for m in range(6):
                w = 128 if m < 4 else 64
                c0 = 512 + 128 * m if m < 4 else 1024 + 64 * (m - 4)
                b, over = take()
                for k in range(2):
                    tok = mm(b.buf[0:w, :], Win[:, k, c0:c0 + w], xc[:, k, :], k == 0, k == 1, over, signal=k == 1)
                a = act(xbc[0:w, m, 3:TB + 3], b.buf[0:w, :], ACT.Identity, tok, halo_tok)
                b.free = [a]
                c = cc[0:w, m, :]
                a = ts(DVE, c, xbc[0:w, m, 0:TB], col("cw0", 4 * m)[0:w, :], col("cb0", m)[0:w, :],
                       ALU.mult, ALU.add, a, k_tok, free["cc"])
                for k in range(1, 4):
                    a = stt(c, xbc[0:w, m, k:k + TB], col("cw0", 4 * m + k)[0:w, :], c, ALU.mult, ALU.add, a)
                cv.append(a)
                yield
            halo_tok = [POOL(lambda e: e.tensor_copy(xbc[:, 0:4, 0:3], xbc[:, 0:4, TB:TB + 3]), cv),
                        POOL(lambda e: e.tensor_copy(xbc[0:64, 4:6, 0:3], xbc[0:64, 4:6, TB:TB + 3]), cv)]
            for s in range(4):
                b, over = take()
                for k in range(2):
                    tok = mm(b.buf[:, :], xc[:, k, s * 128:(s + 1) * 128], Win[:, k, 0:512], k == 0, k == 1, over,
                             signal=k == 1)
                zt = act(z[:, s, :], b.buf[:, :], ACT.Identity, tok, free.get("z"))
                b.free = [zt]
            free["xc"] = [tok]
            yield
            sil, ztok = [], []
            tf = free["th"]
            for what, w in ((cc[:, 0:2, :], 128), (cc[:, 2:4, :], 128), (cc[0:64, 4:6, :], 64),
                            (z[:, 0:2, :], 128), (z[:, 2:4, :], 128)):
                a = act(th[0:w, :, :], what, ACT.Tanh, cv, zt, tf)
                a = stt(what, th[0:w, :, :], 1.0, what, ALU.add, ALU.mult, a)
                tf = [a]
                sil.append(a)
            free["th"] = tf
            sil_tok = sil[2]
            z_tok = sil[4]
            yield
            b, over = take()
            for i, w in enumerate((tri, trig, one)):
                tok = mm(b.buf[:, 32 * i:32 * i + 32], w, dA, True, True, over, dA_tok, signal=i == 2)
            ecd_tok = act(ecd[:, :, :, :].rearrange("p a c h -> p (a c h)"), b.buf[:, 0:96], ACT.Exp, tok, free.get("ecd"))
            b.free = [ecd_tok]
            ms_tok = []
            rd_free = free.get("rdA")
            for s in range(4):
                ts_ = slice(s * 128, (s + 1) * 128)
                Es, xd = E[s % 2], xdt[s % 2]
                rd = tt(POOL, rdA[:, :, :], tri[:, None, :].broadcast_to([128, 8, 128]),
                        dA[:, 8 * s:8 * s + 8, None].broadcast_to([128, 8, 128]), ALU.mult, dA_tok, rd_free)
                seg = []
                for i in range(2):
                    b, over = take()
                    rd_free = mm(b.buf[:, :], trig, rdA[:, 4 * i:4 * i + 4, :].rearrange("p h l -> p (h l)"), True, True,
                                 over, rd, signal=True)
                    a = act(Es[:, 4 * i:4 * i + 4, :].rearrange("p h l -> p (h l)"), b.buf[:, :], ACT.Exp, rd_free,
                            free.get(("E", s % 2)))
                    b.free = [a]
                    seg.append(a)
                yield
                X, over = take()
                for m in range(4):
                    tok = tr(X.buf[:, m * 128:(m + 1) * 128], cc[:, m, ts_], ident, over, sil_tok, signal=m == 3)
                xd_tok = tt(DVE, xd[:, :].rearrange("p (h q) -> p h q", h=8), X.buf[:, :].rearrange("p (h q) -> p h q", h=8),
                            dt[:, 8 * s:8 * s + 8, None].broadcast_to([128, 8, 64]), ALU.mult, tok, dt_tok,
                            free.get(("xdt", s % 2)))
                X.free = [xd_tok]
                b, over = take()
                tr(b.buf[:, 0:64], cc[0:64, 4, ts_], ident[0:64, 0:64], over)
                tok = mm(b.buf[:, 128:256], cc[0:64, 4, ts_], cc[0:64, 5, ts_], True, True, signal=True)
                bn_tok = DVE(lambda e, b=b: e.tensor_copy(bn[:, :], b.buf[:, 0:64]), tok, free.get("bn"))
                cb_tok = tt(DVE, cbm[:, :], b.buf[:, 128:256], tri, ALU.mult, bn_tok)
                b.free = [cb_tok]
                M_tok = tt(DVE, Es[:, :, :], Es[:, :, :], cbm[:, None, :].broadcast_to([128, 8, 128]), ALU.mult, seg, cb_tok)
                xdec_tok = tt(POOL, xdec[:, :].rearrange("p (h q) -> p h q", h=8),
                              xd[:, :].rearrange("p (h q) -> p h q", h=8),
                              ecd[:, 1, s, :, None].broadcast_to([128, 8, 64]), ALU.mult, xd_tok, ecd_tok,
                              free.get("xdec"))
                hd_tok = tt(POOL, hd[:, :].rearrange("p (h q) -> p h q", h=8),
                            h0[:, :].rearrange("p (h q) -> p h q", h=8),
                            ecd[0:64, 2, s, :, None].broadcast_to([64, 8, 64]), ALU.mult, h_tok, ecd_tok)
                yield
                Yo, over = take()
                off = mm(Yo.buf[:, :], cc[0:64, 5, ts_], h0[:, :], True, True, over, h_tok, signal=True)
                Y, over = take()
                for m in range(4):
                    mm(Y.buf[:, m * 128:(m + 1) * 128], cc[:, m, ts_], diagD[:, m, :], m == 0, False, over, dd_tok,
                       skip=True)
                for h in range(8):
                    dia = mm(Y.buf[:, h * 64:(h + 1) * 64], Es[:, h, :], xd[:, h * 64:(h + 1) * 64], False, h == 7,
                             M_tok, xd_tok, signal=h == 7, skip=True)
                free[("E", s % 2)] = dia
                S, over = take()
                st = mm(S.buf[0:64, :], bn[:, :], xdec[:, :], True, True, over, bn_tok, xdec_tok, signal=True)
                free["xdec"], free["bn"] = st, st
                free[("xdt", s % 2)] = [dia, xdec_tok]
                a = tt(DVE, tmp[:, :].rearrange("p (h q) -> p h q", h=8), Yo.buf[:, :].rearrange("p (h q) -> p h q", h=8),
                       ecd[:, 0, s, :, None].broadcast_to([128, 8, 64]), ALU.mult, off, ecd_tok)
                Yo.free = [a]
                h_tok = tt(DVE, h0[:, :], hd[:, :], S.buf[0:64, :], ALU.add, st, hd_tok, off)
                S.free = [h_tok]
                a = tt(DVE, tmp[:, :], tmp[:, :], Y.buf[:, :], ALU.add, a, dia)
                Y.free = [a]
                a = tt(DVE, Y2[:, s, :], tmp[:, :], z[:, s, :], ALU.mult, a, z_tok, free.get("Y2"), wc_tok)
                a = act(tmp[:, :], Y2[:, s, :], ACT.Square, a, accum=ms[:, s:s + 1])
                free_tmp = a
                ms_tok.append(a)
                DVE(lambda e: e.memset(sm[:, 7, 0:1], 0.0), free_tmp)
                yield
            free["cc"], free["z"], free["rdA"] = [dia, off], [a], rd_free
            free["ecd"] = [st, h_tok, a, xdec_tok]
            free["sm"] = [rd_free, h_tok]
            a = act(rms[:, :], ms[:, :], ACT.Ln, ms_tok, scale=1.0 / 512, bias=EPS)
            rms_tok = act(rms[:, :], rms[:, :], ACT.Exp, a, scale=-0.5)
            for s in range(4):
                y3 = ts(DVE, Y2[:, s, :], Y2[:, s, :], rms[:, s:s + 1], None, ALU.mult, None, rms_tok)
                b, over = take()
                for m in range(4):
                    tok = tr(b.buf[:, m * 128:(m + 1) * 128], Y2[:, s, m * 128:(m + 1) * 128], ident, over, y3,
                             signal=m == 3)
                yt = act(YT[:, :, s * 128:(s + 1) * 128], b.buf[:, :].rearrange("p (m l) -> p m l", m=4), ACT.Identity,
                         tok, free.get("YT"))
                b.free = [yt]
                if s % 2:
                    yield
            free["Y2"] = tok
            for m in range(2):
                b, over = take()
                for k in range(4):
                    tok = mm(b.buf[:, :], Wc[:, k, m * 128:(m + 1) * 128], YT[:, k, :], k == 0, k == 3, over, yt, wc_tok,
                             signal=k == 3)
                x2 = stt(xb[:, m, :], b.buf[:, :], col("blin", m), xb[:, m, :], ALU.add, ALU.add, tok)
                b.free = [x2]
                yield
            free["YT"] = tok
            x2_tok[ib] = SP.dma(lane(f"x2_{ib}"), t["x2"][:, :, ib * TB:(ib + 1) * TB], xb[:, :, :], x2)
            yield from layer_norm(take, xb, xc, sq, rr, x2, free["xc"])
            xn = done[0]
            free["xb"] = [xn, x2_tok[ib]]
            yield
            for s in range(4):
                b, over = take()
                for k in range(2):
                    tok = mm(b.buf[:, 0:256], xc[:, k, s * 128:(s + 1) * 128], Wg[:, k, :], k == 0, k == 1,
                             over, xn, wg_tok, signal=k == 1)
                msg2_tok[4 * ib + s] = act(msg2[:, 4 * ib + s, :], b.buf[:, 0:256], ACT.Identity, tok)
                b.free = [msg2_tok[4 * ib + s]]
            free["xc"] = [tok]
            yield

        Wg = W0
        wg_tok = SP.dma(lane("W0"), W0[:, :, :], t["Wg"], bufs["a"], bufs["b"])

        raw_free = {}

        def product_b(ib):
            for q in range(NJ // 2):
                g = NCH + ib * (NJ // 2) + q
                for l in range(2):
                    j = 2 * q + l
                    for d in range(2):
                        tok = mm(P[d][:, :], msg2[:, j, d * 128:(d + 1) * 128], raw[g % 4][:, l, :], j == 0, j == NJ - 1,
                                 raw_tok[g], msg2_tok[j], P_free[d] if j == 0 else None,
                                 signal=(l == 1 and d == 1) or j == NJ - 1)
                        if j == NJ - 1:
                            P_tok[d] = tok
                    if l == 0:
                        yield
                load_raw(g + 4, tok)
                yield

        STEPS_A = 34
        for ib in range(NB):
            side = product_a(ib + 1) if ib + 1 < NB else product_b(0)
            limit = 32 if ib + 1 < NB else 28
            gone = 0
            for i, _ in enumerate(mamba_a(ib)):
                want = min(limit, (i + 1) * limit // STEPS_A)
                while gone < want:
                    next(side)
                    gone += 1
            while gone < limit:
                next(side)
                gone += 1
            if ib + 1 < NB:
                run(side)
        run(side)
        over_a = barrier()
        cA.close()

        cB = ExitStack()
        w1 = sb(cB, "w1", [128, 2, 1024])
        wxp = sb(cB, "wxp", [128, 4, 48])
        wdt = sb(cB, "wdt", [16, 512])
        wo1 = sb(cB, "wo1", [128, 4, D])
        sums = sb(cB, "sums", [128, 2, NB])
        u = [sb(cB, f"u{i}", [128, 4, TB]) for i in range(2)]
        sz = [sb(cB, f"sz{i}", [128, 4, TB]) for i in range(2)]
        dtt = [sb(cB, f"dt{i}", [128, 4, TB]) for i in range(2)]
        du = sb(cB, "du", [128, 4, TB])
        bcr = [sb(cB, f"bc{i}", [128, 2, 2, TB]) for i in range(3)]
        dAr = Ring([sb(cB, f"dA{i}", [128, 2, TB]) for i in range(2)])
        dBr = Ring([sb(cB, f"dB{i}", [128, 2, TB]) for i in range(2)])
        hr = Ring([sb(cB, f"h{i}", [128, 2, TB]) for i in range(2)])
        hst = sb(cB, "hst", [128, 4, 16])
        xcb = sb(cB, "xcb", [128, 4, TB + 3])
        hb = sb(cB, "hb", [128, 2, TB])
        sq1 = sb(cB, "sq1", [128, 2, TB])
        x3 = sb(cB, "x3", [128, 2, TB])
        r1 = sb(cB, "r1", [128, TB])
        th1 = sb(cB, "th1", [128, 2, TB])
        dbc = sb(cB, "dbc", [48, TB])

        ring_b = Ring(P[2:4])
        for s, o in zip(ring_b.slots, ring.slots[0:2]):
            s.free = o.free
        takeb = ring_b.take
        yb = P[4:8]
        y_free = [o.free for o in ring.slots[2:6]]

        w_tok1 = SP.dma(lane("w1"), w1[:, :, :], t["w1"], over_a)
        wxp_tok = SP.dma(lane("wxp"), wxp[:, :, :], t["wxp"], over_a)
        wdt_tok = SP.dma(lane("wdt"), wdt[:, :], t["wdt"], over_a)
        wo1_tok = SP.dma(lane("wo1"), wo1[:, :, :], t["wo1"], over_a)
        w_tok1 = ts(DVE, w1[:, :, 512:1024], w1[:, :, 512:1024], 0.5, None, ALU.mult, None, w_tok1, over_a)
        A1 = cols[:, COLS["A1"][0]:COLS["A1"][0] + 64]
        a = act(A1, A1, ACT.Exp, k_tok)
        A1_tok = ts(DVE, A1, A1, -1.0, None, ALU.mult, None, a)
        halo1 = [POOL(lambda e: e.memset(xcb[:, :, 0:3], 0.0), over_a)]
        hst_tok = [POOL(lambda e: e.memset(hst[:, :, :], 0.0), over_a)]
        SCA(lambda e: e.activation(th1[:, 0, 0:1], cols[:, 0:1], ACT.Identity), over_a)
        fb = {}
        u_tok, sz_tok, dt1_tok, bcs_tok = {}, {}, {}, {}
        h_prev = {(m, n): hst_tok for m in range(4) for n in range(8)}

        def pre_b(ib):
            nonlocal halo1
            p = ib % 2
            for k in range(2):
                hbt = act(hb[:, k, :], P[k][:, :], ACT.Relu, P_tok[k], fb.get("hb"), k_tok, bias=col("gcnb", k))
                P_free[k] = [hbt]
            yield
            yield from layer_norm(takeb, hb, hb, sq1, r1, hbt, None)
            a = done[0]
            for k in range(2):
                xn = ts(DVE, hb[:, k, :], hb[:, k, :], col("lng", k), col("lnb", k), ALU.mult, ALU.add, a)
            yield
            cv = []
            for m in range(4):
                b, over = takeb()
                for k in range(2):
                    tok = mm(b.buf[:, :], w1[:, k, m * 128:(m + 1) * 128], hb[:, k, :], k == 0, k == 1, over, xn, w_tok1,
                             signal=k == 1)
                a = act(xcb[:, m, 3:TB + 3], b.buf[:, :], ACT.Identity, tok, halo1)
                b.free = [a]
                yield
                c = u[p][:, m, :]
                a = ts(DVE, c, xcb[:, m, 0:TB], col("cw1", 4 * m), col("cb1", m), ALU.mult, ALU.add, a, fb.get(("u", p)))
                for k in range(1, 4):
                    a = stt(c, xcb[:, m, k:k + TB], col("cw1", 4 * m + k), c, ALU.mult, ALU.add, a)
                    if k == 2:
                        yield
                cv.append(a)
                yield
            halo1 = [SCA(lambda e: e.activation(xcb[:, :, 0:3], xcb[:, :, TB:TB + 3], ACT.Identity), a)]
            for m in range(4):
                b, over = takeb()
                for k in range(2):
                    tok = mm(b.buf[:, :], w1[:, k, 512 + m * 128:640 + m * 128], hb[:, k, :], k == 0, k == 1, over,
                             signal=k == 1)
                zt = act(sz[p][:, m, :], b.buf[:, :], ACT.Identity, tok, fb.get(("sz", p)))
                b.free = [zt]
                yield
            fb["hb"] = [tok]
            tf = fb.get("th")
            for i in range(4):
                what = (u[p], sz[p])[i // 2][:, 2 * (i % 2):2 * (i % 2) + 2, :]
                a = act(th1[:, :, :], what, ACT.Tanh, cv, zt, tf)
                a = stt(what, th1[:, :, :], 1.0, what, ALU.add, ALU.mult, a)
                tf = [a]
                if i == 1:
                    u_tok[ib] = a
                if i == 3:
                    sz_tok[ib] = a
            yield
            b, over = takeb()
            for k in range(4):
                tok = mm(b.buf[0:48, :], wxp[:, k, :], u[p][:, k, :], k == 0, k == 3, over, u_tok[ib], wxp_tok,
                         signal=k == 3)
            db = act(dbc[:, :], b.buf[0:48, :], ACT.Identity, tok, fb.get("dbc"))
            b.free = [db]
            bcs_tok[ib] = SP.dma(lane("bcs"), t["bc"][ib], dbc[16:48, :], db)
            yield
            for m in range(4):
                b, over = takeb()
                tok = mm(b.buf[:, :], wdt[:, m * 128:(m + 1) * 128], dbc[0:16, :], True, True, over, db, wdt_tok,
                         signal=True)
                v = ts(DVE, dtt[p][:, m, :], b.buf[:, :], col("bdt", m), None, ALU.add, None, tok, fb.get(("dt", p)))
                b.free = [v]
                if m % 2 == 0:
                    yield
                    continue
                what = dtt[p][:, m - 1:m + 1, :]
                a = act(th1[:, :, :], what, ACT.Abs, v, tf)
                a = act(th1[:, :, :], th1[:, :, :], ACT.Exp, a, scale=-1.0)
                a = act(th1[:, :, :], th1[:, :, :], ACT.Ln, a, bias=1.0)
                yield
                dt1_tok[ib] = stt(what, what, 0.0, th1[:, :, :], ALU.max, ALU.add, a)
                tf = [dt1_tok[ib]]
                yield
            fb["dbc"] = [tok, bcs_tok[ib]]
            fb["th"] = tf

        bc_tok, bc_free = {}, {}

        def load_bc(i):
            ib, n = divmod(i, 8)
            if ib >= NB:
                return
            src = t["bc"][ib].rearrange("(w n) s -> w n s", w=2)[:, 2 * n:2 * n + 2, :]
            toks = []
            for w in range(2):
                toks.append(SP.dma(lane(f"bc{w}{i % 3}"), bcr[i % 3][:, w, :, :],
                                   src[w:w + 1, :, :].broadcast_to([128, 2, TB]), bcs_tok[ib], bc_free.get(i - 3)))
            bc_tok[i] = toks

        def scan_b(ib):
            p = ib % 2
            for k in range(3 if ib == 0 else 0):
                load_bc(k)
            if ib:
                for k in range(3):
                    load_bc(8 * ib + k)
            du_tok = {}
            for m in range(4):
                du_tok[m] = tt(DVE, du[:, m, :], dtt[p][:, m, :], u[p][:, m, :], ALU.mult, dt1_tok[ib], u_tok[ib],
                               fb.get("du"))
            for n in range(8):
                i = 8 * ib + n
                bc = bcr[i % 3]
                for m in range(4):
                    dB, over = dBr.take()
                    db_tok = tt(POOL, dB.buf[:, :, :], du[:, m, None, :].broadcast_to([128, 2, TB]), bc[:, 0, :, :],
                                ALU.mult, du_tok[m], bc_tok[i], over)
                    dA_, over = dAr.take()
                    for j in range(2):
                        q = 16 * m + 2 * n + j
                        da_tok = act(dA_.buf[:, j, :], dtt[p][:, m, :], ACT.Exp, dt1_tok[ib], A1_tok, over,
                                     scale=A1[:, q:q + 1])
                    hh, over = hr.take()
                    for j in range(2):
                        s_tok = DVE(lambda e, hh=hh, dA_=dA_, dB=dB, j=j, m=m, n=n: e.tensor_tensor_scan(
                            hh.buf[:, j, :], dA_.buf[:, j, :], dB.buf[:, j, :], hst[:, m, 2 * n + j:2 * n + j + 1],
                            ALU.mult, ALU.add), da_tok, db_tok, h_prev[m, n], over)
                    dB.free, dA_.free = [s_tok], [s_tok]
                    h_prev[m, n] = [DVE(lambda e, hh=hh, m=m, n=n: e.tensor_copy(
                        hst[:, m, 2 * n:2 * n + 2], hh.buf[:, :, TB - 1]), s_tok)]
                    c_ = tt(DVE, hh.buf[:, :, :], hh.buf[:, :, :], bc[:, 1, :, :], ALU.mult, s_tok, bc_tok[i],
                            h_prev[m, n])
                    for j in range(2):
                        tok = mm(yb[m][:, :], ident, hh.buf[:, j, :], n == 0 and j == 0, n == 7 and j == 1,
                                 c_, y_free[m] if n == 0 and j == 0 else None, signal=j == 1)
                    hh.free = [tok]
                    y_tok[m] = tok
                    yield
                bc_free[i] = [db_tok, c_]
                if n < 5:
                    load_bc(i + 3)
            fb["du"] = [db_tok]
            fb[("dt", p)] = [da_tok, du_tok[3]]
            for m in range(4):
                a = stt(u[p][:, m, :], u[p][:, m, :], col("D1", m), yb[m][:, :], ALU.mult, ALU.add, y_tok[m], du_tok[m])
                y_free[m] = [a]
                g_tok = tt(DVE, u[p][:, m, :], u[p][:, m, :], sz[p][:, m, :], ALU.mult, a, sz_tok[ib])
            fb[("sz", p)] = [g_tok]
            gate_tok[ib] = g_tok

        y_tok, gate_tok = {}, {}
        out_toks = []
        x3_free = [over_a]
        xs_tok, xn3_tok = {}, {}
        sum_toks = []

        def post_b(ib):
            nonlocal x3_free
            p = ib % 2
            blk = slice(ib * TB, (ib + 1) * TB)
            x_tok = SP.dma(lane("x3"), x3[:, :, :], t["x2"][:, :, blk], x2_tok[ib], x3_free)
            for m in range(2):
                b, over = takeb()
                for k in range(4):
                    tok = mm(b.buf[:, :], wo1[:, k, m * 128:(m + 1) * 128], u[p][:, k, :], k == 0, k == 3, over,
                             gate_tok[ib], wo1_tok, signal=k == 3)
                x_tok = tt(DVE, x3[:, m, :], x3[:, m, :], b.buf[:, :], ALU.add, tok, x_tok)
                b.free = [x_tok]
                yield
            fb[("u", p)] = [tok]
            xs_tok[ib] = SP.dma(lane(f"x3s{ib}"), t["x3"][:, :, blk], x3[:, :, :], x_tok)
            yield from layer_norm(takeb, x3, x3, sq1, r1, [x_tok], [xs_tok[ib]])
            xn = done[0]
            sum_toks.append(DVE(lambda e: e.tensor_reduce(sums[:, :, ib], x3[:, :, :], AX.X, ALU.add), xn))
            xn3_tok[ib] = SP.dma(lane(f"xn3{ib}"), t["xn3"][:, :, blk], x3[:, :, :], xn)
            x3_free = [xn3_tok[ib], sum_toks[-1]]
            yield

        def chain(*gens):
            for g in gens:
                yield from g

        run(pre_b(0))
        for ib in range(NB):
            parts = []
            if ib >= 1:
                parts.append(post_b(ib - 1))
            if ib + 1 < NB:
                parts += [product_b(ib + 1), pre_b(ib + 1)]
            side = chain(*parts)
            total = 32 + 33 + 8
            gone = 0
            for i, _ in enumerate(scan_b(ib)):
                want = (i + 1) * total // 31
                while gone < want:
                    next(side, None)
                    gone += 1
            run(side)
        run(post_b(NB - 1))
        over_b = barrier()
        cB.close()

        cC = ExitStack()
        mean = sb(cC, "mean", [128, 2])
        Wr = sb(cC, "Wr", [128, 2, 8])
        br = sb(cC, "br", [1, 8])
        q = sb(cC, "q", [1, 16, 8])
        idx = sb(cC, "idx", [1, 8], U32)
        tw = sb(cC, "tw", [128, 2])
        W1 = sb(cC, "W1", [128, 2, 2, 512])
        W2 = sb(cC, "W2", [128, 2, 4, D])
        b1 = sb(cC, "b1", [128, 2, 4])
        b2 = sb(cC, "b2", [128, 2, 2])
        b2c = sb(cC, "b2c", [128, 2])
        xn = [sb(cC, f"xn{i}", [128, 2, TB]) for i in range(3)]
        xr = [sb(cC, f"xr{i}", [128, 2, TB]) for i in range(3)]
        G = [sb(cC, f"G{i}", [128, 8, TB]) for i in range(2)]
        o = [sb(cC, f"o{i}", [128, 2, TB]) for i in range(2)]
        sq2 = [sb(cC, f"sq2{i}", [128, 2, TB]) for i in range(2)]
        r2 = [sb(cC, f"r2{i}", [128, TB]) for i in range(2)]

        ring_c = Ring(P)
        takec = ring_c.take

        wr_tok = SP.dma(lane("Wr"), Wr[:, :, :], t["Wr"], over_b)
        br_tok = SP.dma(lane("br"), br[:, :], t["br"], over_b)
        xn_tok, xr_tok, c_free = {}, {}, {}

        def load_c(ib):
            if ib < NB:
                blk = slice(ib * TB, (ib + 1) * TB)
                xn_tok[ib] = SP.dma(lane(f"cxn{ib % 3}"), xn[ib % 3][:, :, :], t["xn3"][:, :, blk], over_b,
                                    xn3_tok[ib], c_free.get(ib - 3))
                xr_tok[ib] = SP.dma(lane(f"cxr{ib % 3}"), xr[ib % 3][:, :, :], t["x3"][:, :, blk], over_b,
                                    xs_tok[ib], c_free.get(ib - 3))

        for ib in range(3):
            load_c(ib)
        a = DVE(lambda e: e.tensor_reduce(mean[:, :], sums[:, :, :], AX.X, ALU.add), over_b, sum_toks)
        b, over = takec()
        for k in range(2):
            tok = mm(b.buf[0:1, 0:8], mean[:, k:k + 1], Wr[:, k, :], k == 0, k == 1, over_b, a, wr_tok, signal=k == 1)
        row = [q[:, i, :] for i in range(16)]

        def softmax_row(x, y, a):
            mx, s, rs = row[13][:, 0:1], row[14][:, 0:1], row[15][:, 0:1]
            a = DVE(lambda e: e.tensor_reduce(mx, x, AX.X, ALU.max), a)
            a = ts(DVE, y, x, mx, None, ALU.subtract, None, a)
            a = act(y, y, ACT.Exp, a, accum=s)
            a = DVE(lambda e: e.reciprocal(rs, s), a)
            return ts(DVE, y, y, rs, None, ALU.mult, None, a)

        a = stt(row[0], b.buf[0:1, 0:8], 1.0 / N, br[:, :], ALU.mult, ALU.add, tok, br_tok)
        b.free = [a]
        a = softmax_row(row[0], row[1], a)
        cap = float(-(-N * 5 // 4 // 8))
        a = ts(DVE, row[2], row[1], float(N), 1e-30, ALU.mult, ALU.max, a)
        a = DVE(lambda e: e.reciprocal(row[3], row[2]), a)
        a = ts(DVE, row[3], row[3], cap, 1.0, ALU.mult, ALU.min, a)
        a = tt(DVE, row[4], row[1], row[3], ALU.mult, a)
        a = softmax_row(row[4], row[5], a)
        a = DVE(lambda e: e.max(row[6], row[5]), a)
        idx_tok = DVE(lambda e: e.max_index(idx[:, :], row[6], row[5]), a)
        a = ts(DVE, row[7][:, 0:2], row[6][:, 0:2], row[6][:, 0:1], None, ALU.subtract, None, idx_tok)
        a = act(row[8][:, 0:2], row[7][:, 0:2], ACT.Exp, a, accum=row[9][:, 0:1])
        a = DVE(lambda e: e.reciprocal(row[10][:, 0:1], row[9][:, 0:1]), a)
        a = ts(DVE, row[11][:, 0:2], row[8][:, 0:2], row[10][:, 0:1], None, ALU.mult, None, a)
        b, over = takec()
        tok = mm(b.buf[:, 0:2], one[0:1, :], row[11][:, 0:2], True, True, over, a, signal=True)
        tw_tok = DVE(lambda e: e.tensor_copy(tw[:, :], b.buf[:, 0:2]), tok)
        b.free = [tw_tok]

        e_tok = []
        for k in range(2):
            got = {}

            def first(e, k=k, got=got):
                v = e.value_load(idx[0:1, k:k + 1], min_val=0, max_val=7)
                got["v"] = v
                return e.dma_start(W1[:, k, :, :], t["W1"][bass.ds(v, 1)].rearrange("o p k f -> p (o k) f"))

            ln = lane(f"e1{k}")
            ln.count += 16
            SP.ops.append(([idx_tok], first, ln.sem, 16))
            e_tok.append((ln.sem, ln.count))
            for name, dst, pat in (("b1", b1[:, k, :], "o p m -> p (o m)"), ("W2", W2[:, k, :, :], "o p k f -> p (o k) f"),
                                   ("b2", b2[:, k, :], "o p m -> p (o m)")):
                ln = lane(f"{name}{k}")
                ln.count += 16
                SP.ops.append(([], lambda e, name=name, dst=dst, pat=pat, got=got: e.dma_start(
                    dst, t[name][bass.ds(got["v"], 1)].rearrange(pat)), ln.sem, 16))
                e_tok.append((ln.sem, ln.count))
        ew = []
        for k in range(2):
            ew.append(ts(DVE, W2[:, k, :, :], W2[:, k, :, :], tw[:, k:k + 1], None, ALU.mult, None, tw_tok, e_tok))
        a = ts(DVE, b2[:, 0, :], b2[:, 0, :], tw[:, 0:1], None, ALU.mult, None, tw_tok, e_tok)
        b2_tok = stt(b2c[:, :], b2[:, 1, :], tw[:, 1:2], b2[:, 0, :], ALU.mult, ALU.add, a)

        def experts(ib):
            x, res, g, oo = xn[ib % 3], xr[ib % 3], G[ib % 2], o[ib % 2]
            gt = []
            for e in range(2):
                for f in range(4):
                    b, over = takec()
                    for k in range(2):
                        tok = mm(b.buf[:, :], W1[:, e, k, f * 128:(f + 1) * 128], x[:, k, :], k == 0, k == 1, over,
                                 xn_tok[ib], e_tok, signal=k == 1)
                    a = act(g[:, 4 * e + f, :], b.buf[:, :], ACT.Gelu, tok, c_free.get(("G", ib - 2)),
                            bias=b1[:, e, f:f + 1])
                    b.free = [a]
                    gt.append(a)
            yield
            for d in range(2):
                b, over = takec()
                for i in range(8):
                    tok = mm(b.buf[:, :], W2[:, i // 4, i % 4, d * 128:(d + 1) * 128], g[:, i, :], i == 0, i == 7, over,
                             gt[i], ew, signal=i == 7)
                a = stt(oo[:, d, :], b.buf[:, :], b2c[:, d:d + 1], x[:, d, :], ALU.add, ALU.add, tok, b2_tok,
                        c_free.get(("o", ib - 2)))
                b.free = [a]
            c_free[("G", ib)] = tok
            yield
            yield from layer_norm(takec, oo, oo, sq2[ib % 2], r2[ib % 2], a, c_free.get(("o", ib - 2)))
            a = done[0]
            for k in range(2):
                a = ts(DVE, oo[:, k, :], oo[:, k, :], col("gamma", k), col("beta", k), ALU.mult, ALU.add, a)
            a = tt(DVE, oo[:, :, :], oo[:, :, :], res[:, :, :], ALU.add, a, xr_tok[ib])
            c_free[ib] = [a]
            c_free[("o", ib)] = SP.dma(lane(f"out{ib % 2}"), t["out"][:, :, ib * TB:(ib + 1) * TB], oo[:, :, :], a)
            load_c(ib + 3)

        prev = None
        for ib in range(NB):
            gen = experts(ib)
            next(gen)
            if prev is not None:
                run(prev)
            next(gen)
            prev = gen
        run(prev)
        ends = [c_free[("o", NB - 1)], c_free[("o", NB - 2)]]
        cC.close()

        block = ctx.enter_context(nc.Block())

        @block.sync
        def _(e):
            SP.play(e)
            for s, v in ends:
                e.wait_ge(s, v)
            for ln in lanes.values():
                e.wait_ge(ln.sem, ln.count)

        @block.tensor
        def _(e):
            PE.play(e)

        @block.vector
        def _(e):
            DVE.play(e)

        @block.scalar
        def _(e):
            SCA.play(e)

        @block.gpsimd
        def _(e):
            POOL.play(e)


def kernel(**inputs):
    import concourse.bacc as bacc
    from concourse.bass_utils import run_bass_kernel_spmd

    a = {k: np.asarray(v) for k, v in inputs.items()}
    f = np.float32

    def tiles(w):
        return w.reshape(-1, 128, w.shape[-1]).transpose(1, 0, 2)

    def cols(v):
        return v.reshape(-1, 128).T

    def pad(v):
        return np.concatenate([v, np.zeros((64,) + v.shape[1:], f)])

    tri = np.triu(np.ones((128, 128), f))
    consts = np.stack([np.eye(128, dtype=f), tri, np.tril(np.ones((128, 128), f), -1), np.full((128, 128), 1 / 256, f),
                       np.ones((128, 128), f)], 1)
    cw, cb = a["L0_ffn_conv_w"], a["L0_ffn_conv_b"]
    cw = np.concatenate([cw[:512], pad(cw[512:576]), pad(cw[576:])])
    cb = np.concatenate([cb[:512], pad(cb[512:576]), pad(cb[576:])])
    parts = {
        "cw0": cw.reshape(6, 128, 4).transpose(1, 0, 2).reshape(128, 24), "cb0": cols(cb),
        "cw1": a["L1_gnn_conv_w"].reshape(4, 128, 4).transpose(1, 0, 2).reshape(128, 16),
        "cb1": cols(a["L1_gnn_conv_b"]), "D0": cols(np.repeat(a["L0_ffn_D"], 64)), "nw": cols(a["L0_ffn_norm_w"]),
        "blin": cols(a["L0_ffn_b_lin"]), "gcnb": cols(a["L1_gnn_gcn_b"]), "lng": cols(a["L1_gnn_ln_g"]),
        "lnb": cols(a["L1_gnn_ln_b"]), "bdt": cols(a["L1_gnn_b_dt"]),
        "A1": a["L1_gnn_A_log"].reshape(4, 128, 16).transpose(1, 0, 2).reshape(128, 64),
        "D1": cols(a["L1_gnn_D_skip"]), "gamma": cols(a["L1_ffn_gamma"]), "beta": cols(a["L1_ffn_beta"]),
    }
    wp = np.zeros((128, 4, 512), f)
    wp[:, 0:2, :] = tiles(np.ascontiguousarray(a["L0_ffn_W_out"].T))
    arrays = {
        "xT": tiles(a["x"].T),
        "adjT": a["adj"].reshape(NB, TB, NJ, 128).transpose(0, 3, 2, 1),
        "consts": consts,
        "cols": np.concatenate([parts[k] for k in COLS], 1),
        "rows": np.concatenate([a["L0_gnn_B"], np.tile(a["L0_ffn_dt_bias"], 4), a["L0_ffn_A_log"]])[None],
        "W0": tiles(a["L0_gnn_W"]), "Win": tiles(a["L0_ffn_W_in"]), "WoutT": wp,
        "Wlin": tiles(a["L0_ffn_W_lin"]), "Wg": tiles(a["L1_gnn_gcn_w"]), "w1": tiles(a["L1_gnn_w_in"]),
        "wxp": tiles(a["L1_gnn_w_xp"]), "wdt": a["L1_gnn_w_dt"], "wo1": tiles(a["L1_gnn_w_out"]),
        "Wr": tiles(a["L1_ffn_Wr"]), "br": a["L1_ffn_br"][None],
        "W1": a["L1_ffn_W1"].reshape(8, 2, 128, 512).transpose(0, 2, 1, 3),
        "W2": a["L1_ffn_W2"].reshape(8, 4, 128, 256).transpose(0, 2, 1, 3),
        "b1": a["L1_ffn_b1"].reshape(8, 4, 128).transpose(0, 2, 1),
        "b2": a["L1_ffn_b2"].reshape(8, 2, 128).transpose(0, 2, 1),
    }
    arrays = {"in_" + k: np.ascontiguousarray(v) for k, v in arrays.items()}
    nc = bacc.Bacc("TRN2", target_bir_lowering=False, num_devices=1)
    t = {k[3:]: nc.dram_tensor(k, v.shape, mybir.dt.from_np(v.dtype), kind="ExternalInput").ap()
         for k, v in arrays.items()}
    for name, shape in (("x2", (128, 2, N)), ("x3", (128, 2, N)), ("xn3", (128, 2, N)), ("bc", (NB, 32, TB))):
        t[name] = nc.dram_tensor("tmp_" + name, shape, F32, kind="Internal").ap()
    t["out"] = nc.dram_tensor("out_0", (128, 2, N), F32, kind="ExternalOutput").ap()
    build(nc, t)
    r = run_bass_kernel_spmd(nc, [arrays], core_ids=[0])
    got = r.results[0]["out_0"]
    return np.ascontiguousarray(got.transpose(2, 1, 0).reshape(N, D))
```

```python
import numpy as np
import concourse.bass as bass
from concourse import mybir
from contextlib import ExitStack

F32 = mybir.dt.float32
U32 = mybir.dt.uint32
ALU = mybir.AluOpType
ACT = mybir.ActivationFunctionType
AX = mybir.AxisListType

N, D, TB = 4096, 256, 512
NB = N // TB
NJ = N // 128
NW = 5
EA, EB, ES = 3000.0, 0.0, 2000.0
EPS = 1e-5
TINY = 1e-18
LNEXP = "natural_log_exp_and_others"
TANH = "exp_and_others"
GELU = "gelu_and_others"

COLS = {}
_at = 0
for _name, _n in (("cw0", 24), ("cb0", 6), ("cw1", 16), ("cb1", 4), ("D0", 4), ("nw", 4), ("blin", 2), ("gcnb", 2),
                  ("lng", 2), ("lnb", 2), ("bdt", 4), ("A1", 64), ("D1", 4), ("gamma", 2), ("beta", 2)):
    COLS[_name] = (_at, _n)
    _at += _n
NCOL = _at
HALVED = COLS["D0"][0]
NROW = 256 + 32 + 8


class Line:

    def __init__(self, sem, times):
        self.sem, self.count, self.ops, self.times, self.clock, self.last = sem, 0, [], times, 0.0, 0.0

    def guess(self, after, cost, mark, late=0.0):
        start = max([self.clock] + [self.times.get((id(s), v), 0.0) for s, v in after])
        self.clock = start + cost
        self.times["now"] = max(self.times.get("now", 0.0), self.clock + late)
        if mark is not None:
            self.times[(id(mark[0]), mark[1])] = self.clock + late

    def __call__(self, fn, *after, signal=True, cost=200.0):
        after = list(flat(after))
        self.ops.append((after, fn, self.sem if signal else None, 1))
        self.count += signal
        mark = (self.sem, self.count) if signal else None
        self.guess(after, cost, mark)
        return mark

    def dma(self, lane, out, in_, *after, **kw):
        lane.count += 16
        after = list(flat(after))
        self.ops.append((after, lambda e: e.dma_start(out, in_, **kw), lane.sem, 16))
        self.guess(after, 60.0, (lane.sem, lane.count), 2500.0 + size(out) / 1.5)
        return (lane.sem, lane.count)

    def play(self, engine):
        seen = {}
        for after, fn, sem, step in self.ops:
            for s, value in after:
                if seen.get(id(s), 0) < value:
                    seen[id(s)] = value
                    engine.wait_ge(s, value)
            ins = fn(engine)
            if sem is not None:
                ins.then_inc(sem, step)


def tuple_of(tok):
    return None if tok is None else (id(tok[0]), tok[1])


def size(ap):
    n = 1
    for d in list(ap.shape)[1:]:
        n *= d
    return n


def weave(*parts):
    live = [[0.0, line, ease, g] for g, line, ease in parts]
    while live:
        part = min(live, key=lambda p: max(p[0], p[1].clock) - p[2])
        times = part[1].times
        times["now"] = 0.0
        got = next(part[3], "end")
        if isinstance(got, str):
            live.remove(part)
        else:
            part[0] = times["now"] if got is None else got


def steps(gen, n):
    for _ in range(n):
        got = next(gen, "end")
        if isinstance(got, str):
            return
        yield got


class Lane:

    def __init__(self, sem):
        self.sem, self.count = sem, 0


def flat(after):
    for a in after:
        if a is None:
            continue
        if isinstance(a, list):
            yield from flat(a)
        else:
            yield a


class Slot:

    def __init__(self, buf):
        self.buf, self.free = buf, []


class Ring:
    def __init__(self, bufs):
        self.slots, self.at = [Slot(b) for b in bufs], 0

    def take(self):
        s = self.slots[self.at % len(self.slots)]
        self.at += 1
        assert s.free is not None, "the slot has no reader yet"
        over, s.free = s.free, None
        return s, over


def build(nc, t):
    with ExitStack() as ctx:
        def sem(name):
            return ctx.enter_context(nc.semaphore(name))

        def sb(c, name, shape, dt=F32):
            return c.enter_context(nc.sbuf_tensor(name, shape, dt))

        times = {}
        PE, DVE, SCA, POOL, SP = (Line(sem(n), times) for n in ("s_pe", "s_dve", "s_act", "s_pool", "s_sp"))
        lanes = {}

        def lane(name):
            if name not in lanes:
                lanes[name] = Lane(sem("d_" + name))
            return lanes[name]

        def mm(out, lhsT, rhs, start, stop, *after, signal=False, skip=False):
            return PE(lambda e: e.matmul(out, lhsT, rhs, start=start, stop=stop, skip_group_check=skip),
                      *after, signal=signal, cost=max(64, size(out)) * 1.667 + 4)

        def tr(out, in_, ident, *after, signal=False):
            return PE(lambda e: e.transpose(out, in_, ident), *after, signal=signal, cost=109)

        table = [None]

        def act(out, in_, func, *after, scale=1.0, bias=0.0, accum=None):
            need = {ACT.Ln: LNEXP, ACT.Exp: LNEXP, ACT.Tanh: TANH, ACT.Gelu: GELU}.get(func)
            if need is not None and table[0] != need:
                table[0] = need
                SCA(lambda e: e.preload_act_table_set(need), signal=False, cost=1283)
            if accum is None:
                return SCA(lambda e: e.activation(out, in_, func, bias=bias, scale=scale), *after,
                           cost=size(out) / 1.2 + 120)
            return SCA(lambda e: e.activation(out, in_, func, bias=bias, scale=scale, accum_out=accum), *after,
                       cost=size(out) / 1.2 + 250)

        def tt(line, out, a, b, op, *after):
            return line(lambda e: e.tensor_tensor(out, a, b, op), *after,
                        cost=size(out) * (2.2 if line is POOL else 1.04) + 130)

        def ts(line, out, a, s1, s2, op0, op1, *after):
            if op1 is None:
                return line(lambda e: e.tensor_scalar(out, a, s1, None, op0), *after, cost=size(out) * 0.6 + 130)
            return line(lambda e: e.tensor_scalar(out, a, s1, s2, op0, op1), *after, cost=size(out) * 0.6 + 130)

        def stt(out, a, s, b, op0, op1, *after):
            return DVE(lambda e: e.scalar_tensor_tensor(out, a, s, b, op0, op1), *after, cost=size(out) * 1.04 + 130)

        def barrier():
            now = [(l.sem, l.count) for l in (PE, DVE, SCA, POOL) if l.count]
            now += [(l.sem, l.count) for l in lanes.values() if not l.sem in raw_sems]
            return now

        P = [ctx.enter_context(nc.psum_tensor(f"ps{i}", [128, 512], F32)) for i in range(8)]
        consts = sb(ctx, "consts", [128, 5, 128])
        ident, tri, trig, avg, one = (consts[:, i, :] for i in range(5))
        cols = sb(ctx, "cols", [128, NCOL])
        raw = [sb(ctx, f"raw{i}", [128, 2, TB]) for i in range(4)]
        msg = sb(ctx, "msg", [128, NJ, D])

        def col(name, i=0, n=1):
            a = COLS[name][0] + i
            return cols[:, a:a + n]

        c_tok = SP.dma(lane("consts"), consts[:, :, :], t["consts"])
        k_tok = SP.dma(lane("cols"), cols[:, :], t["cols"])
        k_tok = ts(DVE, cols[:, 0:HALVED], cols[:, 0:HALVED], 0.5, None, ALU.mult, None, k_tok)

        NCH = NB * NJ // 2
        raw_tok = {}
        raw_lanes = [lane(f"raw{i}") for i in range(4)]
        raw_sems = [l.sem for l in raw_lanes]

        def load_raw(g, *after):
            if g >= 2 * NCH:
                return
            ib, q = divmod(g % NCH, NJ // 2)
            raw_tok[g] = SP.dma(raw_lanes[g % 4], raw[g % 4][:, :, :], t["adjT"][ib, :, 2 * q:2 * q + 2, :], *after)

        for g in range(4):
            load_raw(g)

        def layer_norm(take, x, xc, sq, r, x_tok, free):
            m, over = take()
            for k in range(2):
                tok = mm(m.buf[:, :], avg, x[:, k, :], k == 0, k == 1, over, x_tok, c_tok, signal=k == 1)
            sub = tt(DVE, xc[:, :, :], x[:, :, :], m.buf[:, None, :].broadcast_to([128, 2, TB]), ALU.subtract, tok, free)
            m.free = [sub]
            yield
            s = act(sq[:, :, :], xc[:, :, :], ACT.Square, sub, free)
            yield
            v, over = take()
            for k in range(2):
                tok = mm(v.buf[:, :], avg, sq[:, k, :], k == 0, k == 1, over, s, signal=k == 1)
            yield
            l = act(r[:, :], v.buf[:, :], ACT.Ln, tok, free, bias=EPS)
            v.free = [l]
            l = act(r[:, :], r[:, :], ACT.Exp, l, scale=-0.5)
            yield
            done[0] = tt(DVE, xc[:, :, :], xc[:, :, :], r[:, None, :].broadcast_to([128, 2, TB]), ALU.mult, l)

        done = [None]

        def run(gen):
            for _ in gen:
                pass

        cA = ExitStack()
        wgt = [sb(cA, f"wgt{i}", [128, 2, TB]) for i in range(NW)]
        W0 = sb(cA, "W0", [128, 2, D])
        Win = sb(cA, "Win", [128, 2, 1160])
        Wc = sb(cA, "Wc", [128, 4, D])
        rows = sb(cA, "rows", [128, NROW])
        Bbc, dtb, Abc = rows[:, 0:256], rows[:, 256:288], rows[:, 288:296]
        diagD = sb(cA, "diagD", [128, 4, 128])
        xbs = [sb(cA, f"xb{i}", [128, 2, TB]) for i in range(2)]
        xb = xbs[0]
        xc = sb(cA, "xc", [128, 2, TB])
        sq = sb(cA, "sq", [128, 2, TB])
        rr = sb(cA, "rr", [128, TB])
        xbc = sb(cA, "xbc", [128, 6, TB + 3])
        ccs = [sb(cA, f"cc{i}", [128, 6, TB]) for i in range(2)]
        cc = ccs[0]
        th = sb(cA, "th", [128, 2, TB])
        zs = [sb(cA, f"z{i}", [128, 4, TB]) for i in range(2)]
        sms = [sb(cA, f"sm{i}", [128, 4, 32]) for i in range(2)]
        ecd = sb(cA, "ecd", [128, 3, 4, 8])
        ms = sb(cA, "ms", [128, 4])
        rms = sb(cA, "rms", [128, 4])
        rdA = sb(cA, "rdA", [128, 8, 128])
        E = [sb(cA, f"E{i}", [128, 8, 128]) for i in range(2)]
        xdt = [sb(cA, f"xdt{i}", [128, 512]) for i in range(2)]
        xdecs = [sb(cA, f"xdec{i}", [128, 512]) for i in range(2)]
        bns = [sb(cA, f"bn{i}", [128, 64]) for i in range(2)]
        cbms = [sb(cA, "cbm", [128, 128])] * 2
        tmp = sb(cA, "tmp", [128, 512])
        Y2 = sb(cA, "Y2", [128, 4, 512])
        YT = sb(cA, "YT", [128, 4, TB])
        h0 = sb(cA, "hs0", [64, 512])
        hd = sb(cA, "hd", [64, 512])

        w0_tok = SP.dma(lane("W0"), W0[:, :, :], t["W0"])
        rows_tok = SP.dma(lane("rows"), rows[:, :], t["rows"].broadcast_to([128, NROW]))
        win_tok = SP.dma(lane("Win"), Win[:, :, :], t["Win"])
        wout_tok = SP.dma(lane("Wout"), Y2[:, :, :], t["WoutT"])
        wlin_tok = SP.dma(lane("Wlin"), YT[:, 0:2, 0:256], t["Wlin"])

        ring = Ring(P[2:8])
        take = ring.take

        a_tok = act(Abc, Abc, ACT.Exp, rows_tok)
        a_tok = ts(DVE, Abc, Abc, -1.0, None, ALU.mult, None, a_tok)
        win_tok = ts(DVE, Win[:, :, 0:512], Win[:, :, 0:512], 0.5, None, ALU.mult, None, win_tok)
        for m in range(4):
            dd_tok = ts(DVE, diagD[:, m, :], ident, col("D0", m), None, ALU.mult, None, c_tok, k_tok)
        woutT = Y2[:, 0:2, :]
        for m in range(4):
            b, over = take()
            for k in range(2):
                tok = mm(b.buf[:, 0:256], woutT[:, k, m * 128:(m + 1) * 128], YT[:, k, 0:256], k == 0, k == 1,
                         over, wout_tok, wlin_tok, signal=k == 1)
            wc_tok = ts(DVE, Wc[:, m, :], b.buf[:, 0:256], col("nw", m), None, ALU.mult, None, tok, k_tok)
            b.free = [wc_tok]
        zero_tok = [POOL(lambda e: e.memset(xbc[:, :, 0:3], 0.0)), POOL(lambda e: e.memset(h0[:, :], 0.0))]

        raw_read = {}
        w_tok = {}
        w_free = {}

        def prep_a(g):
            if g >= NCH:
                return
            two = [(i, wgt[i % NW], raw[i % 4]) for i in (g, g + 1)]
            a = {i: act(w[:, :, :], r[:, :, :], ACT.Ln, raw_tok[i], w_free.get(i - NW), bias=TINY) for i, w, r in two}
            a = {i: act(w[:, :, :], w[:, :, :], ACT.Exp, a[i], scale=-1.0) for i, w, r in two}
            a = {i: stt(w[:, :, :], w[:, :, :], -2.0, w[:, :, :], ALU.add, ALU.mult, a[i]) for i, w, r in two}
            a = {i: act(w[:, :, :], w[:, :, :], ACT.Exp, a[i], scale=-2.0, bias=-2.0) for i, w, r in two}
            for i, w, r in two:
                w_tok[i] = stt(w[:, :, :], r[:, :, :], 1.0, w[:, :, :], ALU.is_lt, ALU.mult, a[i])
                load_raw(i + 4, w_tok[i])

        P_free = [[], []]
        P_tok = [None, None]
        msg1_tok = {}

        def product_a(ib):
            if ib == 0:
                prep_a(0)
            for q in range(NJ // 2):
                g = ib * (NJ // 2) + q
                if g % 2 == 0:
                    prep_a(g + 2)
                for l in range(2):
                    j = 2 * q + l
                    for d in range(2):
                        tok = mm(P[d][:, :], msg[:, j, d * 128:(d + 1) * 128], wgt[g % NW][:, l, :], j == 0, j == NJ - 1,
                                 w_tok[g], msg1_tok[j], P_free[d] if j == 0 else None,
                                 signal=(l == 1 and d == 1) or j == NJ - 1)
                        if j == NJ - 1:
                            P_tok[d] = tok
                    if l == 0:
                        yield 0.0
                w_free[g] = tok
                yield times.get(tuple_of(w_tok.get(g + 1)), 0.0)

        x_free = []

        def messages_0(ib, xb, xc, sq, rr, ln):
            x_tok = SP.dma(lane("x" + ln), xb[:, :, :], t["xT"][:, :, ib * TB:(ib + 1) * TB], bufs.get(ln))
            yield from layer_norm(take, xb, xc, sq, rr, x_tok, bufs.get(ln))
            xn = done[0]
            yield
            last = []
            for s in range(4):
                b, over = take()
                for k in range(2):
                    tok = mm(b.buf[:, 0:256], xc[:, k, s * 128:(s + 1) * 128], W0[:, k, :], k == 0, k == 1,
                             over, xn, w0_tok, signal=k == 1)
                msg1_tok[4 * ib + s] = tt(DVE, msg[:, 4 * ib + s, :], b.buf[:, 0:256], Bbc, ALU.add, tok, rows_tok)
                b.free = [msg1_tok[4 * ib + s]]
                last = [tok]
                yield
            bufs[ln] = last

        bufs = {}
        p = product_a(0)
        second = (cc[:, 0:2, :], cc[:, 2:4, :], cc[:, 4:6, :], th[:, 0, :])
        for pair in range(NB // 2):
            weave((messages_0(2 * pair, xb, xc, sq, rr, "a"), PE, EA), (messages_0(2 * pair + 1, *second, "b"), PE, EA),
                  *([(steps(p, 8), PE, 0.0)] if pair else []))
        run(p)

        h_tok, h_read = zero_tok, []
        x2_tok, msg2_tok = {}, {}
        halo_tok = zero_tok
        free = {("xb", 0): bufs["a"], "xc": bufs["a"], ("cc", 0): bufs["b"], "th": bufs["b"]}
        x1_tok, pre_tok = {}, {}

        def evac_a(ib):
            p = ib % 2
            a = POOL.dma(lane(f"xb{p}"), xbs[p][:, :, :], t["xT"][:, :, ib * TB:(ib + 1) * TB], free.get(("xb", p)))
            for k in range(2):
                a = tt(DVE, xbs[p][:, k, :], xbs[p][:, k, :], P[k][:, :], ALU.add, a, P_tok[k])
                P_free[k] = [a]
            x1_tok[ib] = a

        def pre_a(ib):
            nonlocal halo_tok
            p = ib % 2
            xb, cc, z, sm = xbs[p], ccs[p], zs[p], sms[p]
            yield from layer_norm(take, xb, xc, sq, rr, x1_tok[ib], free["xc"])
            xn = done[0]
            yield
            b, over = take()
            for s in range(4):
                for k in range(2):
                    tok = mm(b.buf[:, 8 * s:8 * s + 8], xc[:, k, s * 128:(s + 1) * 128], Win[:, k, 1152:1160],
                             k == 0, k == 1, over, xn, win_tok, signal=k == 1)
            v, av, dt, dA = sm[:, 0, :], sm[:, 1, :], sm[:, 2, :], sm[:, 3, :]
            a = tt(DVE, v, b.buf[:, 0:32], dtb, ALU.add, tok, rows_tok, free.get(("sm", p)))
            b.free = [a]
            a = act(av, v, ACT.Abs, a)
            a = act(av, av, ACT.Exp, a, scale=-1.0)
            a = act(av, av, ACT.Ln, a, bias=1.0)
            dt_tok = stt(dt, v, 0.0, av, ALU.max, ALU.add, a)
            dA_tok = tt(DVE, dA.rearrange("p (c h) -> p c h", c=4), dt.rearrange("p (c h) -> p c h", c=4),
                        Abc[:, None, :].broadcast_to([128, 4, 8]), ALU.mult, dt_tok, a_tok)
            yield
            cv = []
            for m in range(6):
                w = 128 if m < 4 else 64
                c0 = 512 + 128 * m if m < 4 else 1024 + 64 * (m - 4)
                b, over = take()
                for k in range(2):
                    tok = mm(b.buf[0:w, :], Win[:, k, c0:c0 + w], xc[:, k, :], k == 0, k == 1, over, signal=k == 1)
                a = act(xbc[0:w, m, 3:TB + 3], b.buf[0:w, :], ACT.Identity, tok, halo_tok)
                b.free = [a]
                c = cc[0:w, m, :]
                a = ts(DVE, c, xbc[0:w, m, 0:TB], col("cw0", 4 * m)[0:w, :], col("cb0", m)[0:w, :],
                       ALU.mult, ALU.add, a, k_tok, free.get(("cc", p)))
                for k in range(1, 4):
                    a = stt(c, xbc[0:w, m, k:k + TB], col("cw0", 4 * m + k)[0:w, :], c, ALU.mult, ALU.add, a)
                    if k == 1:
                        yield
                cv.append(a)
                yield
            halo_tok = [POOL(lambda e: e.tensor_copy(xbc[:, 0:4, 0:3], xbc[:, 0:4, TB:TB + 3]), cv),
                        POOL(lambda e: e.tensor_copy(xbc[0:64, 4:6, 0:3], xbc[0:64, 4:6, TB:TB + 3]), cv)]
            for s in range(4):
                b, over = take()
                for k in range(2):
                    tok = mm(b.buf[:, :], xc[:, k, s * 128:(s + 1) * 128], Win[:, k, 0:512], k == 0, k == 1, over,
                             signal=k == 1)
                zt = act(z[:, s, :], b.buf[:, :], ACT.Identity, tok, free.get(("z", p)))
                b.free = [zt]
                if s == 1:
                    yield
            free["xc"] = [tok]
            yield
            sil, ztok = [], []
            tf = free["th"]
            tb = [th, sq]
            for what, w in ((cc[:, 0:2, :], 128), (cc[:, 2:4, :], 128), (cc[0:64, 4:6, :], 64),
                            (z[:, 0:2, :], 128), (z[:, 2:4, :], 128)):
                tz = tb[len(sil) % 2]
                a = act(tz[0:w, :, :], what, ACT.Tanh, cv, zt, tf, sil[-2:-1])
                a = stt(what, tz[0:w, :, :], 1.0, what, ALU.add, ALU.mult, a)
                sil.append(a)
                if len(sil) == 3:
                    yield
            free["th"] = sil[-2:]
            free["xc"] = [tok, sil[-2:]]
            pre_tok[ib] = (sil[2], sil[4], dt_tok, dA_tok)
            yield

        def ssd_a(ib):
            nonlocal h_tok, h_read
            p = ib % 2
            xb, cc, z, sm = xbs[p], ccs[p], zs[p], sms[p]
            dt, dA = sm[:, 2, :], sm[:, 3, :]
            sil_tok, z_tok, dt_tok, dA_tok = pre_tok[ib]
            b, over = take()
            for i, w in enumerate((tri, trig, one)):
                tok = mm(b.buf[:, 32 * i:32 * i + 32], w, dA, True, True, over, dA_tok, signal=i == 2)
            ecd_tok = act(ecd[:, :, :, :].rearrange("p a c h -> p (a c h)"), b.buf[:, 0:96], ACT.Exp, tok, free.get("ecd"))
            b.free = [ecd_tok]
            ms_tok = []
            tmp_free = free.get("tmp")
            rd_free = free.get("rdA")
            made = {}

            def inner(s):
                nonlocal rd_free
                ts_ = slice(s * 128, (s + 1) * 128)
                Es, xd, bn, cbm, xdec = E[s % 2], xdt[s % 2], bns[s % 2], cbms[s % 2], xdecs[s % 2]
                over_s = free.get(("s", s % 2))
                rd = tt(POOL, rdA[:, :, :], tri[:, None, :].broadcast_to([128, 8, 128]),
                        dA[:, 8 * s:8 * s + 8, None].broadcast_to([128, 8, 128]), ALU.mult, dA_tok, rd_free)
                X, over = take()
                for m in range(4):
                    tok = tr(X.buf[:, m * 128:(m + 1) * 128], cc[:, m, ts_], ident, over, sil_tok, signal=m == 3)
                xd_tok = tt(DVE, xd[:, :].rearrange("p (h q) -> p h q", h=8), X.buf[:, :].rearrange("p (h q) -> p h q", h=8),
                            dt[:, 8 * s:8 * s + 8, None].broadcast_to([128, 8, 64]), ALU.mult, tok, dt_tok, over_s)
                X.free = [xd_tok]
                xdec_tok = tt(POOL, xdec[:, :].rearrange("p (h q) -> p h q", h=8),
                              xd[:, :].rearrange("p (h q) -> p h q", h=8),
                              ecd[:, 1, s, :, None].broadcast_to([128, 8, 64]), ALU.mult, xd_tok, ecd_tok, over_s)
                b, over = take()
                tr(b.buf[:, 0:64], cc[0:64, 4, ts_], ident[0:64, 0:64], over)
                tok = mm(b.buf[:, 128:256], cc[0:64, 4, ts_], cc[0:64, 5, ts_], True, True, signal=True)
                bn_tok = DVE(lambda e, b=b: e.tensor_copy(bn[:, :], b.buf[:, 0:64]), tok, over_s)
                cb_tok = tt(DVE, cbm[:, :], b.buf[:, 128:256], tri, ALU.mult, bn_tok, free.get("cbm"))
                b.free = [cb_tok]
                yield
                seg = []
                for i in range(2):
                    b, over = take()
                    rd_free = mm(b.buf[:, :], trig, rdA[:, 4 * i:4 * i + 4, :].rearrange("p h l -> p (h l)"), True, True,
                                 over, rd, signal=True)
                    a = act(Es[:, 4 * i:4 * i + 4, :].rearrange("p h l -> p (h l)"), b.buf[:, :], ACT.Exp, rd_free, over_s)
                    b.free = [a]
                    seg.append(a)
                M_tok = tt(POOL, Es[:, :, :], Es[:, :, :], cbm[:, None, :].broadcast_to([128, 8, 128]), ALU.mult, seg, cb_tok)
                free["cbm"] = [M_tok]
                made[s] = (bn_tok, xd_tok, xdec_tok, M_tok)

            yield from inner(0)
            yield
            for s in range(4):
                ts_ = slice(s * 128, (s + 1) * 128)
                Es, xd, bn, xdec = E[s % 2], xdt[s % 2], bns[s % 2], xdecs[s % 2]
                if s < 3:
                    yield from inner(s + 1)
                    yield
                bn_tok, xd_tok, xdec_tok, M_tok = made[s]
                hd_tok = tt(POOL, hd[:, :].rearrange("p (h q) -> p h q", h=8),
                            h0[:, :].rearrange("p (h q) -> p h q", h=8),
                            ecd[0:64, 2, s, :, None].broadcast_to([64, 8, 64]), ALU.mult, h_tok, ecd_tok)
                Yo, over = take()
                off = mm(Yo.buf[:, :], cc[0:64, 5, ts_], h0[:, :], True, True, over, h_tok, signal=True)
                S, over = take()
                st = mm(S.buf[0:64, :], bn[:, :], xdec[:, :], True, True, over, bn_tok, xdec_tok, signal=True)
                Y, over = take()
                for m in range(4):
                    mm(Y.buf[:, m * 128:(m + 1) * 128], cc[:, m, ts_], diagD[:, m, :], m == 0, False, over, dd_tok,
                       skip=True)
                for h in range(8):
                    dia = mm(Y.buf[:, h * 64:(h + 1) * 64], Es[:, h, :], xd[:, h * 64:(h + 1) * 64], False, h == 7,
                             M_tok, xd_tok, signal=h == 7, skip=True)
                free[("s", s % 2)] = [dia, st, xdec_tok]
                h_tok = tt(DVE, h0[:, :], hd[:, :], S.buf[0:64, :], ALU.add, st, hd_tok, off)
                S.free = [h_tok]
                a = tt(DVE, tmp[:, :].rearrange("p (h q) -> p h q", h=8), Yo.buf[:, :].rearrange("p (h q) -> p h q", h=8),
                       ecd[:, 0, s, :, None].broadcast_to([128, 8, 64]), ALU.mult, off, ecd_tok, tmp_free)
                Yo.free = [a]
                a = tt(DVE, tmp[:, :], tmp[:, :], Y.buf[:, :], ALU.add, a, dia)
                Y.free = [a]
                a = tt(DVE, Y2[:, s, :], tmp[:, :], z[:, s, :], ALU.mult, a, z_tok, free.get("Y2"), wc_tok)
                a = act(tmp[:, :], Y2[:, s, :], ACT.Square, a, accum=ms[:, s:s + 1])
                tmp_free = [a]
                ms_tok.append(a)
                yield
            free[("cc", p)], free[("z", p)], free["rdA"] = [dia, off], [a], rd_free
            free["ecd"] = [st, h_tok, a, xdec_tok]
            free[("sm", p)] = [rd_free, h_tok]
            a = act(rms[:, :], ms[:, :], ACT.Ln, ms_tok, scale=1.0 / 512, bias=EPS)
            rms_tok = act(rms[:, :], rms[:, :], ACT.Exp, a, scale=-0.5)
            for s in range(4):
                y3 = ts(DVE, Y2[:, s, :], Y2[:, s, :], rms[:, s:s + 1], None, ALU.mult, None, rms_tok)
                b, over = take()
                for m in range(4):
                    tok = tr(b.buf[:, m * 128:(m + 1) * 128], Y2[:, s, m * 128:(m + 1) * 128], ident, over, y3,
                             signal=m == 3)
                yt = act(YT[:, :, s * 128:(s + 1) * 128], b.buf[:, :].rearrange("p (m l) -> p m l", m=4), ACT.Identity,
                         tok, free.get("YT"))
                b.free = [yt]
                if s % 2:
                    yield
            free["Y2"] = tok
            for m in range(2):
                b, over = take()
                for k in range(4):
                    tok = mm(b.buf[:, :], Wc[:, k, m * 128:(m + 1) * 128], YT[:, k, :], k == 0, k == 3, over, yt, wc_tok,
                             signal=k == 3)
                x2 = stt(xb[:, m, :], b.buf[:, :], col("blin", m), xb[:, m, :], ALU.add, ALU.add, tok)
                b.free = [x2]
                yield
            free["YT"] = tok
            x2_tok[ib] = POOL.dma(lane(f"x2_{ib}"), t["x2"][:, :, ib * TB:(ib + 1) * TB], xb[:, :, :], x2)
            yield
            yield from layer_norm(take, xb, Y2[:, 0:2, :], Y2[:, 2:4, :], tmp, x2, [free["Y2"], tmp_free])
            xn = done[0]
            free[("xb", p)] = [xn, x2_tok[ib]]
            free["tmp"] = [xn]
            yield
            a = None
            for s in range(4):
                b, over = take()
                for k in range(2):
                    tok = mm(b.buf[:, 0:256], Y2[:, k, s * 128:(s + 1) * 128], Wg[:, k, :], k == 0, k == 1,
                             over, xn, wg_tok, signal=k == 1)
                if ib < NB - 2:
                    a = act(YT[:, s // 2, s % 2 * 256:s % 2 * 256 + 256], b.buf[:, 0:256], ACT.Identity, tok, free["YT"])
                else:
                    a = msg2_tok[4 * ib + s] = act(msg[:, 4 * ib + s, :], b.buf[:, 0:256], ACT.Identity, tok, last_a[0])
                b.free = [a]
            free["Y2"] = [tok]
            if ib < NB - 2:
                m2_tok[ib] = POOL.dma(lane(f"m2_{ib}"), t["m2"][:, 4 * ib:4 * ib + 4, :].rearrange("p a d -> p (a d)"),
                                    YT[:, 0:2, :].rearrange("p a d -> p (a d)"), a)
                free["YT"] = [m2_tok[ib]]
            yield

        Wg = W0
        wg_tok = SP.dma(lane("W0"), W0[:, :, :], t["Wg"], bufs["a"], bufs["b"])

        raw_free = {}

        def product_b(ib):
            for q in range(NJ // 2):
                g = NCH + ib * (NJ // 2) + q
                for l in range(2):
                    j = 2 * q + l
                    for d in range(2):
                        tok = mm(P[d][:, :], msg[:, j, d * 128:(d + 1) * 128], raw[g % 4][:, l, :], j == 0, j == NJ - 1,
                                 raw_tok[g], msg2_tok[j], P_free[d] if j == 0 else None,
                                 signal=(l == 1 and d == 1) or j == NJ - 1)
                        if j == NJ - 1:
                            P_tok[d] = tok
                    if l == 0:
                        yield 0.0
                load_raw(g + 4, tok)
                yield times.get(tuple_of(raw_tok.get(g + 1)), 0.0)

        m2_tok, last_a = {}, [None]
        evac_a(0)
        p1 = product_a(1)
        weave((pre_a(0), PE, EA), (p1, PE, 0.0))
        for ib in range(NB):
            parts = [(ssd_a(ib), PE, EA)]
            if ib + 1 < NB:
                evac_a(ib + 1)
                parts.append((pre_a(ib + 1), PE, EA))
            if ib + 2 < NB:
                parts.append((product_a(ib + 2), PE, 0.0))
            elif ib + 2 == NB:
                last_a[0] = list(P_tok)
                for b in range(NB - 2):
                    tok = SP.dma(lane(f"m2l{b}"), msg[:, 4 * b:4 * b + 4, :], t["m2"][:, 4 * b:4 * b + 4, :],
                                 m2_tok[b], P_tok)
                    for s in range(4):
                        msg2_tok[4 * b + s] = tok
                pb = product_b(0)
                parts.append((steps(pb, 12), PE, 0.0))
            else:
                parts.append((steps(pb, 16), PE, 0.0))
            weave(*parts)
        run(pb)
        over_a = barrier()
        cA.close()

        cB = ExitStack()
        w1 = sb(cB, "w1", [128, 2, 1024])
        wxp = sb(cB, "wxp", [128, 4, 48])
        wdt = sb(cB, "wdt", [16, 512])
        wo1 = sb(cB, "wo1", [128, 4, D])
        sums = sb(cB, "sums", [128, 2, NB])
        u = [sb(cB, f"u{i}", [128, 4, TB]) for i in range(2)]
        sz = [sb(cB, f"sz{i}", [128, 4, TB]) for i in range(2)]
        dtt = [sb(cB, f"dt{i}", [128, 4, TB]) for i in range(2)]
        du = sb(cB, "du", [128, 4, TB])
        bcr = [sb(cB, f"bc{i}", [128, 4, TB]) for i in range(2)]
        dBr = Ring([sb(cB, f"dB{i}", [128, TB]) for i in range(4)])
        hr = Ring([sb(cB, f"h{i}", [128, 4, TB]) for i in range(3)])
        acc = sb(cB, "acc", [128, 4, TB])
        Ct = [sb(cB, f"Ct{i}", [128, 4, 48]) for i in range(2)]
        hst = sb(cB, "hst", [128, 16, 4])
        xcb = sb(cB, "xcb", [128, 4, TB + 3])
        hb = sb(cB, "hb", [128, 2, TB])
        sq1 = sb(cB, "sq1", [128, 2, TB])
        x3 = sb(cB, "x3", [128, 2, TB])
        r1 = sb(cB, "r1", [128, TB])
        th1 = sb(cB, "th1", [128, 2, TB])
        dbc = sb(cB, "dbc", [48, TB])

        ring_b, dAr, hTr = Ring(P[2:4]), Ring(P[4:6]), Ring(P[6:8])
        for s, o in zip(ring_b.slots + dAr.slots + hTr.slots, ring.slots):
            s.free = o.free
        takeb = ring_b.take

        w_tok1 = SP.dma(lane("w1"), w1[:, :, :], t["w1"], over_a)
        wxp_tok = SP.dma(lane("wxp"), wxp[:, :, :], t["wxp"], over_a)
        wdt_tok = SP.dma(lane("wdt"), wdt[:, :], t["wdt"], over_a)
        wo1_tok = SP.dma(lane("wo1"), wo1[:, :, :], t["wo1"], over_a)
        w_tok1 = ts(DVE, w1[:, :, 512:1024], w1[:, :, 512:1024], 0.5, None, ALU.mult, None, w_tok1, over_a)
        A1 = cols[:, COLS["A1"][0]:COLS["A1"][0] + 64]
        a = act(A1, A1, ACT.Exp, k_tok)
        A1_tok = ts(DVE, A1, A1, -1.0, None, ALU.mult, None, a)
        halo1 = [POOL(lambda e: e.memset(xcb[:, :, 0:3], 0.0), over_a)]
        hst_tok = [POOL(lambda e: e.memset(hst[:, :, :], 0.0), over_a)]
        SCA(lambda e: e.activation(th1[:, 0, 0:1], cols[:, 0:1], ACT.Identity), over_a)
        fb = {}
        u_tok, sz_tok, dt1_tok, bcs_tok = {}, {}, {}, {}
        h_prev = {n: hst_tok for n in range(16)}

        hb_tok = {}

        def evac_b(ib):
            for k in range(2):
                hb_tok[ib] = act(hb[:, k, :], P[k][:, :], ACT.Relu, P_tok[k], fb.get("hb"), k_tok, bias=col("gcnb", k))
                P_free[k] = [hb_tok[ib]]

        def pre_b(ib):
            nonlocal halo1
            p = ib % 2
            hbt = hb_tok[ib]
            yield from layer_norm(takeb, hb, hb, sq1, r1, hbt, None)
            a = done[0]
            for k in range(2):
                xn = ts(DVE, hb[:, k, :], hb[:, k, :], col("lng", k), col("lnb", k), ALU.mult, ALU.add, a)
            yield
            cv = []
            for m in range(4):
                b, over = takeb()
                for k in range(2):
                    tok = mm(b.buf[:, :], w1[:, k, m * 128:(m + 1) * 128], hb[:, k, :], k == 0, k == 1, over, xn, w_tok1,
                             signal=k == 1)
                a = act(xcb[:, m, 3:TB + 3], b.buf[:, :], ACT.Identity, tok, halo1)
                b.free = [a]
                yield
                c = u[p][:, m, :]
                a = ts(DVE, c, xcb[:, m, 0:TB], col("cw1", 4 * m), col("cb1", m), ALU.mult, ALU.add, a, fb.get(("u", p)))
                for k in range(1, 4):
                    a = stt(c, xcb[:, m, k:k + TB], col("cw1", 4 * m + k), c, ALU.mult, ALU.add, a)
                    if k == 2:
                        yield
                cv.append(a)
                yield
            halo1 = [SCA(lambda e: e.activation(xcb[:, :, 0:3], xcb[:, :, TB:TB + 3], ACT.Identity), a)]
            for m in range(4):
                b, over = takeb()
                for k in range(2):
                    tok = mm(b.buf[:, :], w1[:, k, 512 + m * 128:640 + m * 128], hb[:, k, :], k == 0, k == 1, over,
                             signal=k == 1)
                zt = act(sz[p][:, m, :], b.buf[:, :], ACT.Identity, tok, fb.get(("sz", p)))
                b.free = [zt]
                yield
            fb["hb"] = [tok]
            tf = fb.get("th")
            for i in range(4):
                what = (u[p], sz[p])[i // 2][:, 2 * (i % 2):2 * (i % 2) + 2, :]
                a = act(th1[:, :, :], what, ACT.Tanh, cv, zt, tf)
                a = stt(what, th1[:, :, :], 1.0, what, ALU.add, ALU.mult, a)
                tf = [a]
                if i == 1:
                    u_tok[ib] = a
                if i == 3:
                    sz_tok[ib] = a
            yield
            b, over = takeb()
            for k in range(4):
                tok = mm(b.buf[0:48, :], wxp[:, k, :], u[p][:, k, :], k == 0, k == 3, over, u_tok[ib], wxp_tok,
                         signal=k == 3)
            db = act(dbc[:, :], b.buf[0:48, :], ACT.Identity, tok, fb.get("dbc"))
            b.free = [db]
            bcs_tok[ib] = SP.dma(lane("bcs"), t["bc"][ib], dbc[16:32, :], db)
            yield
            b, over = takeb()
            for s in range(4):
                tok = tr(b.buf[:, 48 * s:48 * s + 48], dbc[:, s * 128:(s + 1) * 128], ident[0:48, 0:48], over, db,
                         signal=s == 3)
            ct_tok[ib] = act(Ct[p][:, :, :].rearrange("p a n -> p (a n)"), b.buf[:, 0:192], ACT.Identity, tok,
                             fb.get(("Ct", p)))
            b.free = [ct_tok[ib]]
            for m in range(4):
                b, over = takeb()
                tok = mm(b.buf[:, :], wdt[:, m * 128:(m + 1) * 128], dbc[0:16, :], True, True, over, db, wdt_tok,
                         signal=True)
                v = ts(DVE, dtt[p][:, m, :], b.buf[:, :], col("bdt", m), None, ALU.add, None, tok, fb.get(("dt", p)))
                b.free = [v]
                if m % 2 == 0:
                    yield
                    continue
                what = dtt[p][:, m - 1:m + 1, :]
                a = act(th1[:, :, :], what, ACT.Abs, v, tf)
                a = act(th1[:, :, :], th1[:, :, :], ACT.Exp, a, scale=-1.0)
                a = act(th1[:, :, :], th1[:, :, :], ACT.Ln, a, bias=1.0)
                yield
                dt1_tok[ib] = stt(what, what, 0.0, th1[:, :, :], ALU.max, ALU.add, a)
                tf = [dt1_tok[ib]]
                yield
            fb["dbc"] = [tok, bcs_tok[ib]]
            fb["th"] = tf

        bc_tok, bc_free, ct_tok = {}, {}, {}

        def load_bc(i):
            ib, n = divmod(i, 4)
            if ib < NB:
                src = t["bc"][ib][4 * n:4 * n + 4, :].rearrange("(o n) s -> o n s", o=1)
                bc_tok[i] = SP.dma(lane(f"bc{i % 2}"), bcr[i % 2][:, :, :], src.broadcast_to([128, 4, TB]), bcs_tok[ib],
                                   bc_free.get(i - 2))

        def scan_b(ib):
            p = ib % 2
            load_bc(4 * ib)
            load_bc(4 * ib + 1)
            du_tok = {}
            for m in range(4):
                du_tok[m] = tt(POOL, du[:, m, :], dtt[p][:, m, :], u[p][:, m, :], ALU.mult, dt1_tok[ib], u_tok[ib],
                               fb.get("du"))
            held = {}
            acc_tok = fb.get("acc")

            def gather(n):
                nonlocal acc_tok
                hh, h_toks = held.pop(n)
                new = []
                for s in range(4):
                    b, over = hTr.take()
                    for m in range(4):
                        tok = tr(b.buf[:, m * 128:(m + 1) * 128], hh.buf[:, m, s * 128:(s + 1) * 128], ident, over,
                                 h_toks[m], signal=m == 3)
                    c = Ct[p][:, s, 32 + n:33 + n]
                    if n == 0:
                        a = ts(DVE, acc[:, s, :], b.buf[:, :], c, None, ALU.mult, None, tok, ct_tok[ib], acc_tok)
                    else:
                        a = stt(acc[:, s, :], b.buf[:, :], c, acc[:, s, :], ALU.mult, ALU.add, tok, acc_tok[s])
                    b.free = [a]
                    new.append(a)
                    yield
                acc_tok = new
                hh.free = [tok, h_prev[n]]

            for n in range(17):
                if n < 16:
                    i = 4 * ib + n // 4
                    hh, over_h = hr.take()
                    toks = []
                g = gather(n - 1) if n else iter(())
                for m in range(4):
                    if n < 16:
                        dB, over = dBr.take()
                        db_tok = tt(POOL, dB.buf[:, :], du[:, m, :], bcr[i % 2][:, n % 4, :], ALU.mult, du_tok[m],
                                    bc_tok[i], over)
                        dA_, over = dAr.take()
                        q = 16 * m + n
                        da_tok = act(dA_.buf[:, :], dtt[p][:, m, :], ACT.Exp, dt1_tok[ib], A1_tok, over,
                                     scale=A1[:, q:q + 1])
                        s_tok = DVE(lambda e, hh=hh, dA_=dA_, dB=dB, m=m, n=n: e.tensor_tensor_scan(
                            hh.buf[:, m, :], dA_.buf[:, :], dB.buf[:, :], hst[:, n, m:m + 1],
                            ALU.mult, ALU.add), da_tok, db_tok, h_prev[n], over_h,
                            cost=660)
                        dB.free, dA_.free = [s_tok], [s_tok]
                        toks.append(s_tok)
                    next(g, None)
                    yield
                run(g)
                if n < 16:
                    h_prev[n] = [act(hst[:, n, :], hh.buf[:, :, TB - 1], ACT.Identity, toks)]
                    held[n] = (hh, toks)
                    if n % 4 == 3:
                        bc_free[i] = [db_tok]
                        if n < 11:
                            load_bc(i + 2)
            fb["du"] = [db_tok]
            fb[("dt", p)] = [da_tok, du_tok[3]]
            fb[("Ct", p)] = acc_tok
            for m in range(4):
                b, over = hTr.take()
                for s in range(4):
                    tok = tr(b.buf[:, s * 128:(s + 1) * 128], acc[:, s, m * 128:(m + 1) * 128], ident, over, acc_tok[s],
                             signal=s == 3)
                a = stt(u[p][:, m, :], u[p][:, m, :], col("D1", m), b.buf[:, :], ALU.mult, ALU.add, tok, du_tok[m])
                b.free = [a]
                g_tok = tt(DVE, u[p][:, m, :], u[p][:, m, :], sz[p][:, m, :], ALU.mult, a, sz_tok[ib])
                yield
            fb["acc"] = [tok]
            fb[("sz", p)] = [g_tok]
            gate_tok[ib] = g_tok

        y_tok, gate_tok = {}, {}
        out_toks = []
        x3_free = [over_a]
        xs_tok, xn3_tok = {}, {}
        sum_toks = []

        def post_b(ib):
            nonlocal x3_free
            p = ib % 2
            blk = slice(ib * TB, (ib + 1) * TB)
            x_tok = SP.dma(lane("x3"), x3[:, :, :], t["x2"][:, :, blk], x2_tok[ib], x3_free)
            for m in range(2):
                b, over = takeb()
                for k in range(4):
                    tok = mm(b.buf[:, :], wo1[:, k, m * 128:(m + 1) * 128], u[p][:, k, :], k == 0, k == 3, over,
                             gate_tok[ib], wo1_tok, signal=k == 3)
                x_tok = tt(DVE, x3[:, m, :], x3[:, m, :], b.buf[:, :], ALU.add, tok, x_tok)
                b.free = [x_tok]
                yield
            fb[("u", p)] = [tok]
            xs_tok[ib] = SP.dma(lane(f"x3s{ib}"), t["x3"][:, :, blk], x3[:, :, :], x_tok)
            yield from layer_norm(takeb, x3, x3, sq1, r1, [x_tok], [xs_tok[ib]])
            xn = done[0]
            sum_toks.append(DVE(lambda e: e.tensor_reduce(sums[:, :, ib], x3[:, :, :], AX.X, ALU.add), xn))
            xn3_tok[ib] = SP.dma(lane(f"xn3{ib}"), t["xn3"][:, :, blk], x3[:, :, :], xn)
            x3_free = [xn3_tok[ib], sum_toks[-1]]
            yield

        def chain(*gens):
            for g in gens:
                yield from g

        evac_b(0)
        weave((pre_b(0), PE, EB), (product_b(1), PE, 0.0))
        for ib in range(NB):
            parts = [(scan_b(ib), DVE, ES)]
            sides = []
            if ib >= 1:
                sides.append(post_b(ib - 1))
            if ib + 1 < NB:
                evac_b(ib + 1)
                sides.append(pre_b(ib + 1))
            parts.append((chain(*sides), PE, EB))
            if ib + 2 < NB:
                parts.append((product_b(ib + 2), PE, 0.0))
            weave(*parts)
        run(post_b(NB - 1))
        over_b = barrier()
        cB.close()

        cC = ExitStack()
        mean = sb(cC, "mean", [128, 2])
        Wr = sb(cC, "Wr", [128, 2, 8])
        br = sb(cC, "br", [1, 8])
        q = sb(cC, "q", [1, 16, 8])
        idx = sb(cC, "idx", [1, 8], U32)
        tw = sb(cC, "tw", [128, 2])
        W1 = sb(cC, "W1", [128, 2, 2, 512])
        W2 = sb(cC, "W2", [128, 2, 4, D])
        b1 = sb(cC, "b1", [128, 2, 4])
        b2 = sb(cC, "b2", [128, 2, 2])
        b2c = sb(cC, "b2c", [128, 2])
        xn = [sb(cC, f"xn{i}", [128, 2, TB]) for i in range(3)]
        xr = [sb(cC, f"xr{i}", [128, 2, TB]) for i in range(3)]
        G = [sb(cC, f"G{i}", [128, 8, TB]) for i in range(2)]
        o = [sb(cC, f"o{i}", [128, 2, TB]) for i in range(2)]
        sq2 = [sb(cC, f"sq2{i}", [128, 2, TB]) for i in range(2)]
        r2 = [sb(cC, f"r2{i}", [128, TB]) for i in range(2)]

        ring_c = Ring(P)
        takec = ring_c.take

        wr_tok = SP.dma(lane("Wr"), Wr[:, :, :], t["Wr"], over_b)
        br_tok = SP.dma(lane("br"), br[:, :], t["br"], over_b)
        xn_tok, xr_tok, c_free = {}, {}, {}

        def load_c(ib):
            if ib < NB:
                blk = slice(ib * TB, (ib + 1) * TB)
                xn_tok[ib] = SP.dma(lane(f"cxn{ib % 3}"), xn[ib % 3][:, :, :], t["xn3"][:, :, blk], over_b,
                                    xn3_tok[ib], c_free.get(ib - 3))
                xr_tok[ib] = SP.dma(lane(f"cxr{ib % 3}"), xr[ib % 3][:, :, :], t["x3"][:, :, blk], over_b,
                                    xs_tok[ib], c_free.get(ib - 3))

        for ib in range(3):
            load_c(ib)
        a = DVE(lambda e: e.tensor_reduce(mean[:, :], sums[:, :, :], AX.X, ALU.add), over_b, sum_toks)
        b, over = takec()
        for k in range(2):
            tok = mm(b.buf[0:1, 0:8], mean[:, k:k + 1], Wr[:, k, :], k == 0, k == 1, over_b, a, wr_tok, signal=k == 1)
        row = [q[:, i, :] for i in range(16)]

        def softmax_row(x, y, a):
            mx, s, rs = row[13][:, 0:1], row[14][:, 0:1], row[15][:, 0:1]
            a = DVE(lambda e: e.tensor_reduce(mx, x, AX.X, ALU.max), a)
            a = ts(DVE, y, x, mx, None, ALU.subtract, None, a)
            a = act(y, y, ACT.Exp, a, accum=s)
            a = DVE(lambda e: e.reciprocal(rs, s), a)
            return ts(DVE, y, y, rs, None, ALU.mult, None, a)

        a = stt(row[0], b.buf[0:1, 0:8], 1.0 / N, br[:, :], ALU.mult, ALU.add, tok, br_tok)
        b.free = [a]
        a = softmax_row(row[0], row[1], a)
        cap = float(-(-N * 5 // 4 // 8))
        a = ts(DVE, row[2], row[1], float(N), 1e-30, ALU.mult, ALU.max, a)
        a = DVE(lambda e: e.reciprocal(row[3], row[2]), a)
        a = ts(DVE, row[3], row[3], cap, 1.0, ALU.mult, ALU.min, a)
        a = tt(DVE, row[4], row[1], row[3], ALU.mult, a)
        a = softmax_row(row[4], row[5], a)
        a = DVE(lambda e: e.max(row[6], row[5]), a)
        idx_tok = DVE(lambda e: e.max_index(idx[:, :], row[6], row[5]), a)
        a = ts(DVE, row[7][:, 0:2], row[6][:, 0:2], row[6][:, 0:1], None, ALU.subtract, None, idx_tok)
        a = act(row[8][:, 0:2], row[7][:, 0:2], ACT.Exp, a, accum=row[9][:, 0:1])
        a = DVE(lambda e: e.reciprocal(row[10][:, 0:1], row[9][:, 0:1]), a)
        a = ts(DVE, row[11][:, 0:2], row[8][:, 0:2], row[10][:, 0:1], None, ALU.mult, None, a)
        b, over = takec()
        tok = mm(b.buf[:, 0:2], one[0:1, :], row[11][:, 0:2], True, True, over, a, signal=True)
        tw_tok = DVE(lambda e: e.tensor_copy(tw[:, :], b.buf[:, 0:2]), tok)
        b.free = [tw_tok]

        e_tok = []
        for k in range(2):
            got = {}

            def first(e, k=k, got=got):
                v = e.value_load(idx[0:1, k:k + 1], min_val=0, max_val=7)
                got["v"] = v
                return e.dma_start(W1[:, k, :, :], t["W1"][bass.ds(v, 1)].rearrange("o p k f -> p (o k) f"))

            ln = lane(f"e1{k}")
            ln.count += 16
            SP.ops.append(([idx_tok], first, ln.sem, 16))
            e_tok.append((ln.sem, ln.count))
            for name, dst, pat in (("b1", b1[:, k, :], "o p m -> p (o m)"), ("W2", W2[:, k, :, :], "o p k f -> p (o k) f"),
                                   ("b2", b2[:, k, :], "o p m -> p (o m)")):
                ln = lane(f"{name}{k}")
                ln.count += 16
                SP.ops.append(([], lambda e, name=name, dst=dst, pat=pat, got=got: e.dma_start(
                    dst, t[name][bass.ds(got["v"], 1)].rearrange(pat)), ln.sem, 16))
                e_tok.append((ln.sem, ln.count))
        ew = []
        for k in range(2):
            ew.append(ts(DVE, W2[:, k, :, :], W2[:, k, :, :], tw[:, k:k + 1], None, ALU.mult, None, tw_tok, e_tok))
        a = ts(DVE, b2[:, 0, :], b2[:, 0, :], tw[:, 0:1], None, ALU.mult, None, tw_tok, e_tok)
        b2_tok = stt(b2c[:, :], b2[:, 1, :], tw[:, 1:2], b2[:, 0, :], ALU.mult, ALU.add, a)

        def experts(ib):
            x, res, g, oo = xn[ib % 3], xr[ib % 3], G[ib % 2], o[ib % 2]
            gt = []
            for e in range(2):
                for f in range(4):
                    b, over = takec()
                    for k in range(2):
                        tok = mm(b.buf[:, :], W1[:, e, k, f * 128:(f + 1) * 128], x[:, k, :], k == 0, k == 1, over,
                                 xn_tok[ib], e_tok, signal=k == 1)
                    a = act(g[:, 4 * e + f, :], b.buf[:, :], ACT.Gelu, tok, c_free.get(("G", ib - 2)),
                            bias=b1[:, e, f:f + 1])
                    b.free = [a]
                    gt.append(a)
            yield
            for d in range(2):
                b, over = takec()
                for i in range(8):
                    tok = mm(b.buf[:, :], W2[:, i // 4, i % 4, d * 128:(d + 1) * 128], g[:, i, :], i == 0, i == 7, over,
                             gt[i], ew, signal=i == 7)
                a = stt(oo[:, d, :], b.buf[:, :], b2c[:, d:d + 1], x[:, d, :], ALU.add, ALU.add, tok, b2_tok,
                        c_free.get(("o", ib - 2)))
                b.free = [a]
            c_free[("G", ib)] = tok
            yield
            yield from layer_norm(takec, oo, oo, sq2[ib % 2], r2[ib % 2], a, c_free.get(("o", ib - 2)))
            a = done[0]
            for k in range(2):
                a = ts(DVE, oo[:, k, :], oo[:, k, :], col("gamma", k), col("beta", k), ALU.mult, ALU.add, a)
            a = tt(DVE, oo[:, :, :], oo[:, :, :], res[:, :, :], ALU.add, a, xr_tok[ib])
            c_free[ib] = [a]
            c_free[("o", ib)] = SP.dma(lane(f"out{ib % 2}"), t["out"][:, :, ib * TB:(ib + 1) * TB], oo[:, :, :], a)
            load_c(ib + 3)

        prev = None
        for ib in range(NB):
            gen = experts(ib)
            next(gen)
            if prev is not None:
                run(prev)
            next(gen)
            prev = gen
        run(prev)
        ends = [c_free[("o", NB - 1)], c_free[("o", NB - 2)]]
        cC.close()

        block = ctx.enter_context(nc.Block())

        @block.sync
        def _(e):
            SP.play(e)
            for s, v in ends:
                e.wait_ge(s, v)
            for ln in lanes.values():
                e.wait_ge(ln.sem, ln.count)

        @block.tensor
        def _(e):
            PE.play(e)

        @block.vector
        def _(e):
            DVE.play(e)

        @block.scalar
        def _(e):
            SCA.play(e)

        @block.gpsimd
        def _(e):
            POOL.play(e)


def kernel(**inputs):
    import concourse.bacc as bacc
    from concourse.bass_utils import run_bass_kernel_spmd

    a = {k: np.asarray(v) for k, v in inputs.items()}
    f = np.float32

    def tiles(w):
        return w.reshape(-1, 128, w.shape[-1]).transpose(1, 0, 2)

    def cols(v):
        return v.reshape(-1, 128).T

    def pad(v):
        return np.concatenate([v, np.zeros((64,) + v.shape[1:], f)])

    tri = np.triu(np.ones((128, 128), f))
    consts = np.stack([np.eye(128, dtype=f), tri, np.tril(np.ones((128, 128), f), -1), np.full((128, 128), 1 / 256, f),
                       np.ones((128, 128), f)], 1)
    cw, cb = a["L0_ffn_conv_w"], a["L0_ffn_conv_b"]
    cw = np.concatenate([cw[:512], pad(cw[512:576]), pad(cw[576:])])
    cb = np.concatenate([cb[:512], pad(cb[512:576]), pad(cb[576:])])
    parts = {
        "cw0": cw.reshape(6, 128, 4).transpose(1, 0, 2).reshape(128, 24), "cb0": cols(cb),
        "cw1": a["L1_gnn_conv_w"].reshape(4, 128, 4).transpose(1, 0, 2).reshape(128, 16),
        "cb1": cols(a["L1_gnn_conv_b"]), "D0": cols(np.repeat(a["L0_ffn_D"], 64)), "nw": cols(a["L0_ffn_norm_w"]),
        "blin": cols(a["L0_ffn_b_lin"]), "gcnb": cols(a["L1_gnn_gcn_b"]), "lng": cols(a["L1_gnn_ln_g"]),
        "lnb": cols(a["L1_gnn_ln_b"]), "bdt": cols(a["L1_gnn_b_dt"]),
        "A1": a["L1_gnn_A_log"].reshape(4, 128, 16).transpose(1, 0, 2).reshape(128, 64),
        "D1": cols(a["L1_gnn_D_skip"]), "gamma": cols(a["L1_ffn_gamma"]), "beta": cols(a["L1_ffn_beta"]),
    }
    wp = np.zeros((128, 4, 512), f)
    wp[:, 0:2, :] = tiles(np.ascontiguousarray(a["L0_ffn_W_out"].T))
    arrays = {
        "xT": tiles(a["x"].T),
        "adjT": a["adj"].reshape(NB, TB, NJ, 128).transpose(0, 3, 2, 1),
        "consts": consts,
        "cols": np.concatenate([parts[k] for k in COLS], 1),
        "rows": np.concatenate([a["L0_gnn_B"], np.tile(a["L0_ffn_dt_bias"], 4), a["L0_ffn_A_log"]])[None],
        "W0": tiles(a["L0_gnn_W"]), "Win": tiles(a["L0_ffn_W_in"]), "WoutT": wp,
        "Wlin": tiles(a["L0_ffn_W_lin"]), "Wg": tiles(a["L1_gnn_gcn_w"]), "w1": tiles(a["L1_gnn_w_in"]),
        "wxp": tiles(a["L1_gnn_w_xp"]), "wdt": a["L1_gnn_w_dt"], "wo1": tiles(a["L1_gnn_w_out"]),
        "Wr": tiles(a["L1_ffn_Wr"]), "br": a["L1_ffn_br"][None],
        "W1": a["L1_ffn_W1"].reshape(8, 2, 128, 512).transpose(0, 2, 1, 3),
        "W2": a["L1_ffn_W2"].reshape(8, 4, 128, 256).transpose(0, 2, 1, 3),
        "b1": a["L1_ffn_b1"].reshape(8, 4, 128).transpose(0, 2, 1),
        "b2": a["L1_ffn_b2"].reshape(8, 2, 128).transpose(0, 2, 1),
    }
    arrays = {"in_" + k: np.ascontiguousarray(v) for k, v in arrays.items()}
    nc = bacc.Bacc("TRN2", target_bir_lowering=False, num_devices=1)
    t = {k[3:]: nc.dram_tensor(k, v.shape, mybir.dt.from_np(v.dtype), kind="ExternalInput").ap()
         for k, v in arrays.items()}
    for name, shape in (("x2", (128, 2, N)), ("x3", (128, 2, N)), ("xn3", (128, 2, N)), ("m2", (128, NJ, D)), ("bc", (NB, 16, TB))):
        t[name] = nc.dram_tensor("tmp_" + name, shape, F32, kind="Internal").ap()
    t["out"] = nc.dram_tensor("out_0", (128, 2, N), F32, kind="ExternalOutput").ap()
    build(nc, t)
    r = run_bass_kernel_spmd(nc, [arrays], core_ids=[0])
    got = r.results[0]["out_0"]
    return np.ascontiguousarray(got.transpose(2, 1, 0).reshape(N, D))
```

```python
import numpy as np
import concourse.bass as bass
from concourse import mybir
from contextlib import ExitStack

F32 = mybir.dt.float32
F32R = mybir.dt.float32r
U32 = mybir.dt.uint32
ALU = mybir.AluOpType
ACT = mybir.ActivationFunctionType
AX = mybir.AxisListType

N, D, TB = 4096, 256, 512
NB = N // TB
NJ = N // 128
NW = 5
SIDE, PRE, AHEAD, BAND = 0.95, 56, 500.0, 0.2
LAG = 5
EA, EB, ES = 3000.0, 0.0, 2000.0
EPS = 1e-5
TINY = 1e-18
LNEXP = "natural_log_exp_and_others"
TANH = "exp_and_others"
GELU = "gelu_and_others"

COLS = {}
_at = 0
for _name, _n in (("cw0", 24), ("cb0", 6), ("cw1", 16), ("cb1", 4), ("D0", 4), ("nw", 4), ("blin", 2), ("gcnb", 2),
                  ("lng", 2), ("lnb", 2), ("bdt", 4), ("A1", 64), ("D1", 4), ("gamma", 2), ("beta", 2)):
    COLS[_name] = (_at, _n)
    _at += _n
NCOL = _at
HALVED = COLS["D0"][0]
NROW = 256 + 32 + 8


class Line:

    def __init__(self, sem, times):
        self.sem, self.count, self.ops, self.times, self.clock, self.last = sem, 0, [], times, 0.0, 0.0

    def guess(self, after, cost, mark, late=0.0):
        start = max([self.clock] + [self.times.get((id(s), v), 0.0) for s, v in after])
        self.clock = start + cost
        self.times["now"] = max(self.times.get("now", 0.0), self.clock + late)
        if mark is not None:
            self.times[(id(mark[0]), mark[1])] = self.clock + late

    def __call__(self, fn, *after, signal=True, cost=200.0):
        after = list(flat(after))
        self.ops.append((after, fn, self.sem if signal else None, 1))
        self.count += signal
        mark = (self.sem, self.count) if signal else None
        self.guess(after, cost, mark)
        return mark

    def dma(self, lane, out, in_, *after, **kw):
        lane.count += 16
        after = list(flat(after))
        self.ops.append((after, lambda e: e.dma_start(out, in_, **kw), lane.sem, 16))
        self.guess(after, 60.0, (lane.sem, lane.count), 2500.0 + size(out) / 1.5)
        return (lane.sem, lane.count)

    def play(self, engine):
        seen = {}
        for after, fn, sem, step in self.ops:
            for s, value in after:
                if seen.get(id(s), 0) < value:
                    seen[id(s)] = value
                    engine.wait_ge(s, value)
            ins = fn(engine)
            if sem is not None:
                ins.then_inc(sem, step)


def tuple_of(tok):
    return None if tok is None else (id(tok[0]), tok[1])


def size(ap):
    n = 1
    for d in list(ap.shape)[1:]:
        n *= d
    return n


def weave(*parts):
    live = [[0.0, line, ease, g] for g, line, ease in parts]
    while live:
        part = min(live, key=lambda p: max(p[0], p[1].clock) - p[2])
        times = part[1].times
        times["now"] = 0.0
        got = next(part[3], "end")
        if isinstance(got, str):
            live.remove(part)
        else:
            part[0] = times["now"] if got is None else got


def pace(pe, dve, *parts, fill=None):
    live = [[g, 0, n, share] for g, n, share in parts]
    filled = 0
    while live:
        part = min(live, key=lambda p: p[1] * p[3] / p[2])
        if fill and (pe.clock < dve.clock - AHEAD or filled / 65 < part[1] * part[3] / part[2] - BAND):
            filled += 1
            if isinstance(next(fill, "end"), str):
                fill = None
            continue
        part[1] += 1
        if isinstance(next(part[0], "end"), str):
            live.remove(part)
    if fill:
        run(fill)


def run(gen):
    for _ in gen:
        pass


def steps(gen, n):
    for _ in range(n):
        got = next(gen, "end")
        if isinstance(got, str):
            return
        yield got


class Lane:

    def __init__(self, sem):
        self.sem, self.count = sem, 0


def flat(after):
    for a in after:
        if a is None:
            continue
        if isinstance(a, list):
            yield from flat(a)
        else:
            yield a


class Slot:

    def __init__(self, buf):
        self.buf, self.free = buf, []


class Ring:
    def __init__(self, bufs):
        self.slots, self.at = [Slot(b) for b in bufs], 0

    def take(self):
        s = self.slots[self.at % len(self.slots)]
        self.at += 1
        assert s.free is not None, "the slot has no reader yet"
        over, s.free = s.free, None
        return s, over


def build(nc, t):
    with ExitStack() as ctx:
        def sem(name):
            return ctx.enter_context(nc.semaphore(name))

        def sb(c, name, shape, dt=F32):
            return c.enter_context(nc.sbuf_tensor(name, shape, dt))

        times = {}
        PE, DVE, SCA, POOL, SP = (Line(sem(n), times) for n in ("s_pe", "s_dve", "s_act", "s_pool", "s_sp"))
        lanes = {}

        def lane(name):
            if name not in lanes:
                lanes[name] = Lane(sem("d_" + name))
            return lanes[name]

        def mm(out, lhsT, rhs, start, stop, *after, signal=False, skip=False):
            return PE(lambda e: e.matmul(out, lhsT, rhs, start=start, stop=stop, skip_group_check=skip),
                      *after, signal=signal, cost=max(64, size(out)) * 1.667 + 4)

        def tr(out, in_, ident, *after, signal=False):
            return PE(lambda e: e.transpose(out, in_, ident), *after, signal=signal, cost=109)

        table = [None]

        def act(out, in_, func, *after, scale=1.0, bias=0.0, accum=None):
            need = {ACT.Ln: LNEXP, ACT.Exp: LNEXP, ACT.Tanh: TANH, ACT.Gelu: GELU}.get(func)
            if need is not None and table[0] != need:
                table[0] = need
                SCA(lambda e: e.preload_act_table_set(need), signal=False, cost=1283)
            if accum is None:
                return SCA(lambda e: e.activation(out, in_, func, bias=bias, scale=scale), *after,
                           cost=size(out) / 1.2 + 120)
            return SCA(lambda e: e.activation(out, in_, func, bias=bias, scale=scale, accum_out=accum), *after,
                       cost=size(out) / 1.2 + 250)

        def split(x, hi, lo, *after, by=None):
            if by is None:
                a = DVE(lambda e: e.tensor_copy(hi, x), *after, cost=size(hi) * 0.6 + 130)
            else:
                a = act(hi, x, ACT.Identity, *after)
            return tt(DVE, lo, x, hi.bitcast(F32), ALU.subtract, a, *after)

        def mm3(out, w, x, start, stop, *after, signal=False):
            (wh, wl), (xh, xl) = w, x
            for i, (a, b) in enumerate(((wl, xh), (wh, xh), (wh, xl))):
                tok = PE(lambda e, a=a, b=b, i=i: e.matmul(out, a, b, start=start and i == 0, stop=stop and i == 2),
                         *after, signal=signal and i == 2, cost=size(out) / 2.4 + 3)
            return tok

        def tt(line, out, a, b, op, *after):
            return line(lambda e: e.tensor_tensor(out, a, b, op), *after,
                        cost=size(out) * (2.2 if line is POOL else 1.04) + 130)

        def ts(line, out, a, s1, s2, op0, op1, *after):
            if op1 is None:
                return line(lambda e: e.tensor_scalar(out, a, s1, None, op0), *after, cost=size(out) * 0.6 + 130)
            return line(lambda e: e.tensor_scalar(out, a, s1, s2, op0, op1), *after, cost=size(out) * 0.6 + 130)

        def stt(out, a, s, b, op0, op1, *after):
            return DVE(lambda e: e.scalar_tensor_tensor(out, a, s, b, op0, op1), *after, cost=size(out) * 1.04 + 130)

        def barrier():
            now = [(l.sem, l.count) for l in (PE, DVE, SCA, POOL) if l.count]
            now += [(l.sem, l.count) for l in lanes.values() if not l.sem in raw_sems]
            return now

        P = [ctx.enter_context(nc.psum_tensor(f"ps{i}", [128, 512], F32)) for i in range(8)]
        consts = sb(ctx, "consts", [128, 5, 128])
        ident, tri, trig, avg, one = (consts[:, i, :] for i in range(5))
        cols = sb(ctx, "cols", [128, NCOL])
        raw = [sb(ctx, f"raw{i}", [128, 2, TB]) for i in range(4)]
        msg = sb(ctx, "msg", [128, NJ, D])

        def col(name, i=0, n=1):
            a = COLS[name][0] + i
            return cols[:, a:a + n]

        c_tok = SP.dma(lane("consts"), consts[:, :, :], t["consts"])
        k_tok = SP.dma(lane("cols"), cols[:, :], t["cols"])
        k_tok = ts(DVE, cols[:, 0:HALVED], cols[:, 0:HALVED], 0.5, None, ALU.mult, None, k_tok)

        NCH = NB * NJ // 2
        raw_tok = {}
        raw_lanes = [lane(f"raw{i}") for i in range(4)]
        raw_sems = [l.sem for l in raw_lanes]

        def load_raw(g, *after):
            if g >= 2 * NCH:
                return
            ib, q = divmod(g % NCH, NJ // 2)
            raw_tok[g] = SP.dma(raw_lanes[g % 4], raw[g % 4][:, :, :], t["adjT"][ib, :, 2 * q:2 * q + 2, :], *after)


        def layer_norm(take, x, xc, sq, r, x_tok, free):
            m, over = take()
            for k in range(2):
                tok = mm(m.buf[:, :], avg, x[:, k, :], k == 0, k == 1, over, x_tok, c_tok, signal=k == 1)
            sub = tt(DVE, xc[:, :, :], x[:, :, :], m.buf[:, None, :].broadcast_to([128, 2, TB]), ALU.subtract, tok, free)
            m.free = [sub]
            yield
            s = act(sq[:, :, :], xc[:, :, :], ACT.Square, sub, free)
            yield
            v, over = take()
            for k in range(2):
                tok = mm(v.buf[:, :], avg, sq[:, k, :], k == 0, k == 1, over, s, signal=k == 1)
            yield
            l = act(r[:, :], v.buf[:, :], ACT.Ln, tok, free, bias=EPS)
            v.free = [l]
            l = act(r[:, :], r[:, :], ACT.Exp, l, scale=-0.5)
            yield
            done[0] = tt(DVE, xc[:, :, :], xc[:, :, :], r[:, None, :].broadcast_to([128, 2, TB]), ALU.mult, l)

        done = [None]

        cA = ExitStack()
        wgt = [sb(cA, f"wgt{i}", [128, 2, TB]) for i in range(NW)]
        W0 = sb(cA, "W0", [128, 2, D])
        Win = sb(cA, "Win", [128, 2, 1160])
        Wc = sb(cA, "Wc", [128, 4, D])
        rows = sb(cA, "rows", [128, NROW])
        Bbc, dtb, Abc = rows[:, 0:256], rows[:, 256:288], rows[:, 288:296]
        diagD = sb(cA, "diagD", [128, 4, 128])
        xbs = [sb(cA, f"xb{i}", [128, 2, TB]) for i in range(2)]
        xb = xbs[0]
        xc = sb(cA, "xc", [128, 2, TB])
        sq = sb(cA, "sq", [128, 2, TB])
        rr = sb(cA, "rr", [128, TB])
        xbc = sb(cA, "xbc", [128, 6, TB + 3])
        ccs = [sb(cA, f"cc{i}", [128, 6, TB]) for i in range(2)]
        cc = ccs[0]
        th = sb(cA, "th", [128, 2, TB])
        zs = [sb(cA, f"z{i}", [128, 4, TB]) for i in range(2)]
        sms = [sb(cA, f"sm{i}", [128, 4, 32]) for i in range(2)]
        ecd = sb(cA, "ecd", [128, 3, 4, 8])
        ms = sb(cA, "ms", [128, 4])
        rms = sb(cA, "rms", [128, 4])
        rdA = sb(cA, "rdA", [128, 8, 128])
        E = [sb(cA, f"E{i}", [128, 8, 128]) for i in range(2)]
        xdt = [sb(cA, f"xdt{i}", [128, 512]) for i in range(2)]
        xdecs = [sb(cA, f"xdec{i}", [128, 512]) for i in range(2)]
        bns = [sb(cA, f"bn{i}", [128, 64]) for i in range(2)]
        cbms = [sb(cA, "cbm", [128, 128])] * 2
        tmp = sb(cA, "tmp", [128, 512])
        Y2 = sb(cA, "Y2", [128, 4, 512])
        YT = sb(cA, "YT", [128, 4, TB])
        h0 = sb(cA, "hs0", [64, 512])
        hd = sb(cA, "hd", [64, 512])

        w0_tok = POOL.dma(lane("W0"), W0[:, :, :], t["W0"])
        rows_tok = POOL.dma(lane("rows"), rows[:, :], t["rows"].broadcast_to([128, NROW]))
        win_tok = POOL.dma(lane("Win"), Win[:, :, :], t["Win"])
        wout_tok = POOL.dma(lane("Wout"), Y2[:, :, :], t["WoutT"])
        wlin_tok = POOL.dma(lane("Wlin"), YT[:, 0:2, 0:256], t["Wlin"])

        early = [SCA.dma(lane("xa"), xb[:, :, :], t["xT"][:, :, 0:TB]),
                 SCA.dma(lane("xb"), cc[:, 0:2, :], t["xT"][:, :, TB:2 * TB])]
        for g in range(4):
            load_raw(g)
        ring = Ring(P[2:8])
        take = ring.take

        a_tok = act(Abc, Abc, ACT.Exp, rows_tok)
        a_tok = ts(DVE, Abc, Abc, -1.0, None, ALU.mult, None, a_tok)
        win_tok = ts(DVE, Win[:, :, 0:512], Win[:, :, 0:512], 0.5, None, ALU.mult, None, win_tok)
        for m in range(4):
            dd_tok = ts(DVE, diagD[:, m, :], ident, col("D0", m), None, ALU.mult, None, c_tok, k_tok)
        woutT = Y2[:, 0:2, :]
        for m in range(4):
            b, over = take()
            for k in range(2):
                tok = mm(b.buf[:, 0:256], woutT[:, k, m * 128:(m + 1) * 128], YT[:, k, 0:256], k == 0, k == 1,
                         over, wout_tok, wlin_tok, signal=k == 1)
            wc_tok = ts(DVE, Wc[:, m, :], b.buf[:, 0:256], col("nw", m), None, ALU.mult, None, tok, k_tok)
            b.free = [wc_tok]
        zero_tok = [POOL(lambda e: e.memset(xbc[:, :, 0:3], 0.0)), POOL(lambda e: e.memset(h0[:, :], 0.0))]

        raw_read = {}
        w_tok = {}
        w_free = {}

        def prep_a(g):
            if g >= NCH:
                return
            two = [(i, wgt[i % NW], raw[i % 4]) for i in (g, g + 1)]
            a = {i: act(w[:, :, :], r[:, :, :], ACT.Ln, raw_tok[i], w_free.get(i - NW), bias=TINY) for i, w, r in two}
            a = {i: act(w[:, :, :], w[:, :, :], ACT.Exp, a[i], scale=-1.0) for i, w, r in two}
            a = {i: stt(w[:, :, :], w[:, :, :], -2.0, w[:, :, :], ALU.add, ALU.mult, a[i]) for i, w, r in two}
            a = {i: act(w[:, :, :], w[:, :, :], ACT.Exp, a[i], scale=-2.0, bias=-2.0) for i, w, r in two}
            for i, w, r in two:
                w_tok[i] = stt(w[:, :, :], r[:, :, :], 1.0, w[:, :, :], ALU.is_lt, ALU.mult, a[i])
                load_raw(i + 4, w_tok[i])

        P_free = [[], []]
        P_tok = [None, None]
        msg1_tok = {}

        def product_a(ib):
            if ib == 0:
                prep_a(0)
            for q in range(NJ // 2):
                g = ib * (NJ // 2) + q
                if g % 2 == 0:
                    prep_a(g + 2)
                for l in range(2):
                    j = 2 * q + l
                    for d in range(2):
                        tok = mm(P[d][:, :], msg[:, j, d * 128:(d + 1) * 128], wgt[g % NW][:, l, :], j == 0, j == NJ - 1,
                                 w_tok[g], msg1_tok[j], P_free[d] if j == 0 else None,
                                 signal=(l == 1 and d == 1) or j == NJ - 1)
                        if j == NJ - 1:
                            P_tok[d] = tok
                    if l == 0:
                        yield 0.0
                w_free[g] = tok
                yield times.get(tuple_of(w_tok.get(g + 1)), 0.0)

        x_free = []

        def messages_0(ib, xb, xc, sq, rr, ln):
            x_tok = early[ib] if ib < 2 else SP.dma(lane("x" + ln), xb[:, :, :], t["xT"][:, :, ib * TB:(ib + 1) * TB],
                                                    bufs.get(ln))
            yield from layer_norm(take, xb, xc, sq, rr, x_tok, bufs.get(ln))
            xn = done[0]
            yield
            last = []
            for s in range(4):
                b, over = take()
                for k in range(2):
                    tok = mm(b.buf[:, 0:256], xc[:, k, s * 128:(s + 1) * 128], W0[:, k, :], k == 0, k == 1,
                             over, xn, w0_tok, signal=k == 1)
                msg1_tok[4 * ib + s] = tt(DVE, msg[:, 4 * ib + s, :], b.buf[:, 0:256], Bbc, ALU.add, tok, rows_tok)
                b.free = [msg1_tok[4 * ib + s]]
                last = [tok]
                yield
            bufs[ln] = last

        bufs = {}
        p = product_a(0)
        second = (ccs[0][:, 0:2, :], cc[:, 2:4, :], cc[:, 4:6, :], th[:, 0, :])
        for pair in range(NB // 2):
            weave((messages_0(2 * pair, xb, xc, sq, rr, "a"), PE, EA), (messages_0(2 * pair + 1, *second, "b"), PE, EA),
                  *([(steps(p, 8), PE, 0.0)] if pair else []))
        run(p)

        h_tok, h_read = zero_tok, []
        x2_tok, msg2_tok = {}, {}
        halo_tok = zero_tok
        free = {("xb", 0): bufs["a"], "xc": bufs["a"], ("cc", 0): bufs["b"], "th": bufs["b"]}
        x1_tok, pre_tok = {}, {}

        def evac_a(ib):
            p = ib % 2
            a = POOL.dma(lane(f"xl{p}"), xbs[p][:, :, :], t["xT"][:, :, ib * TB:(ib + 1) * TB], free.get(("xb", p)))
            for k in range(2):
                a = tt(DVE, xbs[p][:, k, :], xbs[p][:, k, :], P[k][:, :], ALU.add, a, P_tok[k])
                P_free[k] = [a]
            x1_tok[ib] = a

        def pre_a(ib):
            nonlocal halo_tok
            p = ib % 2
            xb, cc, z, sm = xbs[p], ccs[p], zs[p], sms[p]
            yield from layer_norm(take, xb, xc, sq, rr, x1_tok[ib], free["xc"])
            xn = done[0]
            yield
            b, over = take()
            for s in range(4):
                for k in range(2):
                    tok = mm(b.buf[:, 8 * s:8 * s + 8], xc[:, k, s * 128:(s + 1) * 128], Win[:, k, 1152:1160],
                             k == 0, k == 1, over, xn, win_tok, signal=k == 1)
            v, av, dt, dA = sm[:, 0, :], sm[:, 1, :], sm[:, 2, :], sm[:, 3, :]
            a = tt(DVE, v, b.buf[:, 0:32], dtb, ALU.add, tok, rows_tok, free.get(("sm", p)))
            b.free = [a]
            a = act(av, v, ACT.Abs, a)
            a = act(av, av, ACT.Exp, a, scale=-1.0)
            a = act(av, av, ACT.Ln, a, bias=1.0)
            dt_tok = stt(dt, v, 0.0, av, ALU.max, ALU.add, a)
            dA_tok = tt(DVE, dA.rearrange("p (c h) -> p c h", c=4), dt.rearrange("p (c h) -> p c h", c=4),
                        Abc[:, None, :].broadcast_to([128, 4, 8]), ALU.mult, dt_tok, a_tok)
            yield
            cv = []
            for m in range(6):
                w = 128 if m < 4 else 64
                c0 = 512 + 128 * m if m < 4 else 1024 + 64 * (m - 4)
                b, over = take()
                for k in range(2):
                    tok = mm(b.buf[0:w, :], Win[:, k, c0:c0 + w], xc[:, k, :], k == 0, k == 1, over, signal=k == 1)
                a = act(xbc[0:w, m, 3:TB + 3], b.buf[0:w, :], ACT.Identity, tok, halo_tok)
                b.free = [a]
                c = cc[0:w, m, :]
                a = ts(DVE, c, xbc[0:w, m, 0:TB], col("cw0", 4 * m)[0:w, :], col("cb0", m)[0:w, :],
                       ALU.mult, ALU.add, a, k_tok, free.get(("cc", p)))
                for k in range(1, 4):
                    a = stt(c, xbc[0:w, m, k:k + TB], col("cw0", 4 * m + k)[0:w, :], c, ALU.mult, ALU.add, a)
                    if k == 1:
                        yield
                cv.append(a)
                yield
            halo_tok = [POOL(lambda e: e.tensor_copy(xbc[:, 0:4, 0:3], xbc[:, 0:4, TB:TB + 3]), cv),
                        POOL(lambda e: e.tensor_copy(xbc[0:64, 4:6, 0:3], xbc[0:64, 4:6, TB:TB + 3]), cv)]
            for s in range(4):
                b, over = take()
                for k in range(2):
                    tok = mm(b.buf[:, :], xc[:, k, s * 128:(s + 1) * 128], Win[:, k, 0:512], k == 0, k == 1, over,
                             signal=k == 1)
                zt = act(z[:, s, :], b.buf[:, :], ACT.Identity, tok, free.get(("z", p)))
                b.free = [zt]
                if s == 1:
                    yield
            free["xc"] = [tok]
            yield
            sil, ztok = [], []
            tf = free["th"]
            tb = [th, sq]
            for what, w in ((cc[:, 0:2, :], 128), (cc[:, 2:4, :], 128), (cc[0:64, 4:6, :], 64),
                            (z[:, 0:2, :], 128), (z[:, 2:4, :], 128)):
                tz = tb[len(sil) % 2]
                a = act(tz[0:w, :, :], what, ACT.Tanh, cv, zt, tf, sil[-2:-1])
                a = stt(what, tz[0:w, :, :], 1.0, what, ALU.add, ALU.mult, a)
                sil.append(a)
                if len(sil) == 3:
                    yield
            free["th"] = sil[-2:]
            free["xc"] = [tok, sil[-2:]]
            pre_tok[ib] = (sil[2], sil[4], dt_tok, dA_tok)
            yield

        def ssd_a(ib):
            nonlocal h_tok, h_read
            p = ib % 2
            xb, cc, z, sm = xbs[p], ccs[p], zs[p], sms[p]
            dt, dA = sm[:, 2, :], sm[:, 3, :]
            sil_tok, z_tok, dt_tok, dA_tok = pre_tok[ib]
            b, over = take()
            for i, w in enumerate((tri, trig, one)):
                tok = mm(b.buf[:, 32 * i:32 * i + 32], w, dA, True, True, over, dA_tok, signal=i == 2)
            ecd_tok = act(ecd[:, :, :, :].rearrange("p a c h -> p (a c h)"), b.buf[:, 0:96], ACT.Exp, tok, free.get("ecd"))
            b.free = [ecd_tok]
            ms_tok = []
            tmp_free = free.get("tmp")
            rd_free = free.get("rdA")
            made = {}

            def inner(s):
                nonlocal rd_free
                ts_ = slice(s * 128, (s + 1) * 128)
                Es, xd, bn, cbm, xdec = E[s % 2], xdt[s % 2], bns[s % 2], cbms[s % 2], xdecs[s % 2]
                over_s = free.get(("s", s % 2))
                rd = tt(POOL, rdA[:, :, :], tri[:, None, :].broadcast_to([128, 8, 128]),
                        dA[:, 8 * s:8 * s + 8, None].broadcast_to([128, 8, 128]), ALU.mult, dA_tok, rd_free)
                X, over = take()
                for m in range(4):
                    tok = tr(X.buf[:, m * 128:(m + 1) * 128], cc[:, m, ts_], ident, over, sil_tok, signal=m == 3)
                xd_tok = tt(DVE, xd[:, :].rearrange("p (h q) -> p h q", h=8), X.buf[:, :].rearrange("p (h q) -> p h q", h=8),
                            dt[:, 8 * s:8 * s + 8, None].broadcast_to([128, 8, 64]), ALU.mult, tok, dt_tok, over_s)
                X.free = [xd_tok]
                xdec_tok = tt(POOL, xdec[:, :].rearrange("p (h q) -> p h q", h=8),
                              xd[:, :].rearrange("p (h q) -> p h q", h=8),
                              ecd[:, 1, s, :, None].broadcast_to([128, 8, 64]), ALU.mult, xd_tok, ecd_tok, over_s)
                b, over = take()
                tr(b.buf[:, 0:64], cc[0:64, 4, ts_], ident[0:64, 0:64], over)
                tok = mm(b.buf[:, 128:256], cc[0:64, 4, ts_], cc[0:64, 5, ts_], True, True, signal=True)
                bn_tok = DVE(lambda e, b=b: e.tensor_copy(bn[:, :], b.buf[:, 0:64]), tok, over_s)
                cb_tok = tt(DVE, cbm[:, :], b.buf[:, 128:256], tri, ALU.mult, bn_tok, free.get("cbm"))
                b.free = [cb_tok]
                yield
                seg = []
                for i in range(2):
                    b, over = take()
                    rd_free = mm(b.buf[:, :], trig, rdA[:, 4 * i:4 * i + 4, :].rearrange("p h l -> p (h l)"), True, True,
                                 over, rd, signal=True)
                    a = act(Es[:, 4 * i:4 * i + 4, :].rearrange("p h l -> p (h l)"), b.buf[:, :], ACT.Exp, rd_free, over_s)
                    b.free = [a]
                    seg.append(a)
                M_tok = tt(POOL, Es[:, :, :], Es[:, :, :], cbm[:, None, :].broadcast_to([128, 8, 128]), ALU.mult, seg, cb_tok)
                free["cbm"] = [M_tok]
                made[s] = (bn_tok, xd_tok, xdec_tok, M_tok)

            yield from inner(0)
            yield
            for s in range(4):
                ts_ = slice(s * 128, (s + 1) * 128)
                Es, xd, bn, xdec = E[s % 2], xdt[s % 2], bns[s % 2], xdecs[s % 2]
                if s < 3:
                    yield from inner(s + 1)
                    yield
                bn_tok, xd_tok, xdec_tok, M_tok = made[s]
                hd_tok = tt(POOL, hd[:, :].rearrange("p (h q) -> p h q", h=8),
                            h0[:, :].rearrange("p (h q) -> p h q", h=8),
                            ecd[0:64, 2, s, :, None].broadcast_to([64, 8, 64]), ALU.mult, h_tok, ecd_tok)
                Yo, over = take()
                off = mm(Yo.buf[:, :], cc[0:64, 5, ts_], h0[:, :], True, True, over, h_tok, signal=True)
                S, over = take()
                st = mm(S.buf[0:64, :], bn[:, :], xdec[:, :], True, True, over, bn_tok, xdec_tok, signal=True)
                Y, over = take()
                for m in range(4):
                    mm(Y.buf[:, m * 128:(m + 1) * 128], cc[:, m, ts_], diagD[:, m, :], m == 0, False, over, dd_tok,
                       skip=True)
                for h in range(8):
                    dia = mm(Y.buf[:, h * 64:(h + 1) * 64], Es[:, h, :], xd[:, h * 64:(h + 1) * 64], False, h == 7,
                             M_tok, xd_tok, signal=h == 7, skip=True)
                free[("s", s % 2)] = [dia, st, xdec_tok]
                h_tok = tt(DVE, h0[:, :], hd[:, :], S.buf[0:64, :], ALU.add, st, hd_tok, off)
                S.free = [h_tok]
                a = tt(DVE, tmp[:, :].rearrange("p (h q) -> p h q", h=8), Yo.buf[:, :].rearrange("p (h q) -> p h q", h=8),
                       ecd[:, 0, s, :, None].broadcast_to([128, 8, 64]), ALU.mult, off, ecd_tok, tmp_free)
                Yo.free = [a]
                a = tt(DVE, tmp[:, :], tmp[:, :], Y.buf[:, :], ALU.add, a, dia)
                Y.free = [a]
                a = tt(DVE, Y2[:, s, :], tmp[:, :], z[:, s, :], ALU.mult, a, z_tok, free.get("Y2"), wc_tok)
                a = act(tmp[:, :], Y2[:, s, :], ACT.Square, a, accum=ms[:, s:s + 1])
                tmp_free = [a]
                ms_tok.append(a)
                yield
            free[("cc", p)], free[("z", p)], free["rdA"] = [dia, off], [a], rd_free
            free["ecd"] = [st, h_tok, a, xdec_tok]
            free[("sm", p)] = [rd_free, h_tok]
            a = act(rms[:, :], ms[:, :], ACT.Ln, ms_tok, scale=1.0 / 512, bias=EPS)
            rms_tok = act(rms[:, :], rms[:, :], ACT.Exp, a, scale=-0.5)
            for s in range(4):
                y3 = ts(DVE, Y2[:, s, :], Y2[:, s, :], rms[:, s:s + 1], None, ALU.mult, None, rms_tok)
                b, over = take()
                for m in range(4):
                    tok = tr(b.buf[:, m * 128:(m + 1) * 128], Y2[:, s, m * 128:(m + 1) * 128], ident, over, y3,
                             signal=m == 3)
                yt = act(YT[:, :, s * 128:(s + 1) * 128], b.buf[:, :].rearrange("p (m l) -> p m l", m=4), ACT.Identity,
                         tok, free.get("YT"))
                b.free = [yt]
                if s % 2:
                    yield
            free["Y2"] = tok
            for m in range(2):
                b, over = take()
                for k in range(4):
                    tok = mm(b.buf[:, :], Wc[:, k, m * 128:(m + 1) * 128], YT[:, k, :], k == 0, k == 3, over, yt, wc_tok,
                             signal=k == 3)
                x2 = stt(xb[:, m, :], b.buf[:, :], col("blin", m), xb[:, m, :], ALU.add, ALU.add, tok)
                b.free = [x2]
                yield
            free["YT"] = tok
            x2_tok[ib] = POOL.dma(lane(f"x2_{ib}"), t["x2"][:, :, ib * TB:(ib + 1) * TB], xb[:, :, :], x2)
            yield
            yield from layer_norm(take, xb, Y2[:, 0:2, :], Y2[:, 2:4, :], tmp, x2, [free["Y2"], tmp_free])
            xn = done[0]
            free[("xb", p)] = [xn, x2_tok[ib]]
            free["tmp"] = [xn]
            yield
            a = None
            for s in range(4):
                b, over = take()
                for k in range(2):
                    tok = mm(b.buf[:, 0:256], Y2[:, k, s * 128:(s + 1) * 128], Wg[:, k, :], k == 0, k == 1,
                             over, xn, wg_tok, signal=k == 1)
                if ib < NB - 2:
                    a = act(YT[:, s // 2, s % 2 * 256:s % 2 * 256 + 256], b.buf[:, 0:256], ACT.Identity, tok, free["YT"])
                else:
                    a = msg2_tok[4 * ib + s] = act(msg[:, 4 * ib + s, :], b.buf[:, 0:256], ACT.Identity, tok, last_a[0])
                b.free = [a]
            free["Y2"] = [tok]
            if ib < NB - 2:
                m2_tok[ib] = POOL.dma(lane(f"m2_{ib}"), t["m2"][:, 4 * ib:4 * ib + 4, :].rearrange("p a d -> p (a d)"),
                                    YT[:, 0:2, :].rearrange("p a d -> p (a d)"), a)
                free["YT"] = [m2_tok[ib]]
            yield

        Wg = W0
        wg_tok = SP.dma(lane("Wg"), W0[:, :, :], t["Wg"], bufs["a"], bufs["b"])

        raw_free = {}

        def product_b(ib):
            for q in range(NJ // 2):
                g = NCH + ib * (NJ // 2) + q
                for l in range(2):
                    j = 2 * q + l
                    for d in range(2):
                        tok = mm(P[d][:, :], msg[:, j, d * 128:(d + 1) * 128], raw[g % 4][:, l, :], j == 0, j == NJ - 1,
                                 raw_tok[g], msg2_tok[j], P_free[d] if j == 0 else None,
                                 signal=(l == 1 and d == 1) or j == NJ - 1)
                        if j == NJ - 1:
                            P_tok[d] = tok
                        if l + d < 2:
                            yield 0.0
                load_raw(g + 4, tok)
                yield times.get(tuple_of(raw_tok.get(g + 1)), 0.0)

        m2_tok, last_a = {}, [None]
        evac_a(0)
        p1 = product_a(1)
        weave((pre_a(0), PE, EA), (p1, PE, 0.0))
        for ib in range(NB):
            parts = [(ssd_a(ib), PE, EA)]
            if ib + 1 < NB:
                evac_a(ib + 1)
                parts.append((pre_a(ib + 1), PE, EA))
            if ib + 2 < NB:
                parts.append((product_a(ib + 2), PE, 0.0))
            elif ib + 2 == NB:
                last_a[0] = list(P_tok)
                for b in range(NB - 2):
                    tok = SP.dma(lane(f"m2l{b}"), msg[:, 4 * b:4 * b + 4, :], t["m2"][:, 4 * b:4 * b + 4, :],
                                 m2_tok[b], P_tok)
                    for s in range(4):
                        msg2_tok[4 * b + s] = tok
                pb = product_b(0)
                parts.append((steps(pb, 24), PE, 0.0))
            else:
                parts.append((steps(pb, 32), PE, 0.0))
            weave(*parts)
        run(pb)
        over_a = barrier()
        cA.close()

        cB = ExitStack()
        w1 = sb(cB, "w1", [128, 2, 1024])
        wxp = sb(cB, "wxp", [128, 4, 48])
        wdt = sb(cB, "wdt", [16, 512])
        wo1 = sb(cB, "wo1", [128, 4, D])
        sums = sb(cB, "sums", [128, 2, NB])
        u = [sb(cB, f"u{i}", [128, 4, TB]) for i in range(2)]
        sz = [sb(cB, f"sz{i}", [128, 4, TB]) for i in range(2)]
        dtt = [sb(cB, f"dt{i}", [128, 4, TB]) for i in range(2)]
        du = sb(cB, "du", [128, 4, TB])
        bcr = [sb(cB, f"bc{i}", [128, 2, TB]) for i in range(3)]
        dBr = Ring([sb(cB, f"dB{i}", [128, TB]) for i in range(4)])
        hr = Ring([sb(cB, f"h{i}", [128, 4, TB]) for i in range(3)])
        acc = sb(cB, "acc", [128, 4, TB])
        Ct = [sb(cB, f"Ct{i}", [128, 4, 48]) for i in range(2)]
        hst = sb(cB, "hst", [128, 16, 4])
        xcb = sb(cB, "xcb", [128, 4, TB + 3])
        hb = sb(cB, "hb", [128, 2, TB])
        sq1 = sb(cB, "sq1", [128, 2, TB])
        x3 = sb(cB, "x3", [128, 2, TB])
        r1 = sb(cB, "r1", [128, TB])
        th1 = sb(cB, "th1", [128, 2, TB])
        dbc = sb(cB, "dbc", [48, TB])

        ring_b, dAr, hTr = Ring(P[2:4]), Ring(P[4:6]), Ring(P[6:8])
        for s, o in zip(ring_b.slots + dAr.slots + hTr.slots, ring.slots):
            s.free = o.free
        takeb = ring_b.take

        w_tok1 = SP.dma(lane("w1"), w1[:, :, :], t["w1"], over_a)
        wxp_tok = SP.dma(lane("wxp"), wxp[:, :, :], t["wxp"], over_a)
        wdt_tok = SP.dma(lane("wdt"), wdt[:, :], t["wdt"], over_a)
        wo1_tok = SP.dma(lane("wo1"), wo1[:, :, :], t["wo1"], over_a)
        w_tok1 = ts(DVE, w1[:, :, 512:1024], w1[:, :, 512:1024], 0.5, None, ALU.mult, None, w_tok1, over_a)
        A1 = cols[:, COLS["A1"][0]:COLS["A1"][0] + 64]
        a = act(A1, A1, ACT.Exp, k_tok)
        A1_tok = ts(DVE, A1, A1, -1.0, None, ALU.mult, None, a)
        halo1 = [POOL(lambda e: e.memset(xcb[:, :, 0:3], 0.0), over_a)]
        hst_tok = [POOL(lambda e: e.memset(hst[:, :, :], 0.0), over_a)]
        SCA(lambda e: e.activation(th1[:, 0, 0:1], cols[:, 0:1], ACT.Identity), over_a)
        fb = {}
        u_tok, sz_tok, dt1_tok, bcs_tok = {}, {}, {}, {}
        h_prev = {n: hst_tok for n in range(16)}

        hb_tok = {}

        def evac_b(ib):
            for k in range(2):
                hb_tok[ib] = act(hb[:, k, :], P[k][:, :], ACT.Relu, P_tok[k], fb.get("hb"), k_tok,
                                 bias=col("gcnb", k))
                P_free[k] = [hb_tok[ib]]

        def ln_b(x, sq, r, x_tok, free):
            m, over = takeb()
            for k in range(2):
                tok = mm(m.buf[:, :], avg, x[:, k, :], k == 0, k == 1, over, x_tok, c_tok, signal=k == 1)
                yield
            sub = tt(DVE, x[:, :, :], x[:, :, :], m.buf[:, None, :].broadcast_to([128, 2, TB]), ALU.subtract, tok, free)
            m.free = [sub]
            yield
            s = act(sq[:, :, :], x[:, :, :], ACT.Square, sub, free)
            yield
            v, over = takeb()
            for k in range(2):
                tok = mm(v.buf[:, :], avg, sq[:, k, :], k == 0, k == 1, over, s, signal=k == 1)
                yield
            l = act(r[:, :], v.buf[:, :], ACT.Ln, tok, free, bias=EPS)
            v.free = [l]
            l = act(r[:, :], r[:, :], ACT.Exp, l, scale=-0.5)
            yield
            done[0] = tt(DVE, x[:, :, :], x[:, :, :], r[:, None, :].broadcast_to([128, 2, TB]), ALU.mult, l)

        def pre_b(ib):
            nonlocal halo1
            p = ib % 2
            yield from ln_b(hb, sq1, r1, hb_tok[ib], None)
            a = done[0]
            for k in range(2):
                xn = ts(DVE, hb[:, k, :], hb[:, k, :], col("lng", k), col("lnb", k), ALU.mult, ALU.add, a)
            yield
            cv = []
            tf = fb.get("th")
            halo = []
            for m in range(4):
                b, over = takeb()
                for k in range(2):
                    tok = mm(b.buf[:, :], w1[:, k, m * 128:(m + 1) * 128], hb[:, k, :], k == 0, k == 1, over, xn, w_tok1,
                             signal=k == 1)
                    yield
                a = act(xcb[:, m, 3:TB + 3], b.buf[:, :], ACT.Identity, tok, halo1)
                b.free = [a]
                yield
                c = u[p][:, m, :]
                a = ts(DVE, c, xcb[:, m, 0:TB], col("cw1", 4 * m), col("cb1", m), ALU.mult, ALU.add, a, fb.get(("u", p)))
                b, over = takeb()
                for k in range(1, 4):
                    a = stt(c, xcb[:, m, k:k + TB], col("cw1", 4 * m + k), c, ALU.mult, ALU.add, a)
                    if k < 3:
                        tok = mm(b.buf[:, :], w1[:, k - 1, 512 + m * 128:640 + m * 128], hb[:, k - 1, :], k == 1, k == 2,
                                 over, signal=k == 2)
                        yield
                cv.append(a)
                zt = act(sz[p][:, m, :], b.buf[:, :], ACT.Identity, tok, fb.get(("sz", p)))
                b.free = [zt]
                yield
                if m % 2:
                    what = u[p][:, m - 1:m + 1, :]
                    a = act(th1[:, :, :], what, ACT.Tanh, cv, tf)
                    yield
                    a = stt(what, th1[:, :, :], 1.0, what, ALU.add, ALU.mult, a)
                    tf = [a]
                    u_tok[ib] = a
                    what = sz[p][:, m - 1:m + 1, :]
                    a = act(th1[:, :, :], what, ACT.Tanh, zt, tf)
                    yield
                    sz_tok[ib] = stt(what, th1[:, :, :], 1.0, what, ALU.add, ALU.mult, a)
                    tf = [sz_tok[ib]]
            fb["hb"] = [tok]
            halo1 = [SCA(lambda e: e.activation(xcb[:, :, 0:3], xcb[:, :, TB:TB + 3], ACT.Identity), cv)]
            yield
            b, over = takeb()
            for k in range(4):
                tok = mm(b.buf[0:48, :], wxp[:, k, :], u[p][:, k, :], k == 0, k == 3, over, u_tok[ib], wxp_tok,
                         signal=k == 3)
                if k % 2:
                    yield
            db = act(dbc[:, :], b.buf[0:48, :], ACT.Identity, tok, fb.get("dbc"))
            b.free = [db]
            bcs_tok[ib] = SP.dma(lane("bcs"), t["bc"][ib], dbc[16:32, :], db)
            yield
            for m in range(4):
                b, over = takeb()
                tok = mm(b.buf[:, :], wdt[:, m * 128:(m + 1) * 128], dbc[0:16, :], True, True, over, db, wdt_tok,
                         signal=True)
                yield
                v = act(dtt[p][:, m, :], b.buf[:, :], ACT.Identity, tok, fb.get(("dt", p)), bias=col("bdt", m))
                b.free = [v]
                yield
                if m % 2:
                    what = dtt[p][:, m - 1:m + 1, :]
                    a = act(th1[:, :, :], what, ACT.Abs, v, tf)
                    a = act(th1[:, :, :], th1[:, :, :], ACT.Exp, a, scale=-1.0)
                    yield
                    a = act(th1[:, :, :], th1[:, :, :], ACT.Ln, a, bias=1.0)
                    yield
                    dt1_tok[ib] = stt(what, what, 0.0, th1[:, :, :], ALU.max, ALU.add, a)
                    tf = [dt1_tok[ib]]
                    yield
            b, over = takeb()
            for s in range(4):
                tok = tr(b.buf[:, 48 * s:48 * s + 48], dbc[:, s * 128:(s + 1) * 128], ident[0:48, 0:48], over, db,
                         signal=s == 3)
            yield
            ct_tok[ib] = act(Ct[p][:, :, :].rearrange("p a n -> p (a n)"), b.buf[:, 0:192], ACT.Identity, tok,
                             fb.get(("Ct", p)))
            b.free = [ct_tok[ib]]
            fb["dbc"] = [tok, bcs_tok[ib]]
            fb["th"] = tf

        bc_tok, bc_free, ct_tok = {}, {}, {}

        def load_bc(upto):
            for i in range(len(bc_tok), upto + 1):
                ib, n = divmod(i, 8)
                if ib not in bcs_tok:
                    return
                src = t["bc"][ib][2 * n:2 * n + 2, :].rearrange("(o n) s -> o n s", o=1)
                bc_tok[i] = SP.dma(lane(f"bc{i % 3}"), bcr[i % 3][:, :, :], src.broadcast_to([128, 2, TB]), bcs_tok[ib],
                                   bc_free.get(i - 3))

        def scan():
            du_tok, dA, dBs, hs, h_toks, trs, acc_tok = {}, {}, {}, {}, {}, {}, {}

            def exps(k):
                if k == 64 * NB:
                    return
                ib, r = divmod(k, 64)
                n, m = divmod(r, 4)
                p, i = ib % 2, k // 8
                if n == 0:
                    du_tok[m] = tt(POOL, du[:, m, :], dtt[p][:, m, :], u[p][:, m, :], ALU.mult, dt1_tok[ib], u_tok[ib],
                                   fb.get("du"))
                load_bc(i)
                dB, over = dBr.take()
                tok = tt(POOL, dB.buf[:, :], du[:, m, :], bcr[i % 3][:, n % 2, :], ALU.mult, du_tok[m], bc_tok[i], over)
                dBs[k] = (dB, tok)
                if k % 8 == 7:
                    bc_free[i] = [tok]
                    load_bc(i + 3)
                a, over = dAr.take()
                q = 16 * m + n
                a_tok = act(a.buf[:, :], dtt[p][:, m, :], ACT.Exp, dt1_tok[ib], A1_tok, over, scale=A1[:, q:q + 1])
                dA[k] = (a, a_tok)
                if r == 63:
                    fb["du"] = [tok]
                    fb["dt", p] = [a_tok, du_tok[3]]

            def transposes(j):
                if 0 <= j < 64 * NB:
                    n, s = divmod(j, 4)
                    b, over = hTr.take()
                    for m in range(4):
                        tok = tr(b.buf[:, m * 128:(m + 1) * 128], hs[n].buf[:, m, s * 128:(s + 1) * 128], ident, over,
                                 h_toks[4 * n + m], signal=m == 3)
                    trs[j] = (b, tok)
                    if s == 3:
                        hs[n].free = [tok, h_prev[n % 16]]

            def gather(j):
                ib, r = divmod(j, 64)
                n, s = divmod(r, 4)
                p = ib % 2
                b, tok = trs.pop(j)
                c = Ct[p][:, s, 32 + n:33 + n]
                if n == 0:
                    a = ts(DVE, acc[:, s, :], b.buf[:, :], c, None, ALU.mult, None, tok, ct_tok[ib], fb.get("acc"))
                else:
                    a = stt(acc[:, s, :], b.buf[:, :], c, acc[:, s, :], ALU.mult, ALU.add, tok, acc_tok[s])
                b.free = [a]
                acc_tok[s] = a
                if r == 63:
                    fb["Ct", p] = [a]
                    gates(ib)

            def gates(ib):
                p = ib % 2
                for m in range(4):
                    b, over = hTr.take()
                    for s in range(4):
                        tok = tr(b.buf[:, s * 128:(s + 1) * 128], acc[:, s, m * 128:(m + 1) * 128], ident, over,
                                 acc_tok[s], signal=s == 3)
                    a = stt(u[p][:, m, :], u[p][:, m, :], col("D1", m), b.buf[:, :], ALU.mult, ALU.add, tok,
                            fb["dt", p])
                    b.free = [a]
                    g_tok = tt(DVE, u[p][:, m, :], u[p][:, m, :], sz[p][:, m, :], ALU.mult, a, sz_tok[ib])
                fb["acc"] = [tok]
                fb["sz", p] = [g_tok]
                gate_tok[ib] = g_tok

            exps(0)
            yield
            for k in range(64 * NB + LAG):
                if k < 64 * NB:
                    exps(k + 1)
                    n, m = divmod(k, 4)
                    if m == 0:
                        hs[n], over_h = hr.take()
                    (b, b_tok), (a, a_tok) = dBs.pop(k), dA.pop(k)
                    s_tok = DVE(lambda e, h=hs[n], a=a, b=b, m=m, n=n % 16: e.tensor_tensor_scan(
                        h.buf[:, m, :], a.buf[:, :], b.buf[:, :], hst[:, n, m:m + 1], ALU.mult, ALU.add),
                        a_tok, b_tok, h_prev[n % 16], over_h, cost=660)
                    b.free, a.free = [s_tok], [s_tok]
                    h_toks[k] = s_tok
                if k % 4 == 1 and 5 <= k < 64 * NB + 4:
                    n = k // 4 - 1
                    h_prev[n % 16] = [act(hst[:, n % 16, :], hs[n].buf[:, :, TB - 1], ACT.Identity,
                                          [h_toks[4 * n + m] for m in range(4)])]
                last = (k - LAG) % 64 == 63
                if not last:
                    transposes(k - LAG + 1)
                if k >= LAG:
                    gather(k - LAG)
                if last:
                    transposes(k - LAG + 1)
                yield

        y_tok, gate_tok = {}, {}
        out_toks = []
        x3_free = [over_a]
        xs_tok, xn3_tok = {}, {}
        sum_toks = []

        def post_b(ib):
            nonlocal x3_free
            p = ib % 2
            blk = slice(ib * TB, (ib + 1) * TB)
            while ib not in gate_tok:
                yield
            x_tok = SP.dma(lane("x3"), x3[:, :, :], t["x2"][:, :, blk], x2_tok[ib], x3_free)
            for m in range(2):
                b, over = takeb()
                for k in range(4):
                    tok = mm(b.buf[:, :], wo1[:, k, m * 128:(m + 1) * 128], u[p][:, k, :], k == 0, k == 3, over,
                             gate_tok[ib], wo1_tok, signal=k == 3)
                    yield
                x_tok = tt(DVE, x3[:, m, :], x3[:, m, :], b.buf[:, :], ALU.add, tok, x_tok)
                b.free = [x_tok]
                yield
            fb[("u", p)] = [tok]
            xs_tok[ib] = SP.dma(lane(f"x3s{ib}"), t["x3"][:, :, blk], x3[:, :, :], x_tok)
            yield from ln_b(x3, sq1, r1, [x_tok], [xs_tok[ib]])
            xn = done[0]
            sum_toks.append(DVE(lambda e: e.tensor_reduce(sums[:, :, ib], x3[:, :, :], AX.X, ALU.add), xn))
            xn3_tok[ib] = SP.dma(lane(f"xn3{ib}"), t["xn3"][:, :, blk], x3[:, :, :], xn)
            x3_free = [xn3_tok[ib], sum_toks[-1]]
            yield

        def chain(*gens):
            for g in gens:
                yield from g

        evac_b(0)
        pace(PE, DVE, (pre_b(0), PRE, 1.0), fill=product_b(1))
        scanning = scan()
        for ib in range(NB):
            sides, n = [], 0
            if ib + 1 < NB:
                evac_b(ib + 1)
            if ib >= 1:
                sides.append(post_b(ib - 1))
                n += 24
            if ib + 1 < NB:
                sides.append(pre_b(ib + 1))
                n += PRE
            parts = [(steps(scanning, 64), 64, 1.0), (chain(*sides), n, SIDE)]
            pace(PE, DVE, *parts, fill=product_b(ib + 2) if ib + 2 < NB else None)
        run(scanning)
        xn = raw[0:3]
        xn_tok, xr_tok, c_free = {}, {}, {}

        def load_c(ib):
            if ib < NB:
                xn_tok[ib] = SP.dma(lane(f"cxn{ib % 3}"), xn[ib % 3][:, :, :], t["xn3"][:, :, ib * TB:(ib + 1) * TB],
                                    P_tok, xn3_tok[ib], c_free.get(("xn", ib - 3)))

        for ib in range(3):
            load_c(ib)
        run(post_b(NB - 1))
        over_b = barrier()
        cB.close()

        cC = ExitStack()
        mean = sb(cC, "mean", [128, 2])
        Wr = sb(cC, "Wr", [128, 2, 8])
        br = sb(cC, "br", [1, 8])
        q = sb(cC, "q", [1, 16, 8])
        idx = sb(cC, "idx", [1, 8], U32)
        tw = sb(cC, "tw", [128, 2])
        W1 = msg[:, 0:8, :].rearrange("p (e k a) d -> p e k (a d)", e=2, k=2)
        W2 = msg[:, 8:16, :].rearrange("p (e k) d -> p e k d", e=2)
        b1 = sb(cC, "b1", [128, 2, 4])
        b2 = sb(cC, "b2", [128, 2, 2])
        b2c = sb(cC, "b2c", [128, 2])
        xr = [raw[3]] + [sb(cC, f"xr{i}", [128, 2, TB]) for i in range(2)]
        W1s = [sb(cC, f"W1{i}", [128, 2, 2, 512], F32R) for i in "hl"]
        W2s = [sb(cC, f"W2{i}", [128, 2, 4, D], F32R) for i in "hl"]
        xs = [[sb(cC, f"xs{i}{j}", [128, 2, TB], F32R) for j in "hl"] for i in range(2)]
        Gs = [[sb(cC, f"Gs{i}{j}", [128, 8, TB], F32R) for j in "hl"] for i in range(2)]
        gr = Ring([sb(cC, f"g{i}", [128, TB]) for i in range(3)])
        o = [sb(cC, f"o{i}", [128, 2, TB]) for i in range(2)]
        sq2 = [sb(cC, f"sq2{i}", [128, 2, TB]) for i in range(2)]
        r2 = [sb(cC, f"r2{i}", [128, TB]) for i in range(2)]

        ring_c = Ring(P)
        takec = ring_c.take

        wr_tok = SP.dma(lane("Wr"), Wr[:, :, :], t["Wr"], over_b)
        br_tok = SP.dma(lane("br"), br[:, :], t["br"], over_b)
        def load_r(ib):
            if ib < NB:
                blk = slice(ib * TB, (ib + 1) * TB)
                xr_tok[ib] = SP.dma(lane(f"cxr{ib % 3}"), xr[ib % 3][:, :, :], t["x3"][:, :, blk], over_b,
                                    xs_tok[ib], c_free.get(("xr", ib - 3)))

        load_r(0)
        x_tok, gt, o_tok = {}, {}, {}

        def parts_of_x(ib):
            if ib < NB:
                xp = xs[ib % 2]
                x_tok[ib] = split(xn[ib % 3][:, :, :], xp[0][:, :, :], xp[1][:, :, :], xn_tok[ib],
                                  c_free.get(("xs", ib - 2)))

        parts_of_x(0)

        a = DVE(lambda e: e.tensor_reduce(mean[:, :], sums[:, :, :], AX.X, ALU.add), over_b, sum_toks)
        b, over = takec()
        for k in range(2):
            tok = mm(b.buf[0:1, 0:8], mean[:, k:k + 1], Wr[:, k, :], k == 0, k == 1, over_b, a, wr_tok, signal=k == 1)
        row = [q[:, i, :] for i in range(16)]

        def softmax_row(x, y, a):
            mx, s, rs = row[13][:, 0:1], row[14][:, 0:1], row[15][:, 0:1]
            a = DVE(lambda e: e.tensor_reduce(mx, x, AX.X, ALU.max), a)
            a = ts(DVE, y, x, mx, None, ALU.subtract, None, a)
            a = act(y, y, ACT.Exp, a, accum=s)
            a = DVE(lambda e: e.reciprocal(rs, s), a)
            return ts(DVE, y, y, rs, None, ALU.mult, None, a)

        a = stt(row[0], b.buf[0:1, 0:8], 1.0 / N, br[:, :], ALU.mult, ALU.add, tok, br_tok)
        b.free = [a]
        a = softmax_row(row[0], row[1], a)
        cap = float(-(-N * 5 // 4 // 8))
        a = ts(DVE, row[2], row[1], float(N), 1e-30, ALU.mult, ALU.max, a)
        a = DVE(lambda e: e.reciprocal(row[3], row[2]), a)
        a = ts(DVE, row[3], row[3], cap, 1.0, ALU.mult, ALU.min, a)
        a = tt(DVE, row[4], row[1], row[3], ALU.mult, a)
        a = softmax_row(row[4], row[5], a)
        a = DVE(lambda e: e.max(row[6], row[5]), a)
        idx_tok = DVE(lambda e: e.max_index(idx[:, :], row[6], row[5]), a)
        a = ts(DVE, row[7][:, 0:2], row[6][:, 0:2], row[6][:, 0:1], None, ALU.subtract, None, idx_tok)
        a = act(row[8][:, 0:2], row[7][:, 0:2], ACT.Exp, a, accum=row[9][:, 0:1])
        a = DVE(lambda e: e.reciprocal(row[10][:, 0:1], row[9][:, 0:1]), a)
        a = ts(DVE, row[11][:, 0:2], row[8][:, 0:2], row[10][:, 0:1], None, ALU.mult, None, a)
        b, over = takec()
        tok = mm(b.buf[:, 0:2], one[0:1, :], row[11][:, 0:2], True, True, over, a, signal=True)
        tw_tok = DVE(lambda e: e.tensor_copy(tw[:, :], b.buf[:, 0:2]), tok)
        b.free = [tw_tok]

        e_tok, got = {}, {}

        def load_expert(k, name, dst, pat):
            def go(e):
                if k not in got:
                    got[k] = e.value_load(idx[0:1, k:k + 1], min_val=0, max_val=7)
                return e.dma_start(dst, t[name][bass.ds(got[k], 1)].rearrange(pat))

            ln = lane(f"{name}{k}")
            ln.count += 16
            SP.ops.append((list(flat([idx_tok, over_b])), go, ln.sem, 16))
            e_tok[name, k] = (ln.sem, ln.count)

        for k in range(2):
            load_expert(k, "W1", W1[:, k, :, :], "o p k f -> p (o k) f")
            load_expert(k, "b1", b1[:, k, :], "o p m -> p (o m)")
        for k in range(2):
            load_expert(k, "W2", W2[:, k, :, :], "o p k f -> p (o k) f")
            load_expert(k, "b2", b2[:, k, :], "o p m -> p (o m)")
        load_r(1)
        load_r(2)
        w1_tok = [split(W1[:, k, :, :], W1s[0][:, k, :, :], W1s[1][:, k, :, :], e_tok["W1", k], by=SCA) for k in range(2)]
        ew = []

        def second_matrices():
            nonlocal b2_tok
            for k in range(2):
                a = ts(DVE, W2[:, k, :, :], W2[:, k, :, :], tw[:, k:k + 1], None, ALU.mult, None, tw_tok, e_tok["W2", k])
                ew.append(split(W2[:, k, :, :], W2s[0][:, k, :, :], W2s[1][:, k, :, :], a, by=SCA))
                yield
            a = ts(DVE, b2[:, 0, :], b2[:, 0, :], tw[:, 0:1], None, ALU.mult, None, e_tok["b2", 0])
            b2_tok = stt(b2c[:, :], b2[:, 1, :], tw[:, 1:2], b2[:, 0, :], ALU.mult, ALU.add, a, e_tok["b2", 1])

        b2_tok = None
        def hidden(ib):
            g, xp = Gs[ib % 2], xs[ib % 2]
            gt[ib] = []
            for i in range(8):
                e, f = divmod(i, 4)
                b, over = takec()
                for k in range(2):
                    fs = slice(f * 128, (f + 1) * 128)
                    tok = mm3(b.buf[:, :], [w[:, e, k, fs] for w in W1s], [y[:, k, :] for y in xp], k == 0, k == 1,
                              over, x_tok[ib], w1_tok[e], signal=k == 1)
                gg, over = gr.take()
                a = act(gg.buf[:, :], b.buf[:, :], ACT.Gelu, tok, e_tok["b1", e], over, bias=b1[:, e, f:f + 1])
                b.free = [a]
                a = split(gg.buf[:, :], g[0][:, i, :], g[1][:, i, :], a, c_free.get(("G", ib - 2)))
                gg.free = [a]
                gt[ib].append(a)
                yield
            c_free[("xs", ib)] = tok

        def outputs(ib):
            g = Gs[ib % 2]
            for d in range(2):
                b, over = takec()
                for i in range(8):
                    tok = mm3(b.buf[:, :], [w[:, i // 4, i % 4, d * 128:(d + 1) * 128] for w in W2s],
                              [y[:, i, :] for y in g], i == 0, i == 7, over, gt[ib][i], ew, signal=i == 7)
                o_tok[ib] = stt(o[ib % 2][:, d, :], b.buf[:, :], b2c[:, d:d + 1], xn[ib % 3][:, d, :], ALU.add, ALU.add,
                                tok, b2_tok, c_free.get(("o", ib - 2)))
                b.free = [o_tok[ib]]
            c_free[("G", ib)] = tok
            c_free[("xn", ib)] = o_tok[ib]
            load_c(ib + 3)

        def ending(ib):
            oo = o[ib % 2]
            yield from layer_norm(takec, oo, oo, sq2[ib % 2], r2[ib % 2], o_tok[ib], c_free.get(("o", ib - 2)))
            a = done[0]
            yield
            for k in range(2):
                a = ts(DVE, oo[:, k, :], oo[:, k, :], col("gamma", k), col("beta", k), ALU.mult, ALU.add, a)
            a = tt(DVE, oo[:, :, :], oo[:, :, :], xr[ib % 3][:, :, :], ALU.add, a, xr_tok[ib])
            c_free[("xr", ib)] = a
            c_free[("o", ib)] = SP.dma(lane(f"out{ib % 2}"), t["out"][:, :, ib * TB:(ib + 1) * TB], oo[:, :, :], a)
            load_r(ib + 3)

        for i in range(NB + 2):
            h = hidden(i) if i < NB else iter(())
            l = ending(i - 2) if 2 <= i else second_matrices() if i == 0 else iter(())
            for _ in range(9):
                next(h, None)
                next(l, None)
            run(l)
            parts_of_x(i + 1)
            if 1 <= i <= NB:
                outputs(i - 1)
        ends = [c_free[("o", NB - 1)], c_free[("o", NB - 2)]]
        cC.close()

        block = ctx.enter_context(nc.Block())

        @block.sync
        def _(e):
            SP.play(e)
            for s, v in ends:
                e.wait_ge(s, v)
            for ln in lanes.values():
                e.wait_ge(ln.sem, ln.count)

        @block.tensor
        def _(e):
            PE.play(e)

        @block.vector
        def _(e):
            DVE.play(e)

        @block.scalar
        def _(e):
            SCA.play(e)

        @block.gpsimd
        def _(e):
            POOL.play(e)


def kernel(**inputs):
    import concourse.bacc as bacc
    from concourse.bass_utils import run_bass_kernel_spmd

    a = {k: np.asarray(v) for k, v in inputs.items()}
    f = np.float32

    def tiles(w):
        return w.reshape(-1, 128, w.shape[-1]).transpose(1, 0, 2)

    def cols(v):
        return v.reshape(-1, 128).T

    def pad(v):
        return np.concatenate([v, np.zeros((64,) + v.shape[1:], f)])

    tri = np.triu(np.ones((128, 128), f))
    consts = np.stack([np.eye(128, dtype=f), tri, np.tril(np.ones((128, 128), f), -1), np.full((128, 128), 1 / 256, f),
                       np.ones((128, 128), f)], 1)
    cw, cb = a["L0_ffn_conv_w"], a["L0_ffn_conv_b"]
    cw = np.concatenate([cw[:512], pad(cw[512:576]), pad(cw[576:])])
    cb = np.concatenate([cb[:512], pad(cb[512:576]), pad(cb[576:])])
    parts = {
        "cw0": cw.reshape(6, 128, 4).transpose(1, 0, 2).reshape(128, 24), "cb0": cols(cb),
        "cw1": a["L1_gnn_conv_w"].reshape(4, 128, 4).transpose(1, 0, 2).reshape(128, 16),
        "cb1": cols(a["L1_gnn_conv_b"]), "D0": cols(np.repeat(a["L0_ffn_D"], 64)), "nw": cols(a["L0_ffn_norm_w"]),
        "blin": cols(a["L0_ffn_b_lin"]), "gcnb": cols(a["L1_gnn_gcn_b"]), "lng": cols(a["L1_gnn_ln_g"]),
        "lnb": cols(a["L1_gnn_ln_b"]), "bdt": cols(a["L1_gnn_b_dt"]),
        "A1": a["L1_gnn_A_log"].reshape(4, 128, 16).transpose(1, 0, 2).reshape(128, 64),
        "D1": cols(a["L1_gnn_D_skip"]), "gamma": cols(a["L1_ffn_gamma"]), "beta": cols(a["L1_ffn_beta"]),
    }
    wp = np.zeros((128, 4, 512), f)
    wp[:, 0:2, :] = tiles(np.ascontiguousarray(a["L0_ffn_W_out"].T))
    arrays = {
        "xT": tiles(a["x"].T),
        "adjT": a["adj"].reshape(NB, TB, NJ, 128).transpose(0, 3, 2, 1),
        "consts": consts,
        "cols": np.concatenate([parts[k] for k in COLS], 1),
        "rows": np.concatenate([a["L0_gnn_B"], np.tile(a["L0_ffn_dt_bias"], 4), a["L0_ffn_A_log"]])[None],
        "W0": tiles(a["L0_gnn_W"]), "Win": tiles(a["L0_ffn_W_in"]), "WoutT": wp,
        "Wlin": tiles(a["L0_ffn_W_lin"]), "Wg": tiles(a["L1_gnn_gcn_w"]), "w1": tiles(a["L1_gnn_w_in"]),
        "wxp": tiles(a["L1_gnn_w_xp"]), "wdt": a["L1_gnn_w_dt"], "wo1": tiles(a["L1_gnn_w_out"]),
        "Wr": tiles(a["L1_ffn_Wr"]), "br": a["L1_ffn_br"][None],
        "W1": a["L1_ffn_W1"].reshape(8, 2, 128, 512).transpose(0, 2, 1, 3),
        "W2": a["L1_ffn_W2"].reshape(8, 4, 128, 256).transpose(0, 2, 1, 3),
        "b1": a["L1_ffn_b1"].reshape(8, 4, 128).transpose(0, 2, 1),
        "b2": a["L1_ffn_b2"].reshape(8, 2, 128).transpose(0, 2, 1),
    }
    arrays = {"in_" + k: np.ascontiguousarray(v) for k, v in arrays.items()}
    nc = bacc.Bacc("TRN2", target_bir_lowering=False, num_devices=1)
    t = {k[3:]: nc.dram_tensor(k, v.shape, mybir.dt.from_np(v.dtype), kind="ExternalInput").ap()
         for k, v in arrays.items()}
    for name, shape in (("x2", (128, 2, N)), ("x3", (128, 2, N)), ("xn3", (128, 2, N)), ("m2", (128, NJ, D)), ("bc", (NB, 16, TB))):
        t[name] = nc.dram_tensor("tmp_" + name, shape, F32, kind="Internal").ap()
    t["out"] = nc.dram_tensor("out_0", (128, 2, N), F32, kind="ExternalOutput").ap()
    build(nc, t)
    r = run_bass_kernel_spmd(nc, [arrays], core_ids=[0])
    got = r.results[0]["out_0"]
    return np.ascontiguousarray(got.transpose(2, 1, 0).reshape(N, D))
```
